# Optimizing a Trainium2 kernel written in Bass

```python
import numpy as np
import jax
import jax.numpy as jnp

def _softmax(x, axis=-1):
    return jax.nn.softmax(x, axis=axis)

def _gelu(x):
    return jax.nn.gelu(x, approximate=True)

def _silu(x):
    return jax.nn.silu(x)

def _sigmoid(x):
    return jax.nn.sigmoid(x)

def _layernorm(x, axis=-1, eps=1e-05):
    m = jnp.mean(x, axis=axis, keepdims=True)
    v = jnp.var(x, axis=axis, keepdims=True)
    return (x - m) / jnp.sqrt(v + eps)

def _scatter_add(tgt, idx, src, axis=0):
    return tgt.at[idx].add(src)

def _segment_sum(src, seg, n):
    return jax.ops.segment_sum(src, seg, n)
kernel_name = 'mk_flamingo_gated_d2_seqx_r8_1b9f37'

def setup_inputs(seed: int=0):
    np.random.seed(seed)
    _w = jnp.asarray

    def _rec_inputs():
        import jax
        import jax.numpy as jnp
        _rk = jax.random.key(seed)
        x = -0.0003929 + 0.9999 * jax.random.normal(jax.random.fold_in(_rk, 1), (16, 128, 256), jnp.float32)
        _lenS = 128 - jax.random.randint(jax.random.fold_in(_rk, 7), (16,), 0, max(1, 128 // 4) + 1, jnp.int32)
        _lenS2 = 128 - jax.random.randint(jax.random.fold_in(_rk, 8), (16,), 0, max(1, 128 // 4) + 1, jnp.int32)
        _ctx_1024P = jax.random.normal(jax.random.fold_in(_rk, 11), (16, 16, 128), jnp.float32)
        _ctx_1024c = jax.random.dirichlet(jax.random.fold_in(_rk, 511), 0.3 * jnp.ones((16,), jnp.float32), (16, 128))
        _ctx_1024t = jnp.einsum('bsk,bkd->bsd', _ctx_1024c, _ctx_1024P)
        _ctx_1024t = _ctx_1024t * jax.lax.rsqrt(jnp.mean(jnp.square(_ctx_1024t)) + 1e-12) * 0.953939
        ctx_1024 = 0.000227908 + 0.99994 * (_ctx_1024t + 0.3 * jax.random.normal(jax.random.fold_in(_rk, 611), (16, 128, 128), jnp.float32))
        _validS = jnp.arange(128)[None, :] < _lenS[:, None]
        _validS2 = jnp.arange(128)[None, :] < _lenS2[:, None]
        _causal = jnp.tril(jnp.ones((128, 128), dtype=bool))
        mask_BxS2_bf1 = jnp.ones((16, 128), dtype=bool)
        _g = jax.random.normal(jax.random.fold_in(_rk, 9001), (2, 2), jnp.float32)
        _g = jnp.sign(_g) * jnp.maximum(jnp.abs(_g), 1.0) + (_g == 0) * 1.0
        g_xattn = _g[0]
        g_ffn = _g[1]
        return (x, ctx_1024, mask_BxS2_bf1, g_xattn, g_ffn)
    x, ctx_1024, mask_BxS2_bf1, g_xattn, g_ffn = _rec_inputs()

    def _L0_xattn_setup():
        import jax, jax.numpy as jnp
        import numpy as np
        EPS = 1e-05

        def rmsnorm(x, g, eps=EPS):
            var = jnp.mean(jnp.square(x), axis=-1, keepdims=True)
            return x * jax.lax.rsqrt(var + eps) * g
        key = jax.random.key(seed)
        ks = jax.random.split(key, 8)
        B, Sq, Skv = (2, 512, 64)
        dim, cdim, H, D = (256, 128, 16, 128)
        inner = H * D
        s = lambda f: 1.0 / np.sqrt(f)
        return {'hidden_states': jax.random.normal(ks[0], (B, Sq, dim), jnp.float32), 'encoder_hidden_states': jax.random.normal(ks[1], (B, Skv, cdim), jnp.float32), 'Wq': jax.random.normal(ks[2], (dim, inner), jnp.float32) * s(dim), 'Wk': jax.random.normal(ks[3], (cdim, inner), jnp.float32) * s(cdim), 'Wv': jax.random.normal(ks[4], (cdim, inner), jnp.float32) * s(cdim), 'Wo': jax.random.normal(ks[5], (inner, dim), jnp.float32) * s(inner), 'gq': jnp.ones((D,), jnp.float32), 'gk': jnp.ones((D,), jnp.float32)}
    _L0_xattn_all = _L0_xattn_setup()
    _L0_xattn_in = {k: v for k, v in _L0_xattn_all.items() if k in ('Wq', 'Wk', 'Wv', 'Wo', 'gq', 'gk')}
    del _L0_xattn_all

    def _L0_ffn_setup():
        import jax, jax.numpy as jnp
        import numpy as np
        BLOCK_SIZE = 32
        HIDDEN_SIZE = 256
        MLP_DIM = 2048
        NVFP4_LUT = jnp.array([0.0, 0.5, 1.0, 1.5, 2.0, 3.0, 4.0, 6.0, 0.0, -0.5, -1.0, -1.5, -2.0, -3.0, -4.0, -6.0], dtype=jnp.float32)

        def dequant_nvfp4(W_packed, scales, block=BLOCK_SIZE):
            N = W_packed.shape[0]
            low = W_packed & 15
            high = W_packed >> 4 & 15
            idx = jnp.stack([low, high], axis=-1).reshape(N, -1)
            vals = NVFP4_LUT[idx]
            K = vals.shape[1]
            vals = vals.reshape(N, K // block, block) * scales[:, :, None]
            return vals.reshape(N, K)
        key = jax.random.key(seed)
        ks = jax.random.split(key, 7)
        x = jax.random.normal(ks[0], (4, 32, HIDDEN_SIZE), dtype=jnp.float32)
        gate_W_packed = jax.random.randint(ks[1], (MLP_DIM, HIDDEN_SIZE // 2), 0, 32, dtype=jnp.int32)
        gate_scales = jax.random.uniform(ks[2], (MLP_DIM, HIDDEN_SIZE // BLOCK_SIZE), dtype=jnp.float32) * 0.1 + 0.001
        up_W_packed = jax.random.randint(ks[3], (MLP_DIM, HIDDEN_SIZE // 2), 0, 32, dtype=jnp.int32)
        up_scales = jax.random.uniform(ks[4], (MLP_DIM, HIDDEN_SIZE // BLOCK_SIZE), dtype=jnp.float32) * 0.1 + 0.001
        down_W_packed = jax.random.randint(ks[5], (HIDDEN_SIZE, MLP_DIM // 2), 0, 32, dtype=jnp.int32)
        down_scales = jax.random.uniform(ks[6], (HIDDEN_SIZE, MLP_DIM // BLOCK_SIZE), dtype=jnp.float32) * 0.1 + 0.001
        return {'x': x, 'gate_W_packed': gate_W_packed, 'gate_scales': gate_scales, 'up_W_packed': up_W_packed, 'up_scales': up_scales, 'down_W_packed': down_W_packed, 'down_scales': down_scales}
    _L0_ffn_all = _L0_ffn_setup()
    _L0_ffn_in = {k: v for k, v in _L0_ffn_all.items() if k in ('gate_W_packed', 'gate_scales', 'up_W_packed', 'up_scales', 'down_W_packed', 'down_scales')}
    del _L0_ffn_all

    def _L1_xattn_setup():
        import jax, jax.numpy as jnp
        import numpy as np
        N_HEADS = 16
        N_KV_HEADS = 8
        HEAD_DIM = 128
        D_TEXT = 256
        D_VISION = 128
        GROUPS = N_HEADS // N_KV_HEADS
        key = jax.random.key(seed)
        ks = jax.random.split(key, 6)
        B, T_text, T_vis = (4, 256, 72)
        text_hidden = jax.random.normal(ks[0], (B, T_text, D_TEXT), dtype=jnp.float32)
        vision_tokens = jax.random.normal(ks[1], (B, T_vis, D_VISION), dtype=jnp.float32)
        vision_mask = jnp.ones((B, T_vis), dtype=bool)
        s = 0.02
        Wq = jax.random.normal(ks[2], (D_TEXT, N_HEADS * HEAD_DIM), dtype=jnp.float32) * s
        Wk = jax.random.normal(ks[3], (D_VISION, N_KV_HEADS * HEAD_DIM), dtype=jnp.float32) * s
        Wv = jax.random.normal(ks[4], (D_VISION, N_KV_HEADS * HEAD_DIM), dtype=jnp.float32) * s
        Wo = jax.random.normal(ks[5], (N_HEADS * HEAD_DIM, D_TEXT), dtype=jnp.float32) * s
        return {'text_hidden': text_hidden, 'vision_tokens': vision_tokens, 'vision_mask': vision_mask, 'Wq': Wq, 'Wk': Wk, 'Wv': Wv, 'Wo': Wo}
    _L1_xattn_all = _L1_xattn_setup()
    _L1_xattn_in = {k: v for k, v in _L1_xattn_all.items() if k in ('Wq', 'Wk', 'Wv', 'Wo')}
    del _L1_xattn_all

    def _L1_ffn_setup():
        import jax, jax.numpy as jnp
        import numpy as np
        H = 256
        I_MOE = 176
        I_SH = 704
        E = 8
        TOP_K = 2
        B, S = (1, 256)

        def _silu_and_mul(gu, inter):
            return jax.nn.silu(gu[..., :inter]) * gu[..., inter:]
        key = jax.random.key(seed)
        ks = jax.random.split(key, 7)
        sc = 0.02
        return {'hidden_states': jax.random.normal(ks[0], (B, S, H), jnp.float32), 'W_router': jax.random.normal(ks[1], (E, H), jnp.float32) * sc, 'W_sgate': jax.random.normal(ks[2], (1, H), jnp.float32) * sc, 'Ws_gate_up': jax.random.normal(ks[3], (H, 2 * I_SH), jnp.float32) * sc, 'Ws_down': jax.random.normal(ks[4], (I_SH, H), jnp.float32) * sc, 'We_gate_up': jax.random.normal(ks[5], (E, H, 2 * I_MOE), jnp.float32) * sc, 'We_down': jax.random.normal(ks[6], (E, I_MOE, H), jnp.float32) * sc}
    _L1_ffn_all = _L1_ffn_setup()
    _L1_ffn_in = {k: v for k, v in _L1_ffn_all.items() if k in ('W_router', 'W_sgate', 'Ws_gate_up', 'Ws_down', 'We_gate_up', 'We_down')}
    del _L1_ffn_all
    return {'x': x, 'ctx_1024': ctx_1024, 'mask_BxS2_bf1': mask_BxS2_bf1, 'g_xattn': g_xattn, 'g_ffn': g_ffn, 'L0_xattn_Wq': _L0_xattn_in['Wq'], 'L0_xattn_Wk': _L0_xattn_in['Wk'], 'L0_xattn_Wv': _L0_xattn_in['Wv'], 'L0_xattn_Wo': _L0_xattn_in['Wo'], 'L0_xattn_gq': _L0_xattn_in['gq'], 'L0_xattn_gk': _L0_xattn_in['gk'], 'L0_ffn_gate_W_packed': _L0_ffn_in['gate_W_packed'], 'L0_ffn_gate_scales': _L0_ffn_in['gate_scales'], 'L0_ffn_up_W_packed': _L0_ffn_in['up_W_packed'], 'L0_ffn_up_scales': _L0_ffn_in['up_scales'], 'L0_ffn_down_W_packed': _L0_ffn_in['down_W_packed'], 'L0_ffn_down_scales': _L0_ffn_in['down_scales'], 'L1_xattn_Wq': _L1_xattn_in['Wq'], 'L1_xattn_Wk': _L1_xattn_in['Wk'], 'L1_xattn_Wv': _L1_xattn_in['Wv'], 'L1_xattn_Wo': _L1_xattn_in['Wo'], 'L1_ffn_W_router': _L1_ffn_in['W_router'], 'L1_ffn_W_sgate': _L1_ffn_in['W_sgate'], 'L1_ffn_Ws_gate_up': _L1_ffn_in['Ws_gate_up'], 'L1_ffn_Ws_down': _L1_ffn_in['Ws_down'], 'L1_ffn_We_gate_up': _L1_ffn_in['We_gate_up'], 'L1_ffn_We_down': _L1_ffn_in['We_down']}

def reference(x, ctx_1024, mask_BxS2_bf1, g_xattn, g_ffn, L0_xattn_Wq, L0_xattn_Wk, L0_xattn_Wv, L0_xattn_Wo, L0_xattn_gq, L0_xattn_gk, L0_ffn_gate_W_packed, L0_ffn_gate_scales, L0_ffn_up_W_packed, L0_ffn_up_scales, L0_ffn_down_W_packed, L0_ffn_down_scales, L1_xattn_Wq, L1_xattn_Wk, L1_xattn_Wv, L1_xattn_Wo, L1_ffn_W_router, L1_ffn_W_sgate, L1_ffn_Ws_gate_up, L1_ffn_Ws_down, L1_ffn_We_gate_up, L1_ffn_We_down):
    import jax
    import jax.numpy as jnp

    def _L0_xattn_ref(hidden_states, encoder_hidden_states, Wq, Wk, Wv, Wo, gq, gk):
        import jax, jax.numpy as jnp
        import numpy as np
        EPS = 1e-05

        def rmsnorm(x, g, eps=EPS):
            var = jnp.mean(jnp.square(x), axis=-1, keepdims=True)
            return x * jax.lax.rsqrt(var + eps) * g
        B, Sq, _ = hidden_states.shape
        Skv = encoder_hidden_states.shape[1]
        D = gq.shape[0]
        H = Wq.shape[1] // D
        scale = 1.0 / np.sqrt(D)
        q = (hidden_states @ Wq).reshape(B, Sq, H, D)
        k = (encoder_hidden_states @ Wk).reshape(B, Skv, H, D)
        v = (encoder_hidden_states @ Wv).reshape(B, Skv, H, D)
        q = rmsnorm(q, gq)
        k = rmsnorm(k, gk)
        scores = jnp.einsum('bqhd,bkhd->bhqk', q, k) * scale
        attn = jax.nn.softmax(scores, axis=-1)
        out = jnp.einsum('bhqk,bkhd->bqhd', attn, v)
        out = out.reshape(B, Sq, H * D)
        return out @ Wo

    def _L0_ffn_ref(x, gate_W_packed, gate_scales, up_W_packed, up_scales, down_W_packed, down_scales):
        import jax, jax.numpy as jnp
        import numpy as np
        BLOCK_SIZE = 32
        HIDDEN_SIZE = 256
        MLP_DIM = 2048
        NVFP4_LUT = jnp.array([0.0, 0.5, 1.0, 1.5, 2.0, 3.0, 4.0, 6.0, 0.0, -0.5, -1.0, -1.5, -2.0, -3.0, -4.0, -6.0], dtype=jnp.float32)

        def dequant_nvfp4(W_packed, scales, block=BLOCK_SIZE):
            N = W_packed.shape[0]
            low = W_packed & 15
            high = W_packed >> 4 & 15
            idx = jnp.stack([low, high], axis=-1).reshape(N, -1)
            vals = NVFP4_LUT[idx]
            K = vals.shape[1]
            vals = vals.reshape(N, K // block, block) * scales[:, :, None]
            return vals.reshape(N, K)
        B, S, H = x.shape
        xt = x.reshape(B * S, H)
        Wg = dequant_nvfp4(gate_W_packed, gate_scales)
        Wu = dequant_nvfp4(up_W_packed, up_scales)
        Wd = dequant_nvfp4(down_W_packed, down_scales)
        gate = jnp.einsum('th,nh->tn', xt, Wg)
        up = jnp.einsum('th,nh->tn', xt, Wu)
        gelu = jnp.tanh(0.7978845608028654 * (gate + 0.044715 * gate ** 3)) * gate * 0.5 + gate * 0.5
        inter = gelu * up
        out = jnp.einsum('tn,hn->th', inter, Wd)
        return out.reshape(B, S, H)

    def _L1_xattn_ref(text_hidden, vision_tokens, vision_mask, Wq, Wk, Wv, Wo):
        import jax, jax.numpy as jnp
        import numpy as np
        N_HEADS = 16
        N_KV_HEADS = 8
        HEAD_DIM = 128
        D_TEXT = 256
        D_VISION = 128
        GROUPS = N_HEADS // N_KV_HEADS
        B, T_text, _ = text_hidden.shape
        T_vis = vision_tokens.shape[1]
        scale = jnp.float32(np.sqrt(HEAD_DIM))
        q = (text_hidden @ Wq).reshape(B, T_text, N_HEADS, HEAD_DIM).transpose(0, 2, 1, 3)
        k = (vision_tokens @ Wk).reshape(B, T_vis, N_KV_HEADS, HEAD_DIM).transpose(0, 2, 1, 3)
        v = (vision_tokens @ Wv).reshape(B, T_vis, N_KV_HEADS, HEAD_DIM).transpose(0, 2, 1, 3)
        k = jnp.repeat(k, GROUPS, axis=1)
        v = jnp.repeat(v, GROUPS, axis=1)
        scores = jnp.einsum('bhtd,bhsd->bhts', q, k) / scale
        mask = vision_mask[:, None, None, :]
        scores = jnp.where(mask, scores, -jnp.inf)
        attn = jax.nn.softmax(scores, axis=-1)
        attn = jnp.nan_to_num(attn, nan=0.0)
        out = jnp.einsum('bhts,bhsd->bhtd', attn, v)
        out = out.transpose(0, 2, 1, 3).reshape(B, T_text, N_HEADS * HEAD_DIM)
        return out @ Wo

    def _L1_ffn_ref(hidden_states, W_router, W_sgate, Ws_gate_up, Ws_down, We_gate_up, We_down):
        import jax, jax.numpy as jnp
        import numpy as np
        H = 256
        I_MOE = 176
        I_SH = 704
        E = 8
        TOP_K = 2
        B, S = (1, 256)

        def _silu_and_mul(gu, inter):
            return jax.nn.silu(gu[..., :inter]) * gu[..., inter:]
        orig_shape = hidden_states.shape
        x = hidden_states.reshape(-1, H)
        T = x.shape[0]
        logits = x @ W_router.T
        probs = jax.nn.softmax(logits.astype(jnp.float32), axis=-1)
        rw, sel = jax.lax.top_k(probs, TOP_K)
        rw = rw.astype(x.dtype)
        combine = jnp.zeros((T, E), x.dtype).at[jnp.arange(T)[:, None], sel].add(rw)
        sh = _silu_and_mul(x @ Ws_gate_up, I_SH) @ Ws_down
        shared_out = sh * jax.nn.sigmoid(x @ W_sgate.T)
        gu = jnp.einsum('th,ehi->eti', x, We_gate_up)
        h = _silu_and_mul(gu, I_MOE)
        eo = jnp.einsum('eti,eih->eth', h, We_down)
        sparse_out = jnp.einsum('eth,te->th', eo, combine)
        return (shared_out + sparse_out).reshape(orig_shape)
    x = x + jnp.tanh(g_xattn[0]) * _L0_xattn_ref(_layernorm(x, axis=-1), ctx_1024, L0_xattn_Wq, L0_xattn_Wk, L0_xattn_Wv, L0_xattn_Wo, L0_xattn_gq, L0_xattn_gk)
    x = x + jnp.tanh(g_ffn[0]) * _L0_ffn_ref(_layernorm(x, axis=-1), L0_ffn_gate_W_packed, L0_ffn_gate_scales, L0_ffn_up_W_packed, L0_ffn_up_scales, L0_ffn_down_W_packed, L0_ffn_down_scales)
    x = x + jnp.tanh(g_xattn[1]) * _L1_xattn_ref(_layernorm(x, axis=-1), ctx_1024, mask_BxS2_bf1, L1_xattn_Wq, L1_xattn_Wk, L1_xattn_Wv, L1_xattn_Wo)
    x = x + jnp.tanh(g_ffn[1]) * _L1_ffn_ref(_layernorm(x, axis=-1), L1_ffn_W_router, L1_ffn_W_sgate, L1_ffn_Ws_gate_up, L1_ffn_Ws_down, L1_ffn_We_gate_up, L1_ffn_We_down)
    return x

_drawn_inputs = setup_inputs


def setup_inputs(seed=0):
    import zlib

    import numpy as np

    out = dict(_drawn_inputs(seed))
    spreads = {'g_ffn': (-1.0, 0.6), 'L0_xattn_gq': (1.0, 0.2), 'L0_xattn_gk': (1.0, 0.2)}
    factors = {'L1_xattn_Wq': 8.0,
     'L1_xattn_Wk': 8.0,
     'L1_xattn_Wv': 6.415,
     'L1_xattn_Wo': 6.33,
     'L1_ffn_W_router': 8.0,
     'L1_ffn_W_sgate': 8.0,
     'L1_ffn_Ws_gate_up': 8.0,
     'L1_ffn_Ws_down': 8.0,
     'L1_ffn_We_gate_up': 8.0,
     'L1_ffn_We_down': 8.0}
    for name, (base, spread) in spreads.items():
        noise = np.random.default_rng([zlib.crc32(name.encode()), seed]).standard_normal(out[name].shape)
        drawn = base * np.exp(spread * noise) if base else spread * noise
        out[name] = jnp.asarray(drawn.astype(out[name].dtype))
    for name, factor in factors.items():
        out[name] = (out[name] * factor).astype(out[name].dtype)
    return out
```

```python
from contextlib import ExitStack

import concourse.bass as bass
from concourse import mybir

F32 = mybir.dt.float32
F32R = mybir.dt.float32r
I32 = mybir.dt.int32
U8 = mybir.dt.uint8
ALU = mybir.AluOpType
ACT = mybir.ActivationFunctionType
AX = mybir.AxisListType

P = 128
B = 16
D = 256
KD = D // P
H = 16
GB = 4
G = B // GB
N = GB * P
QH = 4
NQ = H // QH
EPS = 1e-5
MASKED = -float(2 ** 100)
SKV = 8
I_SH, I_MOE, E = 704, 176, 8
NF0 = 2048
NF1 = I_SH + E * I_MOE


def f32(ap):
    return ap.bitcast(F32)


class Core:

    def __init__(self, nc, ctx):
        self.nc, self.ctx = nc, ctx
        self.x = self.sb("x_sb", [P, B, D])
        self.ident = self.sb("ident", [P, P])
        self.gates = self.sb("gates", [P, 4])
        self.half = self.sb("half", [P, 16])
        self.ones = self.sb("ones", [P, 1])
        self.bank = [ctx.enter_context(nc.psum_tensor(f"bank{i}", [P, N], F32)) for i in range(8)]

        self.sems = []

    def sem(self, name):
        self.sems.append(self.nc.alloc_semaphore(name))
        return self.sems[-1]

    def recycle_semaphores(self):
        self.nc.clear_and_free_semaphores(self.sems)
        self.sems = []
        self.nc.all_engine_barrier()

    def sb(self, name, shape, dt=F32):
        return self.ctx.enter_context(self.nc.sbuf_tensor(name, shape, dt))


def three_pass(nc, out, w, x, start, stop):
    nc.tensor.matmul(out, w[0], x[0], start=start, stop=False)
    nc.tensor.matmul(out, w[0], x[1], start=False, stop=False)
    return nc.tensor.matmul(out, w[1], x[0], start=False, stop=stop)


def moments(nc, dve, m, bn, mv, sem):
    mean_e, dev_e, mean_o, dev_o = (bn[:, :, k] for k in (1, 2, 4, 5))
    dve.wait_ge(sem("stats_ready"), m * GB + GB)
    nc.vector.tensor_tensor(mv[:, 2, :], mean_e, mean_o, ALU.add)
    nc.vector.tensor_tensor(mv[:, 3, :], mean_e, mean_o, ALU.subtract)
    nc.vector.tensor_tensor(mv[:, 4, :], dev_e, dev_o, ALU.add).then_inc(sem("halves_ready"), 1)
    dve.wait_ge(sem("halves_ready"), m * 2 + 1)
    nc.vector.tensor_scalar(mv[:, 0, :], mv[:, 2, :], 0.5, None, ALU.mult)
    nc.vector.scalar_tensor_tensor(out=mv[:, 5, :], in0=mv[:, 3, :], scalar=0.25, in1=mv[:, 3, :], op0=ALU.mult, op1=ALU.mult)
    nc.vector.tensor_scalar(mv[:, 6, :], mv[:, 4, :], 1.0 / D, EPS, ALU.mult, ALU.add).then_inc(sem("halves_ready"), 1)
    dve.wait_ge(sem("halves_ready"), m * 2 + 2)
    nc.vector.tensor_tensor(mv[:, 1, :], mv[:, 6, :], mv[:, 5, :], ALU.add).then_inc(sem("moments_ready"), 1)


def credit(name):
    return {"k_summed": 2, "E": 1, "pc_ready": 1, "out_read": 1, "h_ready": 1}.get(name, 0)


def flat(ap):
    return ap.rearrange("p a b -> p (a b)")


def setup_stage(nc, core, x, g_xattn, g_ffn):
    with ExitStack() as ctx:
        graw = ctx.enter_context(nc.sbuf_tensor("graw", [P, 4], F32))
        loaded = core.sem("gates_loaded")
        x_loaded = core.sem("x_loaded")
        zeroed = core.sem("ident_zeroed")
        made = core.sem("constants_made")
        with nc.Block() as block:

            @block.sync
            def _(sp):
                sp.dma_start(graw[:, 0:2], g_xattn.partition_broadcast(P)).then_inc(loaded, 16)
                sp.dma_start(graw[:, 2:4], g_ffn.partition_broadcast(P)).then_inc(loaded, 16)
                for g in range(G):
                    sp.dma_start(core.x[:, g * GB:(g + 1) * GB, :],
                                 x[g * GB:(g + 1) * GB].rearrange("b s d -> s b d")).then_inc(x_loaded, 16)
                sp.wait_ge(x_loaded, 16 * G)

            @block.gpsimd
            def _(pool):
                nc.gpsimd.memset(core.ident[:, :], 0.0).then_inc(zeroed, 1)
                nc.gpsimd.memset(core.half[:, :], -0.5).then_inc(made, 1)
                nc.gpsimd.memset(core.ones[:, :], 1.0).then_inc(made, 1)
                pool.wait_ge(zeroed, 1)
                nc.gpsimd.affine_select(out=core.ident[:, :], in_=core.ident[:, :], compare_op=ALU.not_equal,
                                        fill=1.0, base=0, pattern=[[-1, P]], channel_multiplier=1).then_inc(made, 1)
                pool.wait_ge(made, 3)

            @block.scalar
            def _(act):
                act.wait_ge(loaded, 32)
                nc.scalar.activation(core.gates[:, :], graw[:, :], ACT.Tanh)



def prepare_attention(nc, core, layer, Wq, Wk, Wv, Wo, w, extra):
    kv = H if layer == 0 else SKV
    rep = H // kv
    nq_t = 0 if layer == 0 else KD * H // 4
    nk_t = 0 if layer == 0 else kv // 4
    nv_t = kv // 4
    with ExitStack() as ctx:
        def sb(name, shape, dt=F32):
            return ctx.enter_context(nc.sbuf_tensor(f"{name}_p{layer}", shape, dt))

        def sem(name):
            return core.sem(f"{name}_p{layer}")

        q_raw = sb("q_raw", [P, KD, H * P])
        k_raw = sb("k_raw", [P, kv * P])
        v_raw = sb("v_raw", [P, kv * P])
        o_raw = sb("o_raw", [P, H, D])
        v_t = sb("v_t", [P, kv, P])
        loaded_q, loaded_k, loaded_v, loaded_o = (sem(f"loaded_{n}") for n in "qkvo")
        filled, hi_done, drained = sem("bank_filled"), sem("hi_done"), sem("bank_drained")
        if layer == 1:
            q_t = sb("q_t", [P, H, KD, P])
            k_t = sb("k_t", [P, kv, P])
            ctx_raw, maskrow, maskcol8 = sb("ctx_raw", [P, B, P]), sb("maskrow", [1, B * P], U8), sb("maskcol8", [P, B], U8)
            loaded_c, loaded_m, zeroed = sem("loaded_c"), sem("loaded_m"), sem("zeroed")

        units = [("v_t", i) for i in range(nv_t)] + [("q_t", i) for i in range(nq_t)] + [("k_t", i) for i in range(nk_t)]
        if layer == 1:
            units += [("ctx", i) for i in range(G)]
        n_t = len(units)
        units += [("vo", i) for i in range(H // 2)] + ([("m", i) for i in range(KD * H // 4)] if layer else [])
        with nc.Block() as block:

            @block.sync
            def _(sp):
                sp.dma_start(v_raw[:, :], Wv).then_inc(loaded_v, 16)
                sp.dma_start(o_raw[:, :, :], Wo.rearrange("(h d) e -> d h e", d=P)).then_inc(loaded_o, 16)
                sp.dma_start(q_raw[:, :, :], Wq.rearrange("(k c) n -> c k n", c=P)).then_inc(loaded_q, 16)
                sp.dma_start(k_raw[:, :], Wk).then_inc(loaded_k, 16)
                if layer == 1:
                    sp.dma_start(ctx_raw[:, :, :], extra["ctx"].rearrange("b s c -> s b c")).then_inc(loaded_c, 16)
                    sp.dma_start(maskrow[:, :], extra["mask"].rearrange("(a b) s -> a (b s)", a=1)).then_inc(loaded_m, 16)
                    with nc.allow_non_contiguous_dma("2 KB of mask, transposed"):
                        sp.dma_start(maskcol8[:, :], extra["mask"].rearrange("b s -> s b")).then_inc(loaded_m, 16)

            @block.tensor
            def _(pe):
                for n, (kind, i) in enumerate(units):
                    out = core.bank[n % 8]
                    if n >= 8:
                        pe.wait_ge(drained, n - 7)
                    if kind == "v_t":
                        pe.wait_ge(loaded_v, 16)
                        for a in range(4):
                            last = nc.tensor.transpose(out[:, a * P:(a + 1) * P], v_raw[:, (4 * i + a) * P:(4 * i + a + 1) * P], core.ident[:, :])
                    elif kind == "q_t":
                        pe.wait_ge(loaded_q, 16)
                        for a in range(4):
                            h, k = divmod(4 * i + a, KD)
                            last = nc.tensor.transpose(out[:, a * P:(a + 1) * P], q_raw[:, k, h * P:(h + 1) * P], core.ident[:, :])
                    elif kind == "k_t":
                        pe.wait_ge(loaded_k, 16)
                        for a in range(4):
                            last = nc.tensor.transpose(out[:, a * P:(a + 1) * P], k_raw[:, (4 * i + a) * P:(4 * i + a + 1) * P], core.ident[:, :])
                    elif kind == "ctx":
                        pe.wait_ge(loaded_c, 16)
                        for a in range(4):
                            last = nc.tensor.transpose(out[:, a * P:(a + 1) * P], ctx_raw[:, 4 * i + a, :], core.ident[:, :])
                    elif kind == "vo":
                        if i == 0:
                            pe.wait_ge(loaded_o, 16)
                            pe.wait_ge(drained, n_t)
                        for a in range(2):
                            h = 2 * i + a
                            last = nc.tensor.matmul(out[:, a * D:(a + 1) * D], v_t[:, h // rep, :], o_raw[:, h, :], start=True, stop=True)
                    else:
                        for a in range(4):
                            h, k = divmod(4 * i + a, KD)
                            last = nc.tensor.matmul(out[:, a * P:(a + 1) * P], q_t[:, h, k, :], k_t[:, h // rep, :], start=True, stop=True)
                    last.then_inc(filled, 1)

            def target(kind, i, part):
                if kind == "vo":
                    return flat(w["vo"][part][:, 2 * i:2 * i + 2, :])
                return w["q"][part].rearrange("p k (h c) -> p h k c", c=P)[:, 2 * i:2 * i + 2, :, :]

            def bank_view(n, kind):
                return core.bank[n % 8][:, :].rearrange("p (h k c) -> p h k c", h=2, k=KD) if kind == "m" else core.bank[n % 8][:, :]

            @block.scalar
            def _(act):
                if layer == 0:
                    act.wait_ge(loaded_q, 16)
                    for k in range(KD):
                        nc.scalar.activation(w["q"][0][:, k, :], q_raw[:, k, :], ACT.Copy).then_inc(hi_done, 1)
                    act.wait_ge(loaded_k, 16)
                    nc.scalar.activation(w["k"][0][:, :], k_raw[:, :], ACT.Copy).then_inc(hi_done, 1)
                for n, (kind, i) in enumerate(units):
                    act.wait_ge(filled, n + 1)
                    if kind == "v_t":
                        nc.scalar.activation(flat(v_t[:, 4 * i:4 * i + 4, :]), core.bank[n % 8][:, :], ACT.Copy).then_inc(drained, 1)
                    elif kind == "q_t":
                        nc.scalar.activation(q_t[:, 2 * i:2 * i + 2, :, :].rearrange("p h k c -> p (h k c)"), core.bank[n % 8][:, :], ACT.Copy).then_inc(drained, 1)
                    elif kind == "ctx":
                        nc.scalar.activation(w["ctx_t"][:, i * N:(i + 1) * N], core.bank[n % 8][:, :], ACT.Copy).then_inc(drained, 1)
                    elif kind == "k_t":
                        nc.scalar.activation(flat(k_t[:, 4 * i:4 * i + 4, :]), core.bank[n % 8][:, :], ACT.Copy).then_inc(drained, 1)
                    else:
                        nc.scalar.activation(target(kind, i, 0), bank_view(n, kind), ACT.Copy).then_inc(hi_done, 1)

            @block.vector
            def _(dve):
                done = 0
                if layer == 0:
                    for k in range(KD):
                        done += 1
                        dve.wait_ge(hi_done, done)
                        nc.vector.tensor_tensor(w["q"][1][:, k, :], q_raw[:, k, :], f32(w["q"][0][:, k, :]), ALU.subtract)
                    done += 1
                    dve.wait_ge(hi_done, done)
                    nc.vector.tensor_tensor(w["k"][1][:, :], k_raw[:, :], f32(w["k"][0][:, :]), ALU.subtract)
                else:
                    nc.vector.memset(f32(w["bias"][:, :]), 0.0).then_inc(zeroed, 1)
                    dve.wait_ge(loaded_m, 32)
                    dve.wait_ge(zeroed, 1)
                    nc.vector.tensor_scalar(w["bias"][0:1, :], maskrow[:, :], 1.0, -MASKED, ALU.subtract, ALU.mult)
                    nc.vector.tensor_copy(w["mask_col"][:, :], maskcol8[:, :])
                    nc.vector.memset(f32(w["bias_row"][:, :]), 0.0).then_inc(zeroed, 1)
                    dve.wait_ge(zeroed, 2)
                    nc.vector.memset(f32(w["bias_row"][0:1, :]), 1.0)
                for n, (kind, i) in enumerate(units):
                    if n < n_t:
                        continue
                    done += 1
                    dve.wait_ge(hi_done, done)
                    nc.vector.tensor_tensor(target(kind, i, 1), bank_view(n, kind), f32(target(kind, i, 0)),
                                            ALU.subtract).then_inc(drained, 1)



def quad_order(layer, j):
    lna = [("LNA", 0)] if j == 2 else []
    lnb = [("LNB", 0)] if j == 2 else []
    ct = [("CT", 0), ("CT", 1)] if j == 2 and layer == 0 else []
    x = [("X", 0), ("X", 1)] if j == 3 else []
    out = [("OUT", 0)] if j == NQ else []
    e0, e1 = ([("E", 0)], [("E", 1)]) if j == NQ else ([], [])
    cn = [("CN", 0)] if j == NQ - 1 else []
    if layer == 0:
        return ([("EX", 0), ("S", 1), ("K", 0), ("R", 0), ("W", 0), ("EX", 1), ("K", 1), ("T", 0), ("W", 1), ("R", 1), ("K", 2), ("C", 0)]
                + x + lna + [("S", 2), ("K", 3), ("T", 1), ("EX", 2), ("W", 2), ("KN", 0), ("Q", 0), ("C", 1), ("R", 2), ("W", 3)] + out
                + [("KH", 0), ("S", 3), ("Q", 1), ("T", 2), ("EX", 3), ("KH", 1)] + e0 + [("Q", 2), ("KH", 2), ("C", 2), ("R", 3)] + e1
                + [("Q", 3), ("KT", 0), ("KH", 3), ("SSQ", 0)] + lnb + [("KT", 1), ("T", 3), ("KT", 2), ("KT", 3), ("S", 4), ("C", 3)] + cn + ct)
    return ([("EX", 0), ("S", 1), ("W", 0), ("R", 0)] + x + [("Q", 0), ("EX", 1), ("T", 0), ("W", 1), ("R", 1), ("C", 0)] + lna
            + [("Q", 1), ("S", 2), ("W", 2), ("T", 1), ("EX", 2), ("W", 3)] + out + [("R", 2), ("C", 1), ("S", 3)] + e0
            + [("T", 2)] + e1 + [("Q", 2), ("EX", 3), ("R", 3), ("Q", 3), ("C", 2)] + lnb + [("T", 3), ("S", 4), ("C", 3)] + cn)


NEXT = ("LNA", "LNB", "X", "CT", "CN")
PROJ = ("K", "KN", "KH", "Q", "KT", "SSQ")
RING = ("X", "CT", "K", "Q", "KT", "SSQ", "E")


def orders_of(layer):
    def quad(j):
        return [(name, i, j) for name, i in quad_order(layer, j)]

    j = NQ - 1
    if layer == 0:
        first = ([("LNA", 0), ("LNB", 0), ("CT", 0), ("CT", 1)] + [("K", b) for b in range(GB)] + [("X", 0), ("X", 1), ("KN", 0)]
                 + [("KH", b) for b in range(GB)] + [("Q", b) for b in range(GB)] + [("SSQ", 0)] + [("KT", b) for b in range(GB)])
    else:
        first = [("LNA", 0), ("LNB", 0), ("X", 0), ("X", 1)] + [("Q", b) for b in range(QH)]
    start = [(name, i, j) for name, i in first + [("S", 4), ("CN", 0)]]
    start += [s for s in quad(NQ) if s[0] not in ("W", "OUT", "E")]
    body = quad(1) + quad(2) + quad(3) + quad(4)
    last = [s for s in quad(1) + quad(2) if s[0] not in NEXT]
    last += [s for s in quad(3) if s[0] not in NEXT + PROJ and s[:2] != ("S", 4)]
    last += [("W", h, NQ) for h in range(QH)] + [("OUT", 0, NQ), ("E", 0, NQ), ("E", 1, NQ)]
    return {"start": start, "body": body, "last": last}


def attention(nc, core, layer, w, ctx_dram):
    L = layer
    with ExitStack() as ctx:
        def sb(name, shape, dt=F32):
            return ctx.enter_context(nc.sbuf_tensor(f"{name}_a{L}", shape, dt))

        def pair(name, shape):
            return [sb(f"{name}_{p}", shape, F32R) for p in ("hi", "lo")]

        sems = {}

        def sem(name):
            if name not in sems:
                sems[name] = core.sem(f"{name}_a{L}")
            return sems[name]

        q = sb("q", [P, 2, QH, N])
        probs = sb("probs", [P, 2, QH, P])
        pt = pair("pt", [P, QH * P])
        pc = pair("pc", [P, 2, GB, QH, P])
        xt = pair("xt", [P, KD, N])
        cn = pair("cn", [P, GB, P])
        ctx_raw = sb("ctx_raw", [P, GB, P])
        out_sb = sb("out_sb", [P, KD, N])
        bn = sb("bn", [P, GB, 6])
        mv = sb("mv", [P, 7, GB])
        rstd = sb("rstd", [P, GB])
        nmax = sb("nmax", [P, 2, QH])
        nbias = sb("nbias", [P, 2, QH])
        den = sb("den", [P, 2, QH])
        rden = sb("rden", [P, 2, QH])
        if L == 0:
            q_sq = sb("q_sq", [P, QH, N])
            xn = q_sq[:, 2:4, :].rearrange("p a (t d) -> p (a t) d", d=D)
            k_raw = sb("k_raw", [P, GB, QH * P])
            k_sq = sb("k_sq", [P, 2, QH * P])
            kt = sb("kt", [P, GB, QH * P])
            ct = pair("ct", [P, GB, P])
            k_ss = sb("k_ss", [P, GB * QH])
            k_r = sb("k_r", [P, GB * QH])
            q_ss = sb("q_ss", [P, GB * QH])
            q_r = sb("q_r", [P, 2, GB * QH])
        else:
            xn = sb("xn", [P, GB, D])
            cm = sb("cm", [P, GB, P])
        out_t = core.bank[0:2]
        proj_bank, s_bank, t_bank, c_bank = core.bank[2:4], core.bank[4:6], core.bank[6], core.bank[7]
        root = float(P) ** -0.5

        def quads(g, j):
            return g * NQ + j

        def nth(per, m, i):
            return m * per + (i + 1)

        def round_of(name, g, j):
            if name in PROJ:
                return quads(g, j + 1)
            if name in NEXT:
                return g + 1
            if name in ("OUT", "E"):
                return g
            return quads(g, j)

        per = {"X": 2, "CT": 2, "K": 4, "Q": 4, "KT": 4, "SSQ": 1, "E": 2}
        filled = {n: sem(f"{n.lower()}_filled") for n in per}
        released = {"X": sem("x_split"), "CT": sem("ct_split"), "K": sem("k_copied"), "Q": sem("q_copied"), "KT": sem("kt_copied"),
                    "SSQ": sem("ssq_copied"), "E": sem("x_updated")}
        orders = orders_of(L)
        rings = {}
        for part, order in orders.items():
            ring = [s for s in order if s[0] in RING]
            shift = len(ring) % 2 if part == "start" else 0
            rings[part] = ring, {s: (n + shift) % 2 for n, s in enumerate(ring)}
        assert len(rings["body"][0]) % 2 == 0 and rings["start"][0][-2:] == rings["body"][0][-2:]

        def walk(emit):
            for s in orders["start"]:
                emit("start", -1, *s)
            with emit.engine.Fori(0, G - 1) as g:
                for s in orders["body"]:
                    emit("body", g, *s)
            for s in orders["last"]:
                emit("last", G - 1, *s)

        with nc.Block() as block:

            @block.sync
            def _(sp):
                def load(g):
                    src = ctx_dram[bass.ds(g * GB, GB)].rearrange("b s c -> s b c")
                    sp.dma_start(ctx_raw[:, :, :], src).then_inc(sem("ctx_loaded"), 16)

                load(0)
                with sp.Fori(1, G) as g:
                    sp.wait_ge(sem("cn_ready"), g)
                    load(g)

            @block.tensor
            def _(pe):
                def bank_free(part, g, step):
                    ring, slots = rings[part]
                    at = ring.index(step)
                    if at < 2 and part == "start":
                        return proj_bank[slots[step]]
                    before, gb = (ring, g) if at >= 2 else (rings["body"][0], g - 1)
                    n, i, j = before[at - 2]
                    pe.wait_ge(released[n], nth(per[n], round_of(n, gb, j), i))
                    return proj_bank[slots[step]]

                def step(part, g, name, i, j):
                    m = round_of(name, g, j)
                    if name in RING:
                        bank = bank_free(part, g, (name, i, j))
                    if name == "X":
                        if i == 0:
                            pe.wait_ge(sem("xn_ready"), m + 1)
                        for b in range(GB):
                            last = nc.tensor.transpose(bank[:, b * P:(b + 1) * P], xn[:, b, i * P:(i + 1) * P], core.ident[:, :])
                    elif name == "CT":
                        if i == 0:
                            pe.wait_ge(sem("ctx_loaded"), m * 16 + 16)
                        for a in range(2):
                            last = nc.tensor.transpose(bank[:, a * P:(a + 1) * P], ctx_raw[:, 2 * i + a, :], core.ident[:, :])
                    elif name == "K":
                        if i % 2 == 0:
                            pe.wait_ge(sem("ct_split"), nth(2, g + (j + 1) // NQ, i // 2))
                        t = (j + 1) % NQ
                        cols = slice(t * QH * P, (t + 1) * QH * P)
                        last = three_pass(nc, bank[:, :], [c[:, i, :] for c in ct], [k[:, cols] for k in w["k"]], True, True)
                    elif name == "Q":
                        if i == 0:
                            pe.wait_ge(sem("x_split"), nth(2, g + (j + 1) // NQ, 1))
                        h = (j + 1) % NQ * QH + i
                        for k in range(KD):
                            last = three_pass(nc, bank[:, :], [a[:, k, h * P:(h + 1) * P] for a in w["q"]], [a[:, k, :] for a in xt],
                                              k == 0, k == KD - 1)
                    elif name == "KT":
                        pe.wait_ge(sem("kh_ready"), nth(4, m, i))
                        for h in range(QH):
                            last = nc.tensor.transpose(bank[:, h * P:(h + 1) * P], k_raw[:, i, h * P:(h + 1) * P], core.ident[:, :])
                    elif name == "SSQ":
                        pe.wait_ge(sem("q_squared"), nth(4, m, QH - 1))
                        for b in range(GB):
                            for h in range(QH):
                                last = nc.tensor.matmul(bank[:, b * QH + h:b * QH + h + 1], q_sq[:, h, b * P:(b + 1) * P], core.ones[:, :],
                                                        start=True, stop=True)
                    elif name == "S":
                        j, i = j + i // GB, i % GB
                        if i == 0:
                            pe.wait_ge(sem("q_copied"), nth(4, quads(g, j), 3))
                            if L == 0:
                                pe.wait_ge(sem("kt_copied"), nth(4, quads(g, j), 3))
                        bank = s_bank[i % 2]
                        if L == 1:
                            batch = (g + j // NQ) * GB + i
                            bias = w["bias"][:, bass.ds(batch * P, P)].unsqueeze(1).to_broadcast([P, QH, P])
                            nc.tensor.matmul(bank[:, :], w["bias_row"][:, :], bias, start=True, stop=False)
                            keys = w["ctx_t"][:, bass.ds(batch * P, P)]
                        for h in range(QH):
                            last = nc.tensor.matmul(bank[:, h * P:(h + 1) * P], q[:, j % 2, h, i * P:(i + 1) * P],
                                                    kt[:, i, h * P:(h + 1) * P] if L == 0 else keys, start=L == 0, stop=L == 0 or h == QH - 1)
                        last.then_inc(sem("s_filled"), 1)
                        return
                    elif name == "T":
                        pe.wait_ge(sem("probs_scaled"), nth(4, m, i))
                        for h in range(QH):
                            last = nc.tensor.transpose(t_bank[:, h * P:(h + 1) * P], probs[:, i % 2, h, :], core.ident[:, :])
                        last.then_inc(sem("t_filled"), 1)
                        return
                    elif name == "C":
                        if i == 0 and j == NQ:
                            pe.wait_ge(sem("cn_ready"), g + 2)
                        pe.wait_ge(sem("pt_ready"), nth(4, m, i))
                        pe.wait_ge(sem("pc_ready"), m * 4 + i + credit("pc_ready"))
                        last = three_pass(nc, c_bank[:, :], [a[:, i, :] for a in cn], [a[:, :] for a in pt], True, True)
                        last.then_inc(sem("c_filled"), 1)
                        return
                    elif name == "W":
                        if i == 0:
                            pe.wait_ge(sem("pc_ready"), nth(4, m - 1, GB - 1) + credit("pc_ready"))
                        if i == 0 and j == 1:
                            pe.wait_ge(sem("out_read"), 2 * g + credit("out_read"))
                        hh = (j - 1) * QH + i
                        for e in range(KD):
                            last = three_pass(nc, out_t[e][:, :], [a[:, hh, e * P:(e + 1) * P] for a in w["vo"]],
                                              [a[:, (j - 1) % 2, :, i, :] for a in pc], hh == 0, hh == H - 1)
                        last.then_inc(sem("w_done"), 1)
                        return
                    elif name == "E":
                        if i == 0:
                            pe.wait_ge(sem("out_read"), 2 * g + 2 + credit("out_read"))
                        for a in range(2):
                            for e in range(KD):
                                last = nc.tensor.transpose(bank[:, (a * KD + e) * P:(a * KD + e + 1) * P],
                                                           out_sb[:, e, (2 * i + a) * P:(2 * i + a + 1) * P], core.ident[:, :])
                    else:
                        return
                    last.then_inc(filled[name], 1)

                step.engine = pe
                walk(step)

            @block.scalar
            def _(act):
                def step(part, g, name, i, j):
                    m = round_of(name, g, j)
                    bank = proj_bank[rings[part][1][(name, i, j)]] if name in RING else None
                    if name in ("X", "CT", "KT") or name == "Q" and L == 1:
                        act.wait_ge(filled[name], nth(per[name], m, i))
                    if name == "X":
                        nc.scalar.activation(xt[0][:, i, :], bank[:, :], ACT.Copy).then_inc(sem("x_hi_ready"), 1)
                    elif name == "CT":
                        nc.scalar.activation(flat(ct[0][:, 2 * i:2 * i + 2, :]), bank[:, 0:2 * P], ACT.Copy).then_inc(sem("ct_hi_ready"), 1)
                    elif name == "KT":
                        nc.scalar.activation(kt[:, i, :], bank[:, :], ACT.Copy, scale=w["gain"][:, 0:1]).then_inc(sem("kt_copied"), 1)
                    elif name == "Q" and L == 0:
                        act.wait_ge(sem("q_copied"), nth(4, m, i))
                        nc.scalar.activation(q_sq[:, i, :], q[:, (j + 1) % 2, i, :], ACT.Square).then_inc(sem("q_squared"), 1)
                    elif name == "Q":
                        nc.scalar.activation(q[:, (j + 1) % 2, i, :], bank[:, :], ACT.Copy).then_inc(sem("q_copied"), 1)
                    elif name == "K":
                        act.wait_ge(sem("k_summed"), nth(4, m, i) - 2 + credit("k_summed"))
                        act.wait_ge(sem("k_copied"), nth(4, m, i))
                        nc.scalar.activation(k_sq[:, i % 2, :], k_raw[:, i, :], ACT.Square).then_inc(sem("k_squared"), 1)
                    elif name == "EX":
                        act.wait_ge(sem("bias_ready"), nth(4, m, i))
                        for h in range(QH):
                            scale = q_r[:, j % 2, i * QH + h:i * QH + h + 1] if L == 0 else root
                            last = nc.scalar.activation(probs[:, i % 2, h, :], s_bank[i % 2][:, h * P:(h + 1) * P], ACT.Exp,
                                                        bias=nbias[:, i % 2, h:h + 1], scale=scale, accum_out=den[:, i % 2, h:h + 1])
                        last.then_inc(sem("exp_done"), 1)
                    elif name == "T":
                        act.wait_ge(sem("t_filled"), nth(4, m, i))
                        nc.scalar.activation(pt[0][:, :], t_bank[:, :], ACT.Copy).then_inc(sem("pt_hi_ready"), 1)
                    elif name == "C":
                        act.wait_ge(sem("c_filled"), nth(4, m, i))
                        nc.scalar.activation(flat(pc[0][:, j % 2, i, :, :]), c_bank[:, :], ACT.Copy).then_inc(sem("pc_hi_ready"), 1)
                    elif name == "OUT":
                        act.wait_ge(sem("w_done"), g * H + H)
                        for e in range(KD):
                            nc.scalar.activation(out_sb[:, e, :], out_t[e][:, :], ACT.Copy).then_inc(sem("out_read"), 1)
                    elif name == "CN":
                        if L == 0:
                            act.wait_ge(sem("ctx_loaded"), m * 16 + 16)
                            src = ctx_raw
                        else:
                            act.wait_ge(sem("ctx_masked"), m + 1)
                            src = cm
                        nc.scalar.activation(flat(cn[0][:, :, :]), flat(src[:, :, :]), ACT.Copy).then_inc(sem("cn_hi_ready"), 1)

                act.sem_inc(sem("out_read"), credit("out_read"))
                step.engine = act
                walk(step)

            @block.vector
            def _(dve):
                def step(part, g, name, i, j):
                    m = round_of(name, g, j)
                    bank = proj_bank[rings[part][1][(name, i, j)]] if name in RING else None
                    if name == "LNA":
                        for b in range(GB):
                            nc.vector.bn_stats(bn[:, b, :], flat(core.x[:, bass.ds(m * GB + b, 1), :])).then_inc(sem("stats_ready"), 1)
                        moments(nc, dve, m, bn, mv, sem)
                    elif name == "LNB":
                        dve.wait_ge(sem("rstd_ready"), m + 1)
                        for b in range(GB):
                            last = nc.vector.tensor_scalar(xn[:, b, :], flat(core.x[:, bass.ds(m * GB + b, 1), :]), mv[:, 0, b:b + 1],
                                                           rstd[:, b:b + 1], ALU.subtract, ALU.mult)
                        last.then_inc(sem("xn_ready"), 1)
                    elif name == "X":
                        dve.wait_ge(sem("x_hi_ready"), nth(2, m, i))
                        nc.vector.tensor_tensor(xt[1][:, i, :], bank[:, :], f32(xt[0][:, i, :]), ALU.subtract).then_inc(sem("x_split"), 1)
                    elif name == "CT":
                        dve.wait_ge(sem("ct_hi_ready"), nth(2, m, i))
                        hi, lo = (flat(c[:, 2 * i:2 * i + 2, :]) for c in ct)
                        nc.vector.tensor_tensor(lo, bank[:, 0:2 * P], f32(hi), ALU.subtract).then_inc(sem("ct_split"), 1)
                    elif name == "Q" and L == 0:
                        dve.wait_ge(filled[name], nth(4, m, i))
                        nc.vector.tensor_copy(q[:, (j + 1) % 2, i, :], bank[:, :]).then_inc(sem("q_copied"), 1)
                    elif name == "K":
                        dve.wait_ge(filled[name], nth(4, m, i))
                        nc.vector.tensor_copy(k_raw[:, i, :], bank[:, :]).then_inc(sem("k_copied"), 1)
                        dve.wait_ge(sem("k_squared"), nth(4, m, i))
                        nc.vector.tensor_reduce(k_ss[:, i * QH:(i + 1) * QH], k_sq[:, i % 2, :].rearrange("p (h d) -> p h d", d=P), AX.X,
                                                ALU.add).then_inc(sem("k_summed"), 1)
                    elif name == "KN":
                        dve.wait_ge(sem("k_summed"), nth(4, m, GB - 1) + credit("k_summed"))
                        nc.vector.tensor_scalar(k_ss[:, :], k_ss[:, :], P * EPS, None, ALU.add).then_inc(sem("k_ss_ready"), 1)
                    elif name == "SSQ":
                        dve.wait_ge(filled[name], m + 1)
                        nc.vector.tensor_scalar(q_ss[:, :], bank[:, 0:GB * QH], P * EPS, None, ALU.add).then_inc(sem("ssq_copied"), 1)
                    elif name == "S":
                        m, j, i = m + i // GB, j + i // GB, i % GB
                        dve.wait_ge(sem("s_filled"), nth(4, m, i))
                        nc.vector.tensor_reduce(nmax[:, i % 2, :], s_bank[i % 2][:, :].rearrange("p (h s) -> p h s", s=P), AX.X, ALU.max,
                                                negate=True).then_inc(sem("max_ready"), 1)
                        if L == 0 and i == 0:
                            dve.wait_ge(sem("q_norm_ready"), m + 1)
                        dve.wait_ge(sem("max_ready"), nth(4, m, i))
                        if L == 0:
                            last = nc.vector.tensor_tensor(nbias[:, i % 2, :], nmax[:, i % 2, :], q_r[:, j % 2, i * QH:(i + 1) * QH], ALU.mult)
                        else:
                            last = nc.vector.tensor_scalar(nbias[:, i % 2, :], nmax[:, i % 2, :], root, None, ALU.mult)
                        last.then_inc(sem("bias_ready"), 1)
                    elif name == "R":
                        dve.wait_ge(sem("exp_done"), nth(4, m, i))
                        nc.vector.reciprocal(rden[:, i % 2, :], den[:, i % 2, :]).then_inc(sem("rden_ready"), 1)
                    elif name == "T":
                        dve.wait_ge(sem("pt_hi_ready"), nth(4, m, i))
                        nc.vector.tensor_tensor(pt[1][:, :], t_bank[:, :], f32(pt[0][:, :]), ALU.subtract).then_inc(sem("pt_ready"), 1)
                    elif name == "C":
                        dve.wait_ge(sem("pc_hi_ready"), nth(4, m, i))
                        hi, lo = (flat(c[:, j % 2, i, :, :]) for c in pc)
                        nc.vector.tensor_tensor(lo, c_bank[:, :], f32(hi), ALU.subtract).then_inc(sem("pc_ready"), 1)
                    elif name == "CN":
                        if L == 1:
                            dve.wait_ge(sem("ctx_loaded"), m * 16 + 16)
                            mask = w["mask_col"][:, bass.ds(m * GB, GB)].unsqueeze(2).to_broadcast([P, GB, P])
                            nc.vector.tensor_tensor(cm[:, :, :], ctx_raw[:, :, :], mask, ALU.mult).then_inc(sem("ctx_masked"), 1)
                        dve.wait_ge(sem("cn_hi_ready"), m + 1)
                        src = ctx_raw if L == 0 else cm
                        nc.vector.tensor_tensor(flat(cn[1][:, :, :]), flat(src[:, :, :]), f32(flat(cn[0][:, :, :])),
                                                ALU.subtract).then_inc(sem("cn_ready"), 1)
                    elif name == "E":
                        dve.wait_ge(filled[name], nth(2, m, i))
                        here = flat(core.x[:, bass.ds(g * GB + 2 * i, 2), :])
                        nc.vector.scalar_tensor_tensor(out=here, in0=bank[:, :], scalar=core.gates[:, L:L + 1], in1=here,
                                                       op0=ALU.mult, op1=ALU.add).then_inc(sem("x_updated"), 1)

                for first in ["pc_ready"] + (["k_summed"] if L == 0 else []):
                    dve.sem_inc(sem(first), credit(first))
                step.engine = dve
                walk(step)

            @block.gpsimd
            def _(pool):
                def step(part, g, name, i, j):
                    m = round_of(name, g, j)
                    if name == "LNA":
                        pool.wait_ge(sem("moments_ready"), m + 1)
                        nc.gpsimd.tensor_tensor(rstd[:, :], mv[:, 1, :], core.half[:, 0:GB], ALU.pow).then_inc(sem("rstd_ready"), 1)
                    elif name == "R":
                        pool.wait_ge(sem("rden_ready"), nth(4, m, i))
                        scale = rden[:, i % 2, :].unsqueeze(2).to_broadcast([P, QH, P])
                        nc.gpsimd.tensor_tensor(probs[:, i % 2, :, :], probs[:, i % 2, :, :], scale, ALU.mult).then_inc(sem("probs_scaled"), 1)
                    elif name == "KN":
                        pool.wait_ge(sem("k_ss_ready"), m + 1)
                        nc.gpsimd.tensor_tensor(k_r[:, :], k_ss[:, :], core.half[:, :], ALU.pow).then_inc(sem("k_r_ready"), 1)
                        pool.wait_ge(sem("k_r_ready"), m + 1)
                    elif name == "KH":
                        pool.wait_ge(sem("k_copied"), nth(4, m, i))
                        keys = k_raw[:, i, :].rearrange("p (h d) -> p h d", d=P)
                        scale = k_r[:, i * QH:(i + 1) * QH].unsqueeze(2).to_broadcast([P, QH, P])
                        nc.gpsimd.tensor_tensor(keys, keys, scale, ALU.mult).then_inc(sem("kh_ready"), 1)
                    elif name == "SSQ":
                        pool.wait_ge(sem("ssq_copied"), m + 1)
                        nc.gpsimd.tensor_tensor(q_r[:, (j + 1) % 2, :], q_ss[:, :], core.half[:, :], ALU.pow).then_inc(sem("q_norm_ready"), 1)

                step.engine = pool
                walk(step)


def flamingo(nc, a, out):
    with ExitStack() as whole:
        core = Core(nc, whole)
        setup_stage(nc, core, a["x"], a["g_xattn"], a["g_ffn"])
        for layer in range(2):
            with ExitStack() as ctx:
                def pair(name, shape):
                    return [ctx.enter_context(nc.sbuf_tensor(f"{name}_{p}{layer}", shape, F32R)) for p in ("hi", "lo")]

                def sb(name, shape, dt=F32):
                    return ctx.enter_context(nc.sbuf_tensor(f"{name}{layer}", shape, dt))

                w = {"q": pair("wq", [P, KD, H * P]), "vo": pair("wvo", [P, H, D])}
                if layer == 0:
                    w["k"] = pair("wk", [P, H * P])
                    w["gain"] = sb("gain", [P, 1])
                    gain_stage(nc, core, w["gain"], a["L0_xattn_gq"], a["L0_xattn_gk"])
                else:
                    w["ctx_t"] = sb("ctx_t", [P, B * P])
                    w["bias"] = sb("bias", [P, B * P], F32R)
                    w["bias_row"] = sb("bias_row", [P, P], F32R)
                    w["mask_col"] = sb("mask_col", [P, B])
                prepare_attention(nc, core, layer, a[f"L{layer}_xattn_Wq"], a[f"L{layer}_xattn_Wk"], a[f"L{layer}_xattn_Wv"],
                                  a[f"L{layer}_xattn_Wo"], w, {"ctx": a["ctx_1024"], "mask": a["mask_BxS2_bf1"]})
                attention(nc, core, layer, w, a["ctx_1024"])
            feed_forward(nc, core, layer, a, out)
            if layer == 0:
                core.recycle_semaphores()


def gain_stage(nc, core, gain, gq, gk):
    with ExitStack() as ctx:
        raw = ctx.enter_context(nc.sbuf_tensor("gain_raw", [P, 2], F32))
        loaded = core.sem("gain_loaded")
        with nc.Block() as block:

            @block.sync
            def _(sp):
                sp.dma_start(raw[:, 0:1], gq.rearrange("(p a) -> p a", a=1)).then_inc(loaded, 16)
                sp.dma_start(raw[:, 1:2], gk.rearrange("(p a) -> p a", a=1)).then_inc(loaded, 16)

            @block.vector
            def _(dve):
                dve.wait_ge(loaded, 32)
                nc.vector.scalar_tensor_tensor(out=gain[:, :], in0=raw[:, 0:1], scalar=float(P) ** 0.5, in1=raw[:, 1:2],
                                               op0=ALU.mult, op1=ALU.mult)



def dequantise_stage(nc, core, packed, scales, targets):
    CH = 1024
    chunks = [(m, half) for m in range(3) for half in range(2)]
    with ExitStack() as ctx:
        def sb(name, shape, dt=F32):
            return ctx.enter_context(nc.sbuf_tensor(f"{name}_dq", shape, dt))

        def sem(name):
            return core.sem(f"{name}_dq")

        words = [sb(f"words{m}", [P, 2 * CH], I32) for m in range(3)]
        scale = [sb(f"scale{m}", [P, P]) for m in range(3)]
        mag, neg = sb("mag", [P, CH], I32), sb("neg", [P, CH], I32)
        acc, sign = sb("acc", [P, CH]), sb("sign", [P, CH])
        value = sb("value", [P, 2, 2 * CH])
        loaded = [sem(f"loaded{m}") for m in range(3)]
        step_done, ready, filled, hi_done, drained = (sem(n) for n in ("step_done", "ready", "filled", "hi_done", "drained"))
        units = [(c, u) for c in range(len(chunks)) for u in range(4)]
        with nc.Block() as block:

            def target(c, u, part):
                m, half = chunks[c]
                if m < 2:
                    cols = slice((half * 8 + 2 * u) * P, (half * 8 + 2 * u + 2) * P)
                    return targets[m][part][:, :, cols].rearrange("p k (t n) -> p t k n", n=P)
                return targets[2][part][:, 4 * u:4 * u + 4, half * P:(half + 1) * P]

            def view(n):
                c, u = units[n]
                b = core.bank[n % 8][:, :]
                return b.rearrange("p (t k n) -> p t k n", t=2, k=KD) if chunks[c][0] < 2 else b.rearrange("p (t n) -> p t n", n=P)

            @block.sync
            def _(sp):
                for m in range(3):
                    sp.dma_start(words[m][:, :], packed[m]).then_inc(loaded[m], 16)
                    sp.dma_start(scale[m][:, :], scales[m]).then_inc(loaded[m], 16)

            @block.gpsimd
            def _(pool):
                for c, (m, half) in enumerate(chunks):
                    pool.wait_ge(step_done, 10 * (c + 1))
                    v = value[:, c % 2, :].rearrange("p (b e) -> p b e", e=32)
                    sc = scale[m][:, half * 64:(half + 1) * 64].unsqueeze(2).to_broadcast([P, 64, 32])
                    nc.gpsimd.tensor_tensor(v, v, sc, ALU.mult).then_inc(ready, 1)

            @block.vector
            def _(dve):
                steps = [0]

                def chained(ins):
                    steps[0] += 1
                    ins.then_inc(step_done, 1)
                    dve.wait_ge(step_done, steps[0])

                def split(n):
                    c, u = units[n]
                    dve.wait_ge(hi_done, n + 1)
                    nc.vector.tensor_tensor(target(c, u, 1), view(n), f32(target(c, u, 0)), ALU.subtract).then_inc(drained, 1)

                for c, (m, half) in enumerate(chunks):
                    dve.wait_ge(loaded[m], 32)
                    if c >= 2:
                        dve.wait_ge(filled, 4 * (c - 1))
                    w = words[m][:, half * CH:(half + 1) * CH]
                    v = value[:, c % 2, :].rearrange("p (w n) -> p w n", n=2)
                    for nib in range(2):
                        nc.vector.tensor_scalar(neg[:, :], w, 4 * nib + 3, 1, ALU.logical_shift_right, ALU.bitwise_and)
                        chained(nc.vector.tensor_scalar(mag[:, :], w, 4 * nib, 7, ALU.logical_shift_right, ALU.bitwise_and))
                        nc.vector.tensor_scalar(sign[:, :], neg[:, :], -2.0, 1.0, ALU.mult, ALU.add)
                        chained(nc.vector.tensor_scalar(acc[:, :], mag[:, :], 0.5, 8.0, ALU.mult, ALU.add))
                        chained(nc.vector.scalar_tensor_tensor(out=acc[:, :], in0=mag[:, :], scalar=6.0, in1=acc[:, :], op0=ALU.add, op1=ALU.max))
                        chained(nc.vector.scalar_tensor_tensor(out=acc[:, :], in0=mag[:, :], scalar=2.0, in1=acc[:, :], op0=ALU.mult, op1=ALU.max))
                        chained(nc.vector.scalar_tensor_tensor(out=v[:, :, nib], in0=acc[:, :], scalar=-8.0, in1=sign[:, :], op0=ALU.add, op1=ALU.mult))
                    if c:
                        for n in range(4 * (c - 1), 4 * c):
                            split(n)
                for n in range(len(units) - 4, len(units)):
                    split(n)

            @block.tensor
            def _(pe):
                for n, (c, u) in enumerate(units):
                    pe.wait_ge(ready, c + 1)
                    if n >= 8:
                        pe.wait_ge(drained, n - 7)
                    for a in range(4):
                        t = 4 * u + a
                        last = nc.tensor.transpose(core.bank[n % 8][:, a * P:(a + 1) * P], value[:, c % 2, t * P:(t + 1) * P], core.ident[:, :])
                    last.then_inc(filled, 1)

            @block.scalar
            def _(act):
                for n, (c, u) in enumerate(units):
                    act.wait_ge(filled, n + 1)
                    nc.scalar.activation(target(c, u, 0), view(n), ACT.Copy).then_inc(hi_done, 1)


def split_stage(nc, core, a, w):
    NT = w["gate"][0].shape[2] // P
    with ExitStack() as ctx:
        def sb(name, shape, dt=F32):
            return ctx.enter_context(nc.sbuf_tensor(f"{name}_sp", shape, dt))

        def sem(name):
            return core.sem(f"{name}_sp")

        raw = [sb("gate_raw", [P, KD, NF1]), sb("up_raw", [P, KD, NF1])]
        d_raw = sb("down_raw", [P, NT, D])
        router = sb("router_raw", [P, D])
        owner_f = sb("owner_f", [P, NT * P])
        loaded, loaded_d, loaded_r = sem("loaded"), sem("loaded_d"), sem("loaded_r")
        zeroed, owned, hi_done, filled, router_zero = sem("zeroed"), sem("owned"), sem("hi_done"), sem("filled"), sem("router_zero")
        full, tail = divmod(I_SH, P)
        with nc.Block() as block:

            @block.sync
            def _(sp):
                for s in range(2):
                    sp.dma_start(raw[s][:, :, 0:I_SH], a["L1_ffn_Ws_gate_up"][:, s * I_SH:(s + 1) * I_SH].rearrange("(k c) n -> c k n", c=P)).then_inc(loaded, 16)
                    for k in range(KD):
                        sp.dma_start(raw[s][:, k, I_SH:NF1].rearrange("p (e n) -> p e n", e=E),
                                     a["L1_ffn_We_gate_up"][:, k * P:(k + 1) * P, s * I_MOE:(s + 1) * I_MOE].rearrange("e c n -> c e n")).then_inc(loaded, 16)
                experts = a["L1_ffn_We_down"].rearrange("e i d -> (e i) d")
                sp.wait_ge(zeroed, 1)
                sp.dma_start(d_raw[:, 0:full, :], a["L1_ffn_Ws_down"][0:full * P].rearrange("(t p) d -> p t d", p=P)).then_inc(loaded_d, 16)
                sp.dma_start(d_raw[0:tail, full, :], a["L1_ffn_Ws_down"][full * P:I_SH]).then_inc(loaded_d, 16)
                sp.dma_start(d_raw[tail:P, full, :], experts[0:P - tail]).then_inc(loaded_d, 16)
                rest = E * I_MOE - (P - tail)
                sp.dma_start(d_raw[:, full + 1:NT - 1, :], experts[P - tail:P - tail + rest // P * P].rearrange("(t p) d -> p t d", p=P)).then_inc(loaded_d, 16)
                sp.dma_start(d_raw[0:rest % P, NT - 1, :], experts[E * I_MOE - rest % P:E * I_MOE]).then_inc(loaded_d, 16)
                sp.wait_ge(router_zero, 1)
                sp.dma_start(router[0:1, :], a["L1_ffn_W_sgate"]).then_inc(loaded_r, 16)
                sp.dma_start(router[1:1 + E, :], a["L1_ffn_W_router"]).then_inc(loaded_r, 16)

            @block.gpsimd
            def _(pool):
                nc.gpsimd.memset(d_raw[:, NT - 1, :], 0.0).then_inc(zeroed, 1)
                nc.gpsimd.memset(router[:, :], 0.0).then_inc(router_zero, 1)
                nc.gpsimd.memset(owner_f[:, :], 0.0).then_inc(owned, 1)
                n = 1
                shared = owner_f[:, 0:I_SH]
                experts = owner_f[:, I_SH:NF1].rearrange("p (e n) -> p e n", e=E)
                for first in (0, E + 1):
                    for view, pattern, base in ((shared, [[0, I_SH]], -first), (experts, [[-1, E], [0, I_MOE]], -first - 1)):
                        pool.wait_ge(owned, n)
                        nc.gpsimd.affine_select(out=view, in_=view, compare_op=ALU.not_equal, fill=1.0, base=base,
                                                pattern=pattern, channel_multiplier=1).then_inc(owned, 1)
                        n += 1
                pool.wait_ge(owned, n)
                nc.gpsimd.memset(w["tri"][:, :, :], 1.0).then_inc(owned, 1)
                pool.wait_ge(owned, n + 1)
                nc.gpsimd.affine_select(out=w["tri"][:, :, :], in_=w["tri"][:, :, :], compare_op=ALU.is_gt, fill=0.0, base=0,
                                        pattern=[[1, E], [-1, E]], channel_multiplier=0)
                nc.gpsimd.memset(w["factors"][:, :, :], 0.0)

            @block.tensor
            def _(pe):
                pe.wait_ge(loaded_r, 32)
                for k in range(KD):
                    last = nc.tensor.transpose(core.bank[0][:, k * P:(k + 1) * P], router[:, k * P:(k + 1) * P], core.ident[:, :])
                last.then_inc(filled, 1)

            @block.scalar
            def _(act):
                act.wait_ge(loaded, 16 * 6)
                for k in range(KD):
                    for s, name in enumerate(("gate", "up")):
                        nc.scalar.activation(w[name][0][:, k, 0:NF1], raw[s][:, k, :], ACT.Copy).then_inc(hi_done, 1)
                act.wait_ge(loaded_d, 16 * 5)
                nc.scalar.activation(flat(w["down"][0][:, :, :]), flat(d_raw[:, :, :]), ACT.Copy).then_inc(hi_done, 1)
                act.wait_ge(filled, 1)
                nc.scalar.activation(flat(w["router"][0][:, :, :]), core.bank[0][:, 0:D], ACT.Copy).then_inc(hi_done, 1)
                act.wait_ge(owned, 5)
                nc.scalar.activation(w["owner"][:, :], owner_f[:, :], ACT.Copy)

            @block.vector
            def _(dve):
                for name in ("gate", "up"):
                    for part in range(2):
                        nc.vector.memset(f32(w[name][part][:, :, NF1:NT * P]), 0.0)
                n = 0
                for k in range(KD):
                    for s, name in enumerate(("gate", "up")):
                        n += 1
                        dve.wait_ge(hi_done, n)
                        nc.vector.tensor_tensor(w[name][1][:, k, 0:NF1], raw[s][:, k, :], f32(w[name][0][:, k, 0:NF1]), ALU.subtract)
                dve.wait_ge(hi_done, n + 1)
                nc.vector.tensor_tensor(flat(w["down"][1][:, :, :]), flat(d_raw[:, :, :]), f32(flat(w["down"][0][:, :, :])), ALU.subtract)
                dve.wait_ge(hi_done, n + 2)
                nc.vector.tensor_tensor(flat(w["router"][1][:, :, :]), core.bank[0][:, 0:D], f32(flat(w["router"][0][:, :, :])), ALU.subtract)


def feed_forward(nc, core, layer, a, out_dram):
    L = layer
    NT = (NF0 if L == 0 else NF1 + P - 1) // P
    LAG = 2
    with ExitStack() as ctx:
        def sb(name, shape, dt=F32):
            return ctx.enter_context(nc.sbuf_tensor(f"{name}_f{L}", shape, dt))

        def pair(name, shape):
            return [sb(f"{name}_{p}", shape, F32R) for p in ("hi", "lo")]

        sems = {}

        def sem(name):
            if name not in sems:
                sems[name] = core.sem(f"{name}_f{L}")
            return sems[name]

        bn, mv = sb("bn", [P, GB, 6]), sb("mv", [P, 7, GB])
        rstd = sb("rstd", [P, GB])
        w = {"gate": pair("w_gate", [P, KD, NT * P]), "up": pair("w_up", [P, KD, NT * P]), "down": pair("w_down", [P, NT, D])}
        if L == 0:
            def rows(v):
                return v.rearrange("(t p) c -> p t c", p=P)

            def tiled(v):
                return v.rearrange("(e p) c -> p e c", p=P)

            names = ("gate", "up", "down")
            packed = [rows(a["L0_ffn_gate_W_packed"]), rows(a["L0_ffn_up_W_packed"]), tiled(a["L0_ffn_down_W_packed"])]
            scales = [rows(a["L0_ffn_gate_scales"]), rows(a["L0_ffn_up_scales"]), tiled(a["L0_ffn_down_scales"])]
            dequantise_stage(nc, core, packed, scales, [w[n] for n in names])
        else:
            w["router"] = pair("w_router", [P, KD, P])
            w["owner"] = sb("owner", [P, NT * P], F32R)
            w["tri"] = sb("tri", [P, E, E])
            w["factors"] = sb("factors", [P, GB, P])
            split_stage(nc, core, a, w)

        xt = pair("xt", [P, KD, B * P])
        xn = sb("xn", [P, GB, D])
        act_g = sb("act_g", [P, 2, N])
        hid = sb("hid", [P, 2, N])
        hs = pair("hs", [P, LAG + 1, N])
        out_sb = sb("out_sb", [P, KD, N])
        if L == 1:
            ft = sb("ft", [P, B * P], F32R)
            logit_t = sb("logit_t", [P, N])
            NF = E + 1
            logit = sb("logit", [P, GB, NF])
            lmax = sb("lmax", [P, GB])
            shifted, expd = sb("shifted", [P, GB, NF]), sb("expd", [P, GB, NF])
            sums, rsums = sb("sums", [P, GB, 2]), sb("rsums", [P, GB, 2])
            prob, factor = sb("prob", [P, GB, E]), sb("factor", [P, GB, NF])
            above, ties = sb("above", [P, GB, E, E]), sb("ties", [P, GB, E, E])
            rank = sb("rank", [P, GB, E])
        out_t, misc, g_bank, u_bank = core.bank[0:2], core.bank[2:4], core.bank[4:6], core.bank[6:8]

        nxt = [("LNA", 0), ("LNB", 0), ("X", 0), ("X", 1)]
        if L == 1:
            nxt += [("RT", 0), ("RTT", 0), ("FT", 0)]
        at = {3: nxt[:1], 5: nxt[1:2], 6: nxt[2:4], 8: nxt[4:5], 9: nxt[5:6], 12: nxt[6:7]}

        def group_order(last):
            order = []
            for i in range(NT):
                order += [("GU", i)] + ([("F", i)] if L == 1 else []) + [("A", i)] + ([("D", i - LAG)] if i >= LAG else [])
                if not last:
                    order += at.get(i, [])
            return order + [("FLUSH", 0)] + [("D", i) for i in range(NT - LAG, NT)] + [("OUT", 0), ("E", 0), ("E", 1)]

        orders = {"start": nxt, "body": group_order(False), "last": group_order(True)}
        per = {"X": 2, "RT": 1, "RTT": 1, "FT": 1, "F": NT, "E": 2}
        NEXT_STEPS = ("LNA", "LNB", "X", "RT", "RTT", "FT")
        filled = {n: sem(f"{n.lower()}_filled") for n in per if L == 1 or n in ("X", "E")}
        released = {n: sem(f"{n.lower()}_released") for n in filled}
        rings = {}
        for part, order in orders.items():
            ring = [s for s in order if s[0] in per]
            shift = len(ring) % 2 if part == "start" else 0
            rings[part] = ring, {s: (n + shift) % 2 for n, s in enumerate(ring)}
        assert len(rings["body"][0]) % 2 == 0

        def nth(n, m, i):
            return m * n + (i + 1)

        def round_of(name, g):
            return g + 1 if name in NEXT_STEPS else g

        def walk(emit):
            for s in orders["start"]:
                emit("start", -1, *s)
            with emit.engine.Fori(0, G - 1) as g:
                for s in orders["body"]:
                    emit("body", g, *s)
            for s in orders["last"]:
                emit("last", G - 1, *s)

        with nc.Block() as block:

            if L == 1:
                @block.sync
                def _(sp):
                    with sp.Fori(0, G) as g:
                        sp.wait_ge(released["E"], g * 2 + 2 + credit("E"))
                        sp.dma_start(out_dram[bass.ds(g * GB, GB)].rearrange("b s d -> s b d"),
                                     core.x[:, bass.ds(g * GB, GB), :]).then_inc(sem("stored"), 16)
                    sp.wait_ge(sem("stored"), 16 * G)

            @block.tensor
            def _(pe):
                def bank_free(part, g, step):
                    ring, slots = rings[part]
                    k = ring.index(step)
                    if k >= 2:
                        n, i = ring[k - 2]
                        pe.wait_ge(released[n], nth(per[n], round_of(n, g), i) + credit(n))
                    elif part != "start":
                        pe.wait_ge(released["E"], g * 2 + credit("E"))
                        if L == 1:
                            pe.wait_ge(released["FT"], g + 1)
                        else:
                            pe.wait_ge(released["X"], 2 * g + 2)
                    return misc[slots[step]]

                def step(part, g, name, i):
                    m = round_of(name, g)
                    if name in per:
                        bank = bank_free(part, g, (name, i))
                    if name == "X":
                        if i == 0:
                            pe.wait_ge(sem("xn_ready"), m + 1)
                        for b in range(GB):
                            last = nc.tensor.transpose(bank[:, b * P:(b + 1) * P], xn[:, b, i * P:(i + 1) * P], core.ident[:, :])
                    elif name == "GU":
                        if i == 0:
                            pe.wait_ge(released["X"], 2 * g + 2)
                        for key, banks, read in (("gate", g_bank, "gate_read"), ("up", u_bank, "up_read")):
                            if i >= 2:
                                pe.wait_ge(sem(read), g * NT + (i - 1))
                            for k in range(KD):
                                last = three_pass(nc, banks[i % 2][:, :], [v[:, k, i * P:(i + 1) * P] for v in w[key]],
                                                  [v[:, k, bass.ds(g * N, N)] for v in xt], k == 0, k == KD - 1)
                        last.then_inc(sem("up_filled"), 1)
                        return
                    elif name == "F":
                        if i == 0:
                            pe.wait_ge(released["FT"], g + 1)
                        last = nc.tensor.matmul(bank[:, :], w["owner"][:, i * P:(i + 1) * P], ft[:, bass.ds(g * N, N)], start=True, stop=True)
                    elif name == "D":
                        pe.wait_ge(sem("h_ready"), g * NT + i + 1 + credit("h_ready"))
                        if i == 0:
                            pe.wait_ge(sem("out_read"), 2 * g + credit("out_read"))
                        for e in range(KD):
                            last = three_pass(nc, out_t[e][:, :], [v[:, i, e * P:(e + 1) * P] for v in w["down"]],
                                              [v[:, i % (LAG + 1), :] for v in hs], i == 0, i == NT - 1)
                        last.then_inc(sem("down_done"), 1)
                        return
                    elif name == "E":
                        if i == 0:
                            pe.wait_ge(sem("out_read"), 2 * g + 2 + credit("out_read"))
                        for t in range(2):
                            for e in range(KD):
                                last = nc.tensor.transpose(bank[:, (t * KD + e) * P:(t * KD + e + 1) * P],
                                                           out_sb[:, e, (2 * i + t) * P:(2 * i + t + 1) * P], core.ident[:, :])
                    elif name == "RT":
                        pe.wait_ge(released["X"], 2 * m + 2)
                        for k in range(KD):
                            last = three_pass(nc, bank[:, :], [v[:, k, :] for v in w["router"]], [v[:, k, bass.ds(m * N, N)] for v in xt],
                                              k == 0, k == KD - 1)
                    elif name == "RTT":
                        pe.wait_ge(released["RT"], m + 1)
                        for b in range(GB):
                            last = nc.tensor.transpose(bank[:, b * P:(b + 1) * P], logit_t[:, b * P:(b + 1) * P], core.ident[:, :])
                    elif name == "FT":
                        pe.wait_ge(sem("factors_ready"), m + 1)
                        for b in range(GB):
                            last = nc.tensor.transpose(bank[:, b * P:(b + 1) * P], w["factors"][:, b, :], core.ident[:, :])
                    else:
                        return
                    last.then_inc(filled[name], 1)

                step.engine = pe
                walk(step)

            @block.scalar
            def _(act):
                def split_hi(g, i):
                    act.wait_ge(released["F"] if L == 1 else sem("up_read"), g * NT + i + 1)
                    nc.scalar.activation(hs[0][:, i % (LAG + 1), :], hid[:, i % 2, :], ACT.Copy).then_inc(sem("h_hi_ready"), 1)

                def step(part, g, name, i):
                    m = round_of(name, g)
                    bank = misc[rings[part][1][(name, i)]] if name in per else None
                    if name == "X":
                        act.wait_ge(filled[name], nth(2, m, i))
                        nc.scalar.activation(xt[0][:, i, bass.ds(m * N, N)], bank[:, :], ACT.Copy).then_inc(sem("x_hi_ready"), 1)
                    elif name == "A":
                        act.wait_ge(sem("up_filled"), g * NT + i + 1)
                        nc.scalar.activation(act_g[:, i % 2, :], g_bank[i % 2][:, :], ACT.Gelu_apprx_tanh if L == 0 else ACT.Silu).then_inc(sem("gate_read"), 1)
                        if i:
                            split_hi(g, i - 1)
                    elif name == "FLUSH":
                        split_hi(g, NT - 1)
                    elif name == "OUT":
                        act.wait_ge(sem("down_done"), g * NT + NT)
                        for e in range(KD):
                            nc.scalar.activation(out_sb[:, e, :], out_t[e][:, :], ACT.Copy).then_inc(sem("out_read"), 1)
                    elif name == "RT":
                        act.wait_ge(filled["RT"], m + 1)
                        nc.scalar.activation(logit_t[:, :], bank[:, :], ACT.Copy).then_inc(released["RT"], 1)
                    elif name == "RTT":
                        act.wait_ge(sem("shifted_ready"), m + 1)
                        nc.scalar.activation(flat(expd[:, :, :]), flat(shifted[:, :, :]), ACT.Exp).then_inc(sem("exp_ready"), 1)
                        act.wait_ge(sem("factor_ready"), m + 1)
                        nc.scalar.activation(w["factors"][:, :, 0:NF].bitcast(F32R), factor[:, :, :], ACT.Copy).then_inc(sem("factor_hi_ready"), 1)
                    elif name == "FT":
                        act.wait_ge(filled["FT"], m + 1)
                        nc.scalar.activation(ft[:, bass.ds(m * N, N)], bank[:, :], ACT.Copy).then_inc(released["FT"], 1)

                act.sem_inc(sem("out_read"), 1)
                step.engine = act
                walk(step)

            @block.vector
            def _(dve):
                CHAIN = 11

                def router_factors(m, bank):
                    steps = [0]

                    def chained(ins):
                        steps[0] += 1
                        ins.then_inc(sem("router_step"), 1)
                        dve.wait_ge(sem("router_step"), m * CHAIN + steps[0])

                    nc.vector.tensor_copy(logit[:, :, :], bank[:, :].rearrange("p (b r) -> p b r", r=P)[:, :, 0:NF]).then_inc(released["RTT"], 1)
                    dve.wait_ge(released["RTT"], m + 1)
                    chained(nc.vector.tensor_reduce(lmax[:, :], logit[:, :, 1:NF], AX.X, ALU.max))
                    nc.vector.tensor_scalar(shifted[:, :, 0:1], logit[:, :, 0:1], -1.0, None, ALU.mult)
                    nc.vector.tensor_tensor(shifted[:, :, 1:NF], logit[:, :, 1:NF], lmax[:, :].unsqueeze(2).to_broadcast([P, GB, E]),
                                            ALU.subtract).then_inc(sem("shifted_ready"), 1)
                    dve.wait_ge(sem("exp_ready"), m + 1)
                    chained(nc.vector.tensor_reduce(sums[:, :, 0:1], expd[:, :, 1:NF], AX.X, ALU.add))
                    chained(nc.vector.tensor_scalar(sums[:, :, 1:2], expd[:, :, 0:1], 1.0, None, ALU.add))
                    chained(nc.vector.reciprocal(rsums[:, :, :], sums[:, :, :]))
                    chained(nc.vector.tensor_copy(factor[:, :, 0:1], rsums[:, :, 1:2]))
                    chained(nc.vector.tensor_tensor(prob[:, :, :], expd[:, :, 1:NF], rsums[:, :, 0:1].to_broadcast([P, GB, E]), ALU.mult))
                    pj = prob[:, :, :].unsqueeze(2).to_broadcast([P, GB, E, E])
                    pe_ = prob[:, :, :].unsqueeze(3).to_broadcast([P, GB, E, E])
                    chained(nc.vector.tensor_tensor(ties[:, :, :, :], pj, pe_, ALU.is_equal))
                    nc.vector.tensor_tensor(above[:, :, :, :], pj, pe_, ALU.is_gt)
                    chained(nc.vector.tensor_tensor(ties[:, :, :, :], ties[:, :, :, :], w["tri"][:, :, :].unsqueeze(1).to_broadcast([P, GB, E, E]), ALU.mult))
                    chained(nc.vector.tensor_tensor(above[:, :, :, :], above[:, :, :, :], ties[:, :, :, :], ALU.add))
                    chained(nc.vector.tensor_reduce(rank[:, :, :], above[:, :, :, :], AX.X, ALU.add))
                    chained(nc.vector.scalar_tensor_tensor(out=factor[:, :, 1:NF], in0=rank[:, :, :], scalar=2.0, in1=prob[:, :, :],
                                                           op0=ALU.is_lt, op1=ALU.mult))
                    assert steps[0] == CHAIN
                    nc.vector.tensor_copy(logit[:, :, :], factor[:, :, :]).then_inc(sem("factor_ready"), 1)
                    dve.wait_ge(sem("factor_hi_ready"), m + 1)
                    nc.vector.tensor_tensor(w["factors"][:, :, NF:2 * NF], factor[:, :, :], w["factors"][:, :, 0:NF],
                                            ALU.subtract).then_inc(sem("factors_ready"), 1)

                def split_lo(g, i):
                    dve.wait_ge(sem("h_hi_ready"), g * NT + i + 1)
                    s = i % (LAG + 1)
                    nc.vector.tensor_tensor(hs[1][:, s, :], hid[:, i % 2, :], f32(hs[0][:, s, :]), ALU.subtract).then_inc(sem("h_ready"), 1)

                def step(part, g, name, i):
                    m = round_of(name, g)
                    bank = misc[rings[part][1][(name, i)]] if name in per else None
                    if name == "LNA":
                        for b in range(GB):
                            nc.vector.bn_stats(bn[:, b, :], flat(core.x[:, bass.ds(m * GB + b, 1), :])).then_inc(sem("stats_ready"), 1)
                        moments(nc, dve, m, bn, mv, sem)
                    elif name == "LNB":
                        dve.wait_ge(sem("rstd_ready"), m + 1)
                        for b in range(GB):
                            last = nc.vector.tensor_scalar(xn[:, b, :], flat(core.x[:, bass.ds(m * GB + b, 1), :]), mv[:, 0, b:b + 1],
                                                           rstd[:, b:b + 1], ALU.subtract, ALU.mult)
                        last.then_inc(sem("xn_ready"), 1)
                    elif name == "X":
                        dve.wait_ge(sem("x_hi_ready"), nth(2, m, i))
                        nc.vector.tensor_tensor(xt[1][:, i, bass.ds(m * N, N)], bank[:, :], f32(xt[0][:, i, bass.ds(m * N, N)]),
                                                ALU.subtract).then_inc(released["X"], 1)
                    elif name == "A":
                        dve.wait_ge(sem("h_ready"), g * NT + max(i - 1, 0) + credit("h_ready"))
                        dve.wait_ge(sem("gate_read"), g * NT + i + 1)
                        nc.vector.tensor_tensor(hid[:, i % 2, :], act_g[:, i % 2, :], u_bank[i % 2][:, :], ALU.mult).then_inc(sem("up_read"), 1)
                        if i:
                            split_lo(g, i - 1)
                        if L == 1:
                            dve.wait_ge(filled["F"], g * NT + i + 1)
                            dve.wait_ge(sem("up_read"), g * NT + i + 1)
                            nc.vector.tensor_tensor(hid[:, i % 2, :], hid[:, i % 2, :], misc[rings[part][1][("F", i)]][:, :],
                                                    ALU.mult).then_inc(released["F"], 1)
                    elif name == "FLUSH":
                        split_lo(g, NT - 1)
                    elif name == "RTT":
                        dve.wait_ge(filled["RTT"], m + 1)
                        router_factors(m, bank)
                    elif name == "E":
                        dve.wait_ge(filled[name], nth(2, g, i))
                        here = flat(core.x[:, bass.ds(g * GB + 2 * i, 2), :])
                        nc.vector.scalar_tensor_tensor(out=here, in0=bank[:, :], scalar=core.gates[:, 2 + L:3 + L], in1=here,
                                                       op0=ALU.mult, op1=ALU.add).then_inc(released[name], 1)

                dve.sem_inc(released["E"], 1)
                dve.sem_inc(sem("h_ready"), 1)
                step.engine = dve
                walk(step)

            @block.gpsimd
            def _(pool):
                def step(part, g, name, i):
                    m = round_of(name, g)
                    if name == "LNA":
                        pool.wait_ge(sem("moments_ready"), m + 1)
                        nc.gpsimd.tensor_tensor(rstd[:, :], mv[:, 1, :], core.half[:, 0:GB], ALU.pow).then_inc(sem("rstd_ready"), 1)

                step.engine = pool
                walk(step)


_INS = ["x", "ctx_1024", "mask_BxS2_bf1", "g_xattn", "g_ffn",
        "L0_xattn_Wq", "L0_xattn_Wk", "L0_xattn_Wv", "L0_xattn_Wo", "L0_xattn_gq", "L0_xattn_gk",
        "L0_ffn_gate_W_packed", "L0_ffn_gate_scales", "L0_ffn_up_W_packed", "L0_ffn_up_scales",
        "L0_ffn_down_W_packed", "L0_ffn_down_scales", "L1_xattn_Wq", "L1_xattn_Wk", "L1_xattn_Wv", "L1_xattn_Wo",
        "L1_ffn_W_router", "L1_ffn_W_sgate", "L1_ffn_Ws_gate_up", "L1_ffn_Ws_down", "L1_ffn_We_gate_up", "L1_ffn_We_down"]


def kernel(**inputs):
    import numpy as np
    import concourse.bacc as bacc
    from concourse.bass_utils import run_bass_kernel_spmd

    nc = bacc.Bacc("TRN2", target_bir_lowering=False, num_devices=1)
    arrays, aps = {}, {}
    for name in _INS:
        v = np.ascontiguousarray(inputs[name])
        if v.dtype == np.bool_:
            v = v.view(np.uint8)
        arrays[f"in_{name}"] = v
        aps[name] = nc.dram_tensor(f"in_{name}", v.shape, mybir.dt.from_np(v.dtype), kind="ExternalInput").ap()
    out = nc.dram_tensor("out", (B, P, D), F32, kind="ExternalOutput").ap()
    flamingo(nc, aps, out)
    r = run_bass_kernel_spmd(nc, [arrays], core_ids=[0])
    return r.results[0]["out"]
```

```python
from contextlib import ExitStack

import concourse.bass as bass
from concourse import mybir

F32 = mybir.dt.float32
F32R = mybir.dt.float32r
I32 = mybir.dt.int32
U8 = mybir.dt.uint8
F8 = mybir.dt.float8e3
ALU = mybir.AluOpType
ACT = mybir.ActivationFunctionType
AX = mybir.AxisListType

P = 128
B = 16
D = 256
KD = D // P
H = 16
GB = 4
G = B // GB
N = GB * P
QH = 4
NQ = H // QH
EPS = 1e-5
MASKED = -float(2 ** 100)
SKV = 8
I_SH, I_MOE, E = 704, 176, 8
NF0 = 2048
NF1 = I_SH + E * I_MOE


def f32(ap):
    return ap.bitcast(F32)


class Core:

    def __init__(self, nc, ctx):
        self.nc, self.ctx = nc, ctx
        self.x = self.sb("x_sb", [P, B, D])
        self.ident = self.sb("ident", [P, P])
        self.gates = self.sb("gates", [P, 4])
        self.half = self.sb("half", [P, 16])
        self.ones = self.sb("ones", [P, 1])
        self.bank = [ctx.enter_context(nc.psum_tensor(f"bank{i}", [P, N], F32)) for i in range(8)]

        self.sems = []

    def sem(self, name):
        self.sems.append(self.nc.alloc_semaphore(name))
        return self.sems[-1]

    def recycle_semaphores(self):
        self.nc.clear_and_free_semaphores(self.sems)
        self.sems = []
        self.nc.all_engine_barrier()

    def sb(self, name, shape, dt=F32):
        return self.ctx.enter_context(self.nc.sbuf_tensor(name, shape, dt))


def three_pass(nc, out, w, x, start, stop):
    nc.tensor.matmul(out, w[0], x[0], start=start, stop=False)
    nc.tensor.matmul(out, w[0], x[1], start=False, stop=False)
    return nc.tensor.matmul(out, w[1], x[0], start=False, stop=stop)


def moments(nc, dve, m, bn, mv, sem):
    mean_e, dev_e, mean_o, dev_o = (bn[:, :, k] for k in (1, 2, 4, 5))
    dve.wait_ge(sem("stats_ready"), m * GB + GB)
    nc.vector.tensor_tensor(mv[:, 2, :], mean_e, mean_o, ALU.add)
    nc.vector.tensor_tensor(mv[:, 3, :], mean_e, mean_o, ALU.subtract)
    nc.vector.tensor_tensor(mv[:, 4, :], dev_e, dev_o, ALU.add).then_inc(sem("halves_ready"), 1)
    dve.wait_ge(sem("halves_ready"), m * 2 + 1)
    nc.vector.tensor_scalar(mv[:, 0, :], mv[:, 2, :], 0.5, None, ALU.mult)
    nc.vector.scalar_tensor_tensor(out=mv[:, 5, :], in0=mv[:, 3, :], scalar=0.25, in1=mv[:, 3, :], op0=ALU.mult, op1=ALU.mult)
    nc.vector.tensor_scalar(mv[:, 6, :], mv[:, 4, :], 1.0 / D, EPS, ALU.mult, ALU.add).then_inc(sem("halves_ready"), 1)
    dve.wait_ge(sem("halves_ready"), m * 2 + 2)
    nc.vector.tensor_tensor(mv[:, 1, :], mv[:, 6, :], mv[:, 5, :], ALU.add).then_inc(sem("moments_ready"), 1)


def credit(name):
    return {"k_summed": 2, "E": 1, "pc_ready": 1, "out_read": 1, "h_ready": 1}.get(name, 0)


def flat(ap):
    return ap.rearrange("p a b -> p (a b)")



def prepare_attention(nc, core, layer, Wq, Wk, Wv, Wo, w, a):
    kv = H if layer == 0 else SKV
    rep = H // kv
    nq_t = 0 if layer == 0 else KD * H // 4
    nk_t = 0 if layer == 0 else kv // 4
    nv_t = kv // 4
    with ExitStack() as ctx:
        def sb(name, shape, dt=F32):
            return ctx.enter_context(nc.sbuf_tensor(f"{name}_p{layer}", shape, dt))

        def sem(name):
            return core.sem(f"{name}_p{layer}")

        q_raw = sb("q_raw", [P, KD, H * P])
        k_raw = sb("k_raw", [P, kv * P])
        v_raw = sb("v_raw", [P, kv * P])
        o_raw = sb("o_raw", [P, H, D])
        v_t = sb("v_t", [P, kv, P])
        loaded_q, loaded_k, loaded_v, loaded_o = (sem(f"loaded_{n}") for n in "qkvo")
        filled, hi_done, raw_hi, drained = sem("bank_filled"), sem("hi_done"), sem("raw_hi_done"), sem("bank_drained")
        if layer == 1:
            q_t = sb("q_t", [P, H, KD, P])
            k_t = sb("k_t", [P, kv, P])
            ctx_raw, maskrow, maskcol8 = sb("ctx_raw", [P, B, P]), sb("maskrow", [1, B * P], U8), sb("maskcol8", [P, B], U8)
            loaded_c, loaded_m, zeroed = sem("loaded_c"), sem("loaded_m"), sem("zeroed")
        else:
            small = sb("small", [P, 6])
            loaded_s, loaded_x, zeroed, ident_made, made = (sem(n) for n in ("loaded_s", "loaded_x", "zeroed", "ident_made", "made"))

        units = [("v_t", i) for i in range(nv_t)] + [("q_t", i) for i in range(nq_t)] + [("k_t", i) for i in range(nk_t)]
        if layer == 1:
            units += [("ctx", i) for i in range(G)]
        n_t = len(units)
        units += [("vo", i) for i in range(H // 2)] + ([("m", i) for i in range(KD * H // 4)] if layer else [])
        with nc.Block() as block:

            @block.sync
            def _(sp):
                if layer == 0:
                    sp.dma_start(small[:, 0:2], a["g_xattn"].partition_broadcast(P)).then_inc(loaded_s, 16)
                    sp.dma_start(small[:, 2:4], a["g_ffn"].partition_broadcast(P)).then_inc(loaded_s, 16)
                    sp.dma_start(small[:, 4:5], a["L0_xattn_gq"].rearrange("(p a) -> p a", a=1)).then_inc(loaded_s, 16)
                    sp.dma_start(small[:, 5:6], a["L0_xattn_gk"].rearrange("(p a) -> p a", a=1)).then_inc(loaded_s, 16)
                sp.dma_start(v_raw[:, :], Wv).then_inc(loaded_v, 16)
                sp.dma_start(o_raw[:, :, :], Wo.rearrange("(h d) e -> d h e", d=P)).then_inc(loaded_o, 16)
                sp.dma_start(q_raw[:, :, :], Wq.rearrange("(k c) n -> c k n", c=P)).then_inc(loaded_q, 16)
                sp.dma_start(k_raw[:, :], Wk).then_inc(loaded_k, 16)
                if layer == 0:
                    for g in range(G):
                        tokens = slice(g * GB, (g + 1) * GB)
                        sp.dma_start(core.x[:, tokens, :], a["x"][tokens].rearrange("b s d -> s b d")).then_inc(loaded_x, 16)
                    sp.wait_ge(loaded_x, 16 * G)
                else:
                    sp.dma_start(ctx_raw[:, :, :], a["ctx_1024"].rearrange("b s c -> s b c")).then_inc(loaded_c, 16)
                    sp.dma_start(maskrow[:, :], a["mask_BxS2_bf1"].rearrange("(a b) s -> a (b s)", a=1)).then_inc(loaded_m, 16)
                    with nc.allow_non_contiguous_dma("2 KB of mask, transposed"):
                        sp.dma_start(maskcol8[:, :], a["mask_BxS2_bf1"].rearrange("b s -> s b")).then_inc(loaded_m, 16)

            if layer == 0:
                @block.gpsimd
                def _(pool):
                    nc.gpsimd.memset(core.ident[:, :], 0.0).then_inc(zeroed, 1)
                    nc.gpsimd.memset(core.half[:, :], -0.5).then_inc(made, 1)
                    nc.gpsimd.memset(core.ones[:, :], 1.0).then_inc(made, 1)
                    pool.wait_ge(zeroed, 1)
                    nc.gpsimd.affine_select(out=core.ident[:, :], in_=core.ident[:, :], compare_op=ALU.not_equal,
                                            fill=1.0, base=0, pattern=[[-1, P]], channel_multiplier=1).then_inc(ident_made, 1)
                    pool.wait_ge(made, 2)

            @block.tensor
            def _(pe):
                if layer == 0:
                    pe.wait_ge(ident_made, 1)
                for n, (kind, i) in enumerate(units):
                    out = core.bank[n % 8]
                    if n >= 8:
                        pe.wait_ge(drained, n - 7)
                    if kind == "v_t":
                        pe.wait_ge(loaded_v, 16)
                        for a in range(4):
                            last = nc.tensor.transpose(out[:, a * P:(a + 1) * P], v_raw[:, (4 * i + a) * P:(4 * i + a + 1) * P], core.ident[:, :])
                    elif kind == "q_t":
                        pe.wait_ge(loaded_q, 16)
                        for a in range(4):
                            h, k = divmod(4 * i + a, KD)
                            last = nc.tensor.transpose(out[:, a * P:(a + 1) * P], q_raw[:, k, h * P:(h + 1) * P], core.ident[:, :])
                    elif kind == "k_t":
                        pe.wait_ge(loaded_k, 16)
                        for a in range(4):
                            last = nc.tensor.transpose(out[:, a * P:(a + 1) * P], k_raw[:, (4 * i + a) * P:(4 * i + a + 1) * P], core.ident[:, :])
                    elif kind == "ctx":
                        pe.wait_ge(loaded_c, 16)
                        for a in range(4):
                            last = nc.tensor.transpose(out[:, a * P:(a + 1) * P], ctx_raw[:, 4 * i + a, :], core.ident[:, :])
                    elif kind == "vo":
                        if i == 0:
                            pe.wait_ge(loaded_o, 16)
                            pe.wait_ge(drained, n_t)
                        for a in range(2):
                            h = 2 * i + a
                            last = nc.tensor.matmul(out[:, a * D:(a + 1) * D], v_t[:, h // rep, :], o_raw[:, h, :], start=True, stop=True)
                    else:
                        for a in range(4):
                            h, k = divmod(4 * i + a, KD)
                            last = nc.tensor.matmul(out[:, a * P:(a + 1) * P], q_t[:, h, k, :], k_t[:, h // rep, :], start=True, stop=True)
                    last.then_inc(filled, 1)

            def target(kind, i, part):
                if kind == "vo":
                    return flat(w["vo"][part][:, 2 * i:2 * i + 2, :])
                return w["q"][part].rearrange("p k (h c) -> p h k c", c=P)[:, 2 * i:2 * i + 2, :, :]

            def bank_view(n, kind):
                return core.bank[n % 8][:, :].rearrange("p (h k c) -> p h k c", h=2, k=KD) if kind == "m" else core.bank[n % 8][:, :]

            @block.scalar
            def _(act):
                if layer == 0:
                    act.wait_ge(loaded_s, 64)
                    nc.scalar.activation(core.gates[:, :], small[:, 0:4], ACT.Tanh)
                for n, (kind, i) in enumerate(units):
                    if layer == 0 and n == n_t + 2:
                        act.wait_ge(loaded_q, 16)
                        for k in range(KD):
                            nc.scalar.activation(w["q"][0][:, k, :], q_raw[:, k, :], ACT.Copy).then_inc(raw_hi, 1)
                        act.wait_ge(loaded_k, 16)
                        nc.scalar.activation(w["k"][0][:, :], k_raw[:, :], ACT.Copy).then_inc(raw_hi, 1)
                    act.wait_ge(filled, n + 1)
                    if kind == "v_t":
                        nc.scalar.activation(flat(v_t[:, 4 * i:4 * i + 4, :]), core.bank[n % 8][:, :], ACT.Copy).then_inc(drained, 1)
                    elif kind == "q_t":
                        nc.scalar.activation(q_t[:, 2 * i:2 * i + 2, :, :].rearrange("p h k c -> p (h k c)"), core.bank[n % 8][:, :], ACT.Copy).then_inc(drained, 1)
                    elif kind == "ctx":
                        nc.scalar.activation(w["ctx_t"][:, i * N:(i + 1) * N], core.bank[n % 8][:, :], ACT.Copy).then_inc(drained, 1)
                    elif kind == "k_t":
                        nc.scalar.activation(flat(k_t[:, 4 * i:4 * i + 4, :]), core.bank[n % 8][:, :], ACT.Copy).then_inc(drained, 1)
                    else:
                        nc.scalar.activation(target(kind, i, 0), bank_view(n, kind), ACT.Copy).then_inc(hi_done, 1)

            @block.vector
            def _(dve):
                if layer == 0:
                    dve.wait_ge(loaded_s, 64)
                    nc.vector.scalar_tensor_tensor(out=w["gain"][:, :], in0=small[:, 4:5], scalar=float(P) ** 0.5, in1=small[:, 5:6],
                                                   op0=ALU.mult, op1=ALU.mult)
                else:
                    nc.vector.memset(f32(w["bias"][:, :]), 0.0).then_inc(zeroed, 1)
                    dve.wait_ge(loaded_m, 32)
                    dve.wait_ge(zeroed, 1)
                    nc.vector.tensor_scalar(w["bias"][0:1, :], maskrow[:, :], 1.0, -MASKED, ALU.subtract, ALU.mult)
                    nc.vector.tensor_copy(w["mask_col"][:, :], maskcol8[:, :])
                    nc.vector.memset(f32(w["bias_row"][:, :]), 0.0).then_inc(zeroed, 1)
                    dve.wait_ge(zeroed, 2)
                    nc.vector.memset(f32(w["bias_row"][0:1, :]), 1.0)
                for n, (kind, i) in enumerate(units):
                    if n < n_t:
                        continue
                    if layer == 0 and n == n_t + 2:
                        for k in range(KD):
                            dve.wait_ge(raw_hi, k + 1)
                            nc.vector.tensor_tensor(w["q"][1][:, k, :], q_raw[:, k, :], f32(w["q"][0][:, k, :]), ALU.subtract)
                        dve.wait_ge(raw_hi, KD + 1)
                        nc.vector.tensor_tensor(w["k"][1][:, :], k_raw[:, :], f32(w["k"][0][:, :]), ALU.subtract)
                    dve.wait_ge(hi_done, n - n_t + 1)
                    nc.vector.tensor_tensor(target(kind, i, 1), bank_view(n, kind), f32(target(kind, i, 0)),
                                            ALU.subtract).then_inc(drained, 1)



def quad_order(layer, j):
    text = """
        S1 Sm1 X0 EX0 K0 W0 Kc0 X1 R0 K1 W1 K2 EX1 Kc1 Kc2 W2 T0 S2 R1 Ts0 K3 Q0 C0 T1 Kc3 KN0 Sm2 Cs0 Ts1 EX2
        W3 Q1 Qc0 R2 KH0 KH1 OUT0 S3 C1 Qc1 LNA0 SSQ0 T2 KH2 Sm3 E0 Q2 Cs1 Ts2 EX3 Q3 Qc2 C2 Qc3 R3 KH3 SSQ1 KT0
        KT1 T3 Cs2 E1 KTc0 SSQ2 KT2 KTc1 KT3 Ts3 C3 KTc2 KTc3 Cs3 CT0 SSQ3 CN0 LNB0 S4 CT1 Sm4""" if layer == 0 else """
        X0 X1 EX0 S1 Sm1 Q0 R0 Qc0 EX1 W0 LNA0 Q1 R1 W1 T0 S2 Ts0 W2 C0 T1 W3 S3 Sm2 Qc1 EX2 R2 Ts1 Cs0 C1 OUT0
        Sm3 E0 T2 E1 Cs1 Ts2 EX3 Q2 Q3 R3 Qc2 LNB0 Qc3 C2 Cs2 T3 Ts3 S4 Sm4 C3 Cs3 CN0"""
    only = {"LNA": 2, "LNB": 2, "X": 3, "CT": 2, "CN": NQ - 1, "OUT": NQ, "E": NQ}
    order = []
    for word in text.split():
        name, i = word.rstrip("01234"), int(word[-1])
        if only.get(name, j) == j:
            order.append((name, i % GB, j + i // GB))
    return order


NEXT = ("LNA", "LNB", "X", "CT", "CN")
PROJ = ("K", "Kc", "KN", "KH", "Q", "Qc", "KT", "KTc", "SSQ")
RING = ("X", "CT", "K", "Q", "KT", "SSQ", "E")
DRAINED = {"Kc": "K", "Qc": "Q", "KTc": "KT"}


def orders_of(layer):
    def each(j, *names):
        return [(name, i, j) for i in range(4) for name in names]

    pre = NQ - 1
    start = [("LNA", 0, pre), ("LNB", 0, pre)]
    if layer == 0:
        start += [("CT", 0, pre), ("CT", 1, pre)] + each(pre, "K", "Kc")
    start += [("X", 0, pre), ("X", 1, pre)]
    if layer == 0:
        start += [("KN", 0, pre)] + each(pre, "KH") + each(pre, "Q", "Qc") + each(pre, "SSQ") + each(pre, "KT", "KTc")
    else:
        start += each(pre, "Q", "Qc")
    start += [("S", 0, NQ), ("Sm", 0, NQ), ("CN", 0, pre)]
    start += [s for s in quad_order(layer, NQ) if s[0] not in ("W", "OUT", "E")]
    body = [s for j in range(1, NQ + 1) for s in quad_order(layer, j)]
    last = [s for j in range(1, NQ) for s in quad_order(layer, j)
            if s[0] not in NEXT and not (j == NQ - 1 and s[0] in PROJ) and s[2] < NQ]
    last += each(NQ, "W") + [("OUT", 0, NQ), ("E", 0, NQ), ("E", 1, NQ)]
    return {"start": start, "body": body, "last": last}


def attention(nc, core, layer, w, ctx_dram):
    L = layer
    with ExitStack() as ctx:
        def sb(name, shape, dt=F32):
            return ctx.enter_context(nc.sbuf_tensor(f"{name}_a{L}", shape, dt))

        def pair(name, shape):
            return [sb(f"{name}_{p}", shape, F32R) for p in ("hi", "lo")]

        sems = {}

        def sem(name):
            if name not in sems:
                sems[name] = core.sem(f"{name}_a{L}")
            return sems[name]

        q = sb("q", [P, 2, QH, N])
        probs = sb("probs", [P, 2, QH, P])
        pt = pair("pt", [P, QH * P])
        pc = pair("pc", [P, 2, GB, QH, P])
        xt = pair("xt", [P, KD, N])
        cn = pair("cn", [P, GB, P])
        ctx_raw = sb("ctx_raw", [P, GB, P])
        out_sb = sb("out_sb", [P, KD, N])
        bn = sb("bn", [P, GB, 6])
        mv = sb("mv", [P, 7, GB])
        rstd = sb("rstd", [P, GB])
        nmax = sb("nmax", [P, 2, QH])
        nbias = sb("nbias", [P, 2, QH])
        den = sb("den", [P, 2, QH])
        rden = sb("rden", [P, 2, QH])
        if L == 0:
            q_sq = sb("q_sq", [P, QH, N])
            xn = q_sq[:, 2:4, :].rearrange("p a (t d) -> p (a t) d", d=D)
            k_raw = sb("k_raw", [P, GB, QH * P])
            k_sq = sb("k_sq", [P, 2, QH * P])
            kt = sb("kt", [P, GB, QH * P])
            ct = pair("ct", [P, GB, P])
            k_ss = sb("k_ss", [P, GB * QH])
            k_r = sb("k_r", [P, GB * QH])
            q_ss = sb("q_ss", [P, QH, GB])
            q_r = sb("q_r", [P, 2, QH, GB])
        else:
            xn = sb("xn", [P, GB, D])
            cm = sb("cm", [P, GB, P])
        out_t = core.bank[0:2]
        proj_bank, s_bank, t_bank, c_bank = core.bank[2:4], core.bank[4:6], core.bank[6], core.bank[7]
        root = float(P) ** -0.5

        def quads(g, j):
            return g * NQ + j

        def nth(per, m, i):
            return m * per + (i + 1)

        def round_of(name, g, j):
            if name in PROJ:
                return quads(g, j + 1)
            if name in NEXT:
                return g + 1
            if name in ("OUT", "E"):
                return g
            return quads(g, j)

        per = {"X": 2, "CT": 2, "K": 4, "Q": 4, "KT": 4, "SSQ": 4, "E": 2}
        filled = {n: sem(f"{n.lower()}_filled") for n in per}
        released = {"X": sem("x_split"), "CT": sem("ct_split"), "K": sem("k_copied"), "Q": sem("q_copied"), "KT": sem("kt_copied"),
                    "SSQ": sem("ssq_copied"), "E": sem("x_updated")}
        orders = orders_of(L)
        rings = {}
        for part, order in orders.items():
            ring = [s for s in order if s[0] in RING]
            shift = len(ring) % 2 if part == "start" else 0
            rings[part] = ring, {s: (n + shift) % 2 for n, s in enumerate(ring)}
        assert len(rings["body"][0]) % 2 == 0 and rings["start"][0][-2:] == rings["body"][0][-2:]

        def walk(emit):
            for s in orders["start"]:
                emit("start", -1, *s)
            with emit.engine.Fori(0, G - 1) as g:
                for s in orders["body"]:
                    emit("body", g, *s)
            for s in orders["last"]:
                emit("last", G - 1, *s)

        with nc.Block() as block:

            @block.sync
            def _(sp):
                def load(g):
                    src = ctx_dram[bass.ds(g * GB, GB)].rearrange("b s c -> s b c")
                    sp.dma_start(ctx_raw[:, :, :], src).then_inc(sem("ctx_loaded"), 16)

                load(0)
                with sp.Fori(1, G) as g:
                    sp.wait_ge(sem("cn_ready"), g)
                    load(g)

            @block.tensor
            def _(pe):
                def bank_free(part, g, step):
                    ring, slots = rings[part]
                    at = ring.index(step)
                    if at < 2 and part == "start":
                        return proj_bank[slots[step]]
                    before, gb = (ring, g) if at >= 2 else (rings["body"][0], g - 1)
                    n, i, j = before[at - 2]
                    pe.wait_ge(released[n], nth(per[n], round_of(n, gb, j), i))
                    return proj_bank[slots[step]]

                def step(part, g, name, i, j):
                    m = round_of(name, g, j)
                    if name in RING:
                        bank = bank_free(part, g, (name, i, j))
                    if name == "X":
                        if i == 0:
                            pe.wait_ge(sem("xn_ready"), m + 1)
                        for b in range(GB):
                            last = nc.tensor.transpose(bank[:, b * P:(b + 1) * P], xn[:, b, i * P:(i + 1) * P], core.ident[:, :])
                    elif name == "CT":
                        if i == 0:
                            pe.wait_ge(sem("ctx_loaded"), m * 16 + 16)
                        for a in range(2):
                            last = nc.tensor.transpose(bank[:, a * P:(a + 1) * P], ctx_raw[:, 2 * i + a, :], core.ident[:, :])
                    elif name == "K":
                        if i % 2 == 0:
                            pe.wait_ge(sem("ct_split"), nth(2, g + (j + 1) // NQ, i // 2))
                        t = (j + 1) % NQ
                        cols = slice(t * QH * P, (t + 1) * QH * P)
                        last = three_pass(nc, bank[:, :], [c[:, i, :] for c in ct], [k[:, cols] for k in w["k"]], True, True)
                    elif name == "Q":
                        if i == 0:
                            pe.wait_ge(sem("x_split"), nth(2, g + (j + 1) // NQ, 1))
                        h = (j + 1) % NQ * QH + i
                        for k in range(KD):
                            last = three_pass(nc, bank[:, :], [a[:, k, h * P:(h + 1) * P] for a in w["q"]], [a[:, k, :] for a in xt],
                                              k == 0, k == KD - 1)
                    elif name == "KT":
                        pe.wait_ge(sem("kh_ready"), nth(4, m, i))
                        for h in range(QH):
                            last = nc.tensor.transpose(bank[:, h * P:(h + 1) * P], k_raw[:, i, h * P:(h + 1) * P], core.ident[:, :])
                    elif name == "SSQ":
                        pe.wait_ge(sem("q_squared"), nth(4, m, i))
                        for b in range(GB):
                            last = nc.tensor.matmul(bank[:, b:b + 1], q_sq[:, i, b * P:(b + 1) * P], core.ones[:, :], start=True, stop=True)
                    elif name == "S":
                        if i == 0:
                            pe.wait_ge(sem("q_copied"), nth(4, quads(g, j), 3))
                            if L == 0:
                                pe.wait_ge(sem("kt_copied"), nth(4, quads(g, j), 3))
                        bank = s_bank[i % 2]
                        if L == 1:
                            batch = (g + j // NQ) * GB + i
                            bias = w["bias"][:, bass.ds(batch * P, P)].unsqueeze(1).to_broadcast([P, QH, P])
                            nc.tensor.matmul(bank[:, :], w["bias_row"][:, :], bias, start=True, stop=False)
                            keys = w["ctx_t"][:, bass.ds(batch * P, P)]
                        for h in range(QH):
                            last = nc.tensor.matmul(bank[:, h * P:(h + 1) * P], q[:, j % 2, h, i * P:(i + 1) * P],
                                                    kt[:, i, h * P:(h + 1) * P] if L == 0 else keys, start=L == 0, stop=L == 0 or h == QH - 1)
                        last.then_inc(sem("s_filled"), 1)
                        return
                    elif name == "T":
                        pe.wait_ge(sem("probs_scaled"), nth(4, m, i))
                        for h in range(QH):
                            last = nc.tensor.transpose(t_bank[:, h * P:(h + 1) * P], probs[:, i % 2, h, :], core.ident[:, :])
                        last.then_inc(sem("t_filled"), 1)
                        return
                    elif name == "C":
                        if i == 0 and j == NQ:
                            pe.wait_ge(sem("cn_ready"), g + 2)
                        pe.wait_ge(sem("pt_ready"), nth(4, m, i))
                        pe.wait_ge(sem("pc_ready"), m * 4 + i + credit("pc_ready"))
                        last = three_pass(nc, c_bank[:, :], [a[:, i, :] for a in cn], [a[:, :] for a in pt], True, True)
                        last.then_inc(sem("c_filled"), 1)
                        return
                    elif name == "W":
                        if i == 0:
                            pe.wait_ge(sem("pc_ready"), nth(4, m - 1, GB - 1) + credit("pc_ready"))
                        if i == 0 and j == 1:
                            pe.wait_ge(sem("out_read"), 2 * g + credit("out_read"))
                        hh = (j - 1) * QH + i
                        for e in range(KD):
                            last = three_pass(nc, out_t[e][:, :], [a[:, hh, e * P:(e + 1) * P] for a in w["vo"]],
                                              [a[:, (j - 1) % 2, :, i, :] for a in pc], hh == 0, hh == H - 1)
                        last.then_inc(sem("w_done"), 1)
                        return
                    elif name == "E":
                        if i == 0:
                            pe.wait_ge(sem("out_read"), 2 * g + 2 + credit("out_read"))
                        for a in range(2):
                            for e in range(KD):
                                last = nc.tensor.transpose(bank[:, (a * KD + e) * P:(a * KD + e + 1) * P],
                                                           out_sb[:, e, (2 * i + a) * P:(2 * i + a + 1) * P], core.ident[:, :])
                    else:
                        return
                    last.then_inc(filled[name], 1)

                step.engine = pe
                walk(step)

            @block.scalar
            def _(act):
                def step(part, g, name, i, j):
                    m = round_of(name, g, j)
                    fill = DRAINED.get(name, name)
                    bank = proj_bank[rings[part][1][(fill, i, j)]] if fill in RING else None
                    if name in ("X", "CT", "KTc") or name == "Qc" and L == 1:
                        act.wait_ge(filled[fill], nth(per[fill], m, i))
                    if name == "X":
                        nc.scalar.activation(xt[0][:, i, :], bank[:, :], ACT.Copy).then_inc(sem("x_hi_ready"), 1)
                    elif name == "CT":
                        nc.scalar.activation(flat(ct[0][:, 2 * i:2 * i + 2, :]), bank[:, 0:2 * P], ACT.Copy).then_inc(sem("ct_hi_ready"), 1)
                    elif name == "KTc":
                        nc.scalar.activation(kt[:, i, :], bank[:, :], ACT.Copy, scale=w["gain"][:, 0:1]).then_inc(sem("kt_copied"), 1)
                    elif name == "Qc" and L == 0:
                        act.wait_ge(sem("q_copied"), nth(4, m, i))
                        nc.scalar.activation(q_sq[:, i, :], q[:, (j + 1) % 2, i, :], ACT.Square).then_inc(sem("q_squared"), 1)
                    elif name == "Qc":
                        nc.scalar.activation(q[:, (j + 1) % 2, i, :], bank[:, :], ACT.Copy).then_inc(sem("q_copied"), 1)
                    elif name == "Kc":
                        act.wait_ge(sem("k_summed"), nth(4, m, i) - 2 + credit("k_summed"))
                        act.wait_ge(sem("k_copied"), nth(4, m, i))
                        nc.scalar.activation(k_sq[:, i % 2, :], k_raw[:, i, :], ACT.Square).then_inc(sem("k_squared"), 1)
                    elif name == "EX":
                        act.wait_ge(sem("bias_ready"), nth(4, m, i))
                        for h in range(QH):
                            scale = q_r[:, j % 2, h, i:i + 1] if L == 0 else root
                            last = nc.scalar.activation(probs[:, i % 2, h, :], s_bank[i % 2][:, h * P:(h + 1) * P], ACT.Exp,
                                                        bias=nbias[:, i % 2, h:h + 1], scale=scale, accum_out=den[:, i % 2, h:h + 1])
                        last.then_inc(sem("exp_done"), 1)
                    elif name == "Ts":
                        act.wait_ge(sem("t_filled"), nth(4, m, i))
                        nc.scalar.activation(pt[0][:, :], t_bank[:, :], ACT.Copy).then_inc(sem("pt_hi_ready"), 1)
                    elif name == "Cs":
                        act.wait_ge(sem("c_filled"), nth(4, m, i))
                        nc.scalar.activation(flat(pc[0][:, j % 2, i, :, :]), c_bank[:, :], ACT.Copy).then_inc(sem("pc_hi_ready"), 1)
                    elif name == "OUT":
                        act.wait_ge(sem("w_done"), g * H + H)
                        for e in range(KD):
                            nc.scalar.activation(out_sb[:, e, :], out_t[e][:, :], ACT.Copy).then_inc(sem("out_read"), 1)
                    elif name == "CN":
                        if L == 0:
                            act.wait_ge(sem("ctx_loaded"), m * 16 + 16)
                            src = ctx_raw
                        else:
                            act.wait_ge(sem("ctx_masked"), m + 1)
                            src = cm
                        nc.scalar.activation(flat(cn[0][:, :, :]), flat(src[:, :, :]), ACT.Copy).then_inc(sem("cn_hi_ready"), 1)

                act.sem_inc(sem("out_read"), credit("out_read"))
                step.engine = act
                walk(step)

            @block.vector
            def _(dve):
                def step(part, g, name, i, j):
                    m = round_of(name, g, j)
                    fill = DRAINED.get(name, name)
                    bank = proj_bank[rings[part][1][(fill, i, j)]] if fill in RING else None
                    if name == "LNA":
                        for b in range(GB):
                            nc.vector.bn_stats(bn[:, b, :], flat(core.x[:, bass.ds(m * GB + b, 1), :])).then_inc(sem("stats_ready"), 1)
                        moments(nc, dve, m, bn, mv, sem)
                    elif name == "LNB":
                        dve.wait_ge(sem("rstd_ready"), m + 1)
                        for b in range(GB):
                            last = nc.vector.tensor_scalar(xn[:, b, :], flat(core.x[:, bass.ds(m * GB + b, 1), :]), mv[:, 0, b:b + 1],
                                                           rstd[:, b:b + 1], ALU.subtract, ALU.mult)
                        last.then_inc(sem("xn_ready"), 1)
                    elif name == "X":
                        dve.wait_ge(sem("x_hi_ready"), nth(2, m, i))
                        nc.vector.tensor_tensor(xt[1][:, i, :], bank[:, :], f32(xt[0][:, i, :]), ALU.subtract).then_inc(sem("x_split"), 1)
                    elif name == "CT":
                        dve.wait_ge(sem("ct_hi_ready"), nth(2, m, i))
                        hi, lo = (flat(c[:, 2 * i:2 * i + 2, :]) for c in ct)
                        nc.vector.tensor_tensor(lo, bank[:, 0:2 * P], f32(hi), ALU.subtract).then_inc(sem("ct_split"), 1)
                    elif name == "Qc" and L == 0:
                        dve.wait_ge(filled["Q"], nth(4, m, i))
                        nc.vector.tensor_copy(q[:, (j + 1) % 2, i, :], bank[:, :]).then_inc(sem("q_copied"), 1)
                    elif name == "Kc":
                        dve.wait_ge(filled["K"], nth(4, m, i))
                        nc.vector.tensor_copy(k_raw[:, i, :], bank[:, :]).then_inc(sem("k_copied"), 1)
                        dve.wait_ge(sem("k_squared"), nth(4, m, i))
                        nc.vector.tensor_reduce(k_ss[:, i * QH:(i + 1) * QH], k_sq[:, i % 2, :].rearrange("p (h d) -> p h d", d=P), AX.X,
                                                ALU.add).then_inc(sem("k_summed"), 1)
                    elif name == "KN":
                        dve.wait_ge(sem("k_summed"), nth(4, m, GB - 1) + credit("k_summed"))
                        nc.vector.tensor_scalar(k_ss[:, :], k_ss[:, :], P * EPS, None, ALU.add).then_inc(sem("k_ss_ready"), 1)
                    elif name == "SSQ":
                        dve.wait_ge(filled[name], nth(4, m, i))
                        nc.vector.tensor_scalar(q_ss[:, i, :], bank[:, 0:GB], P * EPS, None, ALU.add).then_inc(sem("ssq_copied"), 1)
                    elif name == "Sm":
                        dve.wait_ge(sem("s_filled"), nth(4, m, i))
                        nc.vector.tensor_reduce(nmax[:, i % 2, :], s_bank[i % 2][:, :].rearrange("p (h s) -> p h s", s=P), AX.X, ALU.max,
                                                negate=True).then_inc(sem("max_ready"), 1)
                        if L == 0 and i == 0:
                            dve.wait_ge(sem("q_norm_ready"), nth(4, m, QH - 1))
                        dve.wait_ge(sem("max_ready"), nth(4, m, i))
                        if L == 0:
                            last = nc.vector.tensor_tensor(nbias[:, i % 2, :], nmax[:, i % 2, :], q_r[:, j % 2, :, i], ALU.mult)
                        else:
                            last = nc.vector.tensor_scalar(nbias[:, i % 2, :], nmax[:, i % 2, :], root, None, ALU.mult)
                        last.then_inc(sem("bias_ready"), 1)
                    elif name == "R":
                        dve.wait_ge(sem("exp_done"), nth(4, m, i))
                        nc.vector.reciprocal(rden[:, i % 2, :], den[:, i % 2, :]).then_inc(sem("rden_ready"), 1)
                    elif name == "Ts":
                        dve.wait_ge(sem("pt_hi_ready"), nth(4, m, i))
                        nc.vector.tensor_tensor(pt[1][:, :], t_bank[:, :], f32(pt[0][:, :]), ALU.subtract).then_inc(sem("pt_ready"), 1)
                    elif name == "Cs":
                        dve.wait_ge(sem("pc_hi_ready"), nth(4, m, i))
                        hi, lo = (flat(c[:, j % 2, i, :, :]) for c in pc)
                        nc.vector.tensor_tensor(lo, c_bank[:, :], f32(hi), ALU.subtract).then_inc(sem("pc_ready"), 1)
                    elif name == "CN":
                        if L == 1:
                            dve.wait_ge(sem("ctx_loaded"), m * 16 + 16)
                            mask = w["mask_col"][:, bass.ds(m * GB, GB)].unsqueeze(2).to_broadcast([P, GB, P])
                            nc.vector.tensor_tensor(cm[:, :, :], ctx_raw[:, :, :], mask, ALU.mult).then_inc(sem("ctx_masked"), 1)
                        dve.wait_ge(sem("cn_hi_ready"), m + 1)
                        src = ctx_raw if L == 0 else cm
                        nc.vector.tensor_tensor(flat(cn[1][:, :, :]), flat(src[:, :, :]), f32(flat(cn[0][:, :, :])),
                                                ALU.subtract).then_inc(sem("cn_ready"), 1)
                    elif name == "E":
                        dve.wait_ge(filled[name], nth(2, m, i))
                        here = flat(core.x[:, bass.ds(g * GB + 2 * i, 2), :])
                        nc.vector.scalar_tensor_tensor(out=here, in0=bank[:, :], scalar=core.gates[:, L:L + 1], in1=here,
                                                       op0=ALU.mult, op1=ALU.add).then_inc(sem("x_updated"), 1)

                for first in ["pc_ready"] + (["k_summed"] if L == 0 else []):
                    dve.sem_inc(sem(first), credit(first))
                step.engine = dve
                walk(step)

            @block.gpsimd
            def _(pool):
                def step(part, g, name, i, j):
                    m = round_of(name, g, j)
                    if name == "LNA":
                        pool.wait_ge(sem("moments_ready"), m + 1)
                        nc.gpsimd.tensor_tensor(rstd[:, :], mv[:, 1, :], core.half[:, 0:GB], ALU.pow).then_inc(sem("rstd_ready"), 1)
                    elif name == "R":
                        pool.wait_ge(sem("rden_ready"), nth(4, m, i))
                        scale = rden[:, i % 2, :].unsqueeze(2).to_broadcast([P, QH, P])
                        nc.gpsimd.tensor_tensor(probs[:, i % 2, :, :], probs[:, i % 2, :, :], scale, ALU.mult).then_inc(sem("probs_scaled"), 1)
                    elif name == "KN":
                        pool.wait_ge(sem("k_ss_ready"), m + 1)
                        nc.gpsimd.tensor_tensor(k_r[:, :], k_ss[:, :], core.half[:, :], ALU.pow).then_inc(sem("k_r_ready"), 1)
                        pool.wait_ge(sem("k_r_ready"), m + 1)
                    elif name == "KH":
                        pool.wait_ge(sem("k_copied"), nth(4, m, i))
                        keys = k_raw[:, i, :].rearrange("p (h d) -> p h d", d=P)
                        scale = k_r[:, i * QH:(i + 1) * QH].unsqueeze(2).to_broadcast([P, QH, P])
                        nc.gpsimd.tensor_tensor(keys, keys, scale, ALU.mult).then_inc(sem("kh_ready"), 1)
                    elif name == "SSQ":
                        pool.wait_ge(sem("ssq_copied"), nth(4, m, i))
                        nc.gpsimd.tensor_tensor(q_r[:, (j + 1) % 2, i, :], q_ss[:, i, :], core.half[:, 0:GB], ALU.pow).then_inc(sem("q_norm_ready"), 1)

                step.engine = pool
                walk(step)


def flamingo(nc, a, out):
    with ExitStack() as whole:
        core = Core(nc, whole)
        for layer in range(2):
            with ExitStack() as ctx:
                def pair(name, shape):
                    return [ctx.enter_context(nc.sbuf_tensor(f"{name}_{p}{layer}", shape, F32R)) for p in ("hi", "lo")]

                def sb(name, shape, dt=F32):
                    return ctx.enter_context(nc.sbuf_tensor(f"{name}{layer}", shape, dt))

                w = {"q": pair("wq", [P, KD, H * P]), "vo": pair("wvo", [P, H, D])}
                if layer == 0:
                    w["k"] = pair("wk", [P, H * P])
                    w["gain"] = sb("gain", [P, 1])
                else:
                    w["ctx_t"] = sb("ctx_t", [P, B * P])
                    w["bias"] = sb("bias", [P, B * P], F32R)
                    w["bias_row"] = sb("bias_row", [P, P], F32R)
                    w["mask_col"] = sb("mask_col", [P, B])
                prepare_attention(nc, core, layer, a[f"L{layer}_xattn_Wq"], a[f"L{layer}_xattn_Wk"], a[f"L{layer}_xattn_Wv"],
                                  a[f"L{layer}_xattn_Wo"], w, a)
                attention(nc, core, layer, w, a["ctx_1024"])
            feed_forward(nc, core, layer, a, out)
            if layer == 0:
                core.recycle_semaphores()



def dequantise_stage(nc, core, packed, scales, targets):
    BLOCK = 32
    CODE_BITS = 0xB8 - 256 << 24
    CH = 1024
    chunks = [(m, half) for m in range(3) for half in range(2)]
    with ExitStack() as ctx:
        def sb(name, shape, dt=F32):
            return ctx.enter_context(nc.sbuf_tensor(f"{name}_dq", shape, dt))

        def sem(name):
            return core.sem(f"{name}_dq")

        words = [sb(f"words{m}", [P, 2 * CH], I32) for m in range(3)]
        scale = [sb(f"scale{m}", [P, P]) for m in range(3)]
        codes = sb("codes", [P, 2, 2, CH], I32)
        value = sb("value", [P, 2, 2 * CH])
        loaded = [sem(f"loaded{m}") for m in range(3)]
        scaled, shifted, placed, ready, filled, hi_done, drained = (
            sem(n) for n in ("scaled", "shifted", "placed", "ready", "filled", "hi_done", "drained"))
        units = [(c, u) for c in range(len(chunks)) for u in range(4)]
        with nc.Block() as block:

            def target(c, u, part):
                m, half = chunks[c]
                if m < 2:
                    cols = slice((half * 8 + 2 * u) * P, (half * 8 + 2 * u + 2) * P)
                    return targets[m][part][:, :, cols].rearrange("p k (t n) -> p t k n", n=P)
                return targets[2][part][:, 4 * u:4 * u + 4, half * P:(half + 1) * P]

            def view(n):
                c, u = units[n]
                b = core.bank[n % 8][:, :]
                return b.rearrange("p (t k n) -> p t k n", t=2, k=KD) if chunks[c][0] < 2 else b.rearrange("p (t n) -> p t n", n=P)

            @block.sync
            def _(sp):
                for m in range(3):
                    sp.dma_start(words[m][:, :], packed[m]).then_inc(loaded[m], 16)
                    sp.dma_start(scale[m][:, :], scales[m]).then_inc(loaded[m], 16)

            @block.gpsimd
            def _(pool):
                for c, (m, half) in enumerate(chunks):
                    if c >= 2:
                        pool.wait_ge(filled, 4 * (c - 1))
                    if half == 0:
                        pool.wait_ge(scaled, m + 1)
                    for nib in range(2):
                        pool.wait_ge(placed, 2 * c + nib + 1)
                        v = value[:, c % 2, :].rearrange("p (b e n) -> p b e n", e=BLOCK // 2, n=2)[:, :, :, nib]
                        quarter = codes[:, c % 2, nib, :].bitcast(F8).rearrange("p (b e n) -> p b e n", e=BLOCK // 2, n=4)[:, :, :, 3]
                        blocks = 2 * CH // BLOCK
                        sc = scale[m][:, half * blocks:(half + 1) * blocks].unsqueeze(2).to_broadcast([P, blocks, BLOCK // 2])
                        nc.gpsimd.tensor_tensor(v, quarter, sc, ALU.mult).then_inc(ready, 1)

            @block.vector
            def _(dve):
                def split(n):
                    c, u = units[n]
                    dve.wait_ge(hi_done, n + 1)
                    nc.vector.tensor_tensor(target(c, u, 1), view(n), f32(target(c, u, 0)), ALU.subtract).then_inc(drained, 1)

                for c, (m, half) in enumerate(chunks):
                    dve.wait_ge(loaded[m], 32)
                    if half == 0:
                        nc.vector.tensor_scalar(scale[m][:, :], scale[m][:, :], 4.0, None, ALU.mult).then_inc(scaled, 1)
                    if c >= 2:
                        dve.wait_ge(ready, 2 * (c - 1))
                    word = words[m][:, half * CH:(half + 1) * CH]
                    for nib in range(2):
                        nc.vector.tensor_scalar(codes[:, c % 2, nib, :], word, 28 - 4 * nib, 1, ALU.logical_shift_left,
                                                ALU.arith_shift_right).then_inc(shifted, 1)
                    for nib in range(2):
                        dve.wait_ge(shifted, 2 * c + nib + 1)
                        nc.vector.tensor_scalar(codes[:, c % 2, nib, :], codes[:, c % 2, nib, :], CODE_BITS, None,
                                                ALU.bitwise_and).then_inc(placed, 1)
                    if c:
                        for n in range(4 * (c - 1), 4 * c):
                            split(n)
                for n in range(len(units) - 4, len(units)):
                    split(n)

            @block.tensor
            def _(pe):
                for n, (c, u) in enumerate(units):
                    pe.wait_ge(ready, 2 * c + 2)
                    if n >= 8:
                        pe.wait_ge(drained, n - 7)
                    for a in range(4):
                        t = 4 * u + a
                        last = nc.tensor.transpose(core.bank[n % 8][:, a * P:(a + 1) * P], value[:, c % 2, t * P:(t + 1) * P], core.ident[:, :])
                    last.then_inc(filled, 1)

            @block.scalar
            def _(act):
                for n, (c, u) in enumerate(units):
                    act.wait_ge(filled, n + 1)
                    nc.scalar.activation(target(c, u, 0), view(n), ACT.Copy).then_inc(hi_done, 1)


def split_stage(nc, core, a, w):
    NT = w["gate"][0].shape[2] // P
    with ExitStack() as ctx:
        def sb(name, shape, dt=F32):
            return ctx.enter_context(nc.sbuf_tensor(f"{name}_sp", shape, dt))

        def sem(name):
            return core.sem(f"{name}_sp")

        raw = [sb("gate_raw", [P, KD, NF1]), sb("up_raw", [P, KD, NF1])]
        d_raw = sb("down_raw", [P, NT, D])
        router = sb("router_raw", [P, D])
        owner_f = sb("owner_f", [P, NT * P])
        loaded, loaded_d, loaded_r = sem("loaded"), sem("loaded_d"), sem("loaded_r")
        zeroed, owned, hi_done, filled, router_zero = sem("zeroed"), sem("owned"), sem("hi_done"), sem("filled"), sem("router_zero")
        full, tail = divmod(I_SH, P)
        with nc.Block() as block:

            @block.sync
            def _(sp):
                for s in range(2):
                    sp.dma_start(raw[s][:, :, 0:I_SH], a["L1_ffn_Ws_gate_up"][:, s * I_SH:(s + 1) * I_SH].rearrange("(k c) n -> c k n", c=P)).then_inc(loaded, 16)
                    for k in range(KD):
                        sp.dma_start(raw[s][:, k, I_SH:NF1].rearrange("p (e n) -> p e n", e=E),
                                     a["L1_ffn_We_gate_up"][:, k * P:(k + 1) * P, s * I_MOE:(s + 1) * I_MOE].rearrange("e c n -> c e n")).then_inc(loaded, 16)
                experts = a["L1_ffn_We_down"].rearrange("e i d -> (e i) d")
                sp.wait_ge(zeroed, 1)
                sp.dma_start(d_raw[:, 0:full, :], a["L1_ffn_Ws_down"][0:full * P].rearrange("(t p) d -> p t d", p=P)).then_inc(loaded_d, 16)
                sp.dma_start(d_raw[0:tail, full, :], a["L1_ffn_Ws_down"][full * P:I_SH]).then_inc(loaded_d, 16)
                sp.dma_start(d_raw[tail:P, full, :], experts[0:P - tail]).then_inc(loaded_d, 16)
                rest = E * I_MOE - (P - tail)
                sp.dma_start(d_raw[:, full + 1:NT - 1, :], experts[P - tail:P - tail + rest // P * P].rearrange("(t p) d -> p t d", p=P)).then_inc(loaded_d, 16)
                sp.dma_start(d_raw[0:rest % P, NT - 1, :], experts[E * I_MOE - rest % P:E * I_MOE]).then_inc(loaded_d, 16)
                sp.wait_ge(router_zero, 1)
                sp.dma_start(router[0:1, :], a["L1_ffn_W_sgate"]).then_inc(loaded_r, 16)
                sp.dma_start(router[1:1 + E, :], a["L1_ffn_W_router"]).then_inc(loaded_r, 16)

            @block.gpsimd
            def _(pool):
                nc.gpsimd.memset(d_raw[:, NT - 1, :], 0.0).then_inc(zeroed, 1)
                nc.gpsimd.memset(router[:, :], 0.0).then_inc(router_zero, 1)
                nc.gpsimd.memset(owner_f[:, :], 0.0).then_inc(owned, 1)
                n = 1
                shared = owner_f[:, 0:I_SH]
                experts = owner_f[:, I_SH:NF1].rearrange("p (e n) -> p e n", e=E)
                for first in (0, E + 1):
                    for view, pattern, base in ((shared, [[0, I_SH]], -first), (experts, [[-1, E], [0, I_MOE]], -first - 1)):
                        pool.wait_ge(owned, n)
                        nc.gpsimd.affine_select(out=view, in_=view, compare_op=ALU.not_equal, fill=1.0, base=base,
                                                pattern=pattern, channel_multiplier=1).then_inc(owned, 1)
                        n += 1
                pool.wait_ge(owned, n)
                nc.gpsimd.memset(w["tri"][:, :, :], 1.0).then_inc(owned, 1)
                pool.wait_ge(owned, n + 1)
                nc.gpsimd.affine_select(out=w["tri"][:, :, :], in_=w["tri"][:, :, :], compare_op=ALU.is_gt, fill=0.0, base=0,
                                        pattern=[[1, E], [-1, E]], channel_multiplier=0)
                nc.gpsimd.memset(w["factors"][:, :, :], 0.0)

            @block.tensor
            def _(pe):
                pe.wait_ge(loaded_r, 32)
                for k in range(KD):
                    last = nc.tensor.transpose(core.bank[0][:, k * P:(k + 1) * P], router[:, k * P:(k + 1) * P], core.ident[:, :])
                last.then_inc(filled, 1)

            @block.scalar
            def _(act):
                act.wait_ge(loaded, 16 * 6)
                for k in range(KD):
                    for s, name in enumerate(("gate", "up")):
                        nc.scalar.activation(w[name][0][:, k, 0:NF1], raw[s][:, k, :], ACT.Copy).then_inc(hi_done, 1)
                act.wait_ge(loaded_d, 16 * 5)
                nc.scalar.activation(flat(w["down"][0][:, :, :]), flat(d_raw[:, :, :]), ACT.Copy).then_inc(hi_done, 1)
                act.wait_ge(filled, 1)
                nc.scalar.activation(flat(w["router"][0][:, :, :]), core.bank[0][:, 0:D], ACT.Copy).then_inc(hi_done, 1)
                act.wait_ge(owned, 5)
                nc.scalar.activation(w["owner"][:, :], owner_f[:, :], ACT.Copy)

            @block.vector
            def _(dve):
                for name in ("gate", "up"):
                    for part in range(2):
                        nc.vector.memset(f32(w[name][part][:, :, NF1:NT * P]), 0.0)
                n = 0
                for k in range(KD):
                    for s, name in enumerate(("gate", "up")):
                        n += 1
                        dve.wait_ge(hi_done, n)
                        nc.vector.tensor_tensor(w[name][1][:, k, 0:NF1], raw[s][:, k, :], f32(w[name][0][:, k, 0:NF1]), ALU.subtract)
                dve.wait_ge(hi_done, n + 1)
                nc.vector.tensor_tensor(flat(w["down"][1][:, :, :]), flat(d_raw[:, :, :]), f32(flat(w["down"][0][:, :, :])), ALU.subtract)
                dve.wait_ge(hi_done, n + 2)
                nc.vector.tensor_tensor(flat(w["router"][1][:, :, :]), core.bank[0][:, 0:D], f32(flat(w["router"][0][:, :, :])), ALU.subtract)


def feed_forward(nc, core, layer, a, out_dram):
    L = layer
    NT = (NF0 if L == 0 else NF1 + P - 1) // P
    LAG = 2
    with ExitStack() as ctx:
        def sb(name, shape, dt=F32):
            return ctx.enter_context(nc.sbuf_tensor(f"{name}_f{L}", shape, dt))

        def pair(name, shape):
            return [sb(f"{name}_{p}", shape, F32R) for p in ("hi", "lo")]

        sems = {}

        def sem(name):
            if name not in sems:
                sems[name] = core.sem(f"{name}_f{L}")
            return sems[name]

        bn, mv = sb("bn", [P, GB, 6]), sb("mv", [P, 7, GB])
        rstd = sb("rstd", [P, GB])
        w = {"gate": pair("w_gate", [P, KD, NT * P]), "up": pair("w_up", [P, KD, NT * P]), "down": pair("w_down", [P, NT, D])}
        if L == 0:
            def rows(v):
                return v.rearrange("(t p) c -> p t c", p=P)

            def tiled(v):
                return v.rearrange("(e p) c -> p e c", p=P)

            names = ("gate", "up", "down")
            packed = [rows(a["L0_ffn_gate_W_packed"]), rows(a["L0_ffn_up_W_packed"]), tiled(a["L0_ffn_down_W_packed"])]
            scales = [rows(a["L0_ffn_gate_scales"]), rows(a["L0_ffn_up_scales"]), tiled(a["L0_ffn_down_scales"])]
            dequantise_stage(nc, core, packed, scales, [w[n] for n in names])
        else:
            w["router"] = pair("w_router", [P, KD, P])
            w["owner"] = sb("owner", [P, NT * P], F32R)
            w["tri"] = sb("tri", [P, E, E])
            w["factors"] = sb("factors", [P, GB, P])
            split_stage(nc, core, a, w)

        xt = pair("xt", [P, KD, B * P])
        xn = sb("xn", [P, GB, D])
        act_g = sb("act_g", [P, 2, N])
        hid = sb("hid", [P, 2, N])
        hs = pair("hs", [P, LAG + 1, N])
        out_sb = sb("out_sb", [P, KD, N])
        if L == 1:
            ft = sb("ft", [P, B * P], F32R)
            logit_t = sb("logit_t", [P, N])
            NF = E + 1
            logit = sb("logit", [P, GB, NF])
            lmax = sb("lmax", [P, GB])
            shifted, expd = sb("shifted", [P, GB, NF]), sb("expd", [P, GB, NF])
            sums, rsums = sb("sums", [P, GB, 2]), sb("rsums", [P, GB, 2])
            prob, factor = sb("prob", [P, GB, E]), sb("factor", [P, GB, NF])
            above, ties = sb("above", [P, GB, E, E]), sb("ties", [P, GB, E, E])
            rank = sb("rank", [P, GB, E])
        out_t, misc, g_bank, u_bank = core.bank[0:2], core.bank[2:4], core.bank[4:6], core.bank[6:8]

        nxt = [("LNA", 0), ("LNB", 0), ("X", 0), ("X", 1)]
        if L == 1:
            nxt += [("RT", 0), ("RTT", 0), ("FT", 0)]
        at = {3: nxt[:1], 5: nxt[1:2], 6: nxt[2:4], 8: nxt[4:5], 9: nxt[5:6], 12: nxt[6:7]}

        def group_order(last):
            order = []
            for i in range(NT):
                order += [("GU", i)] + ([("F", i)] if L == 1 else []) + [("A", i)] + ([("D", i - LAG)] if i >= LAG else [])
                if not last:
                    order += at.get(i, [])
            return order + [("FLUSH", 0)] + [("D", i) for i in range(NT - LAG, NT)] + [("OUT", 0), ("E", 0), ("E", 1)]

        orders = {"start": nxt, "body": group_order(False), "last": group_order(True)}
        per = {"X": 2, "RT": 1, "RTT": 1, "FT": 1, "F": NT, "E": 2}
        NEXT_STEPS = ("LNA", "LNB", "X", "RT", "RTT", "FT")
        filled = {n: sem(f"{n.lower()}_filled") for n in per if L == 1 or n in ("X", "E")}
        released = {n: sem(f"{n.lower()}_released") for n in filled}
        rings = {}
        for part, order in orders.items():
            ring = [s for s in order if s[0] in per]
            shift = len(ring) % 2 if part == "start" else 0
            rings[part] = ring, {s: (n + shift) % 2 for n, s in enumerate(ring)}
        assert len(rings["body"][0]) % 2 == 0

        def nth(n, m, i):
            return m * n + (i + 1)

        def round_of(name, g):
            return g + 1 if name in NEXT_STEPS else g

        def walk(emit):
            for s in orders["start"]:
                emit("start", -1, *s)
            with emit.engine.Fori(0, G - 1) as g:
                for s in orders["body"]:
                    emit("body", g, *s)
            for s in orders["last"]:
                emit("last", G - 1, *s)

        with nc.Block() as block:

            if L == 1:
                @block.sync
                def _(sp):
                    with sp.Fori(0, G) as g:
                        sp.wait_ge(released["E"], g * 2 + 2 + credit("E"))
                        sp.dma_start(out_dram[bass.ds(g * GB, GB)].rearrange("b s d -> s b d"),
                                     core.x[:, bass.ds(g * GB, GB), :]).then_inc(sem("stored"), 16)
                    sp.wait_ge(sem("stored"), 16 * G)

            @block.tensor
            def _(pe):
                def bank_free(part, g, step):
                    ring, slots = rings[part]
                    k = ring.index(step)
                    if k >= 2:
                        n, i = ring[k - 2]
                        pe.wait_ge(released[n], nth(per[n], round_of(n, g), i) + credit(n))
                    elif part != "start":
                        pe.wait_ge(released["E"], g * 2 + credit("E"))
                        if L == 1:
                            pe.wait_ge(released["FT"], g + 1)
                        else:
                            pe.wait_ge(released["X"], 2 * g + 2)
                    return misc[slots[step]]

                def step(part, g, name, i):
                    m = round_of(name, g)
                    if name in per:
                        bank = bank_free(part, g, (name, i))
                    if name == "X":
                        if i == 0:
                            pe.wait_ge(sem("xn_ready"), m + 1)
                        for b in range(GB):
                            last = nc.tensor.transpose(bank[:, b * P:(b + 1) * P], xn[:, b, i * P:(i + 1) * P], core.ident[:, :])
                    elif name == "GU":
                        if i == 0:
                            pe.wait_ge(released["X"], 2 * g + 2)
                        for key, banks, read in (("gate", g_bank, "gate_read"), ("up", u_bank, "up_read")):
                            if i >= 2:
                                pe.wait_ge(sem(read), g * NT + (i - 1))
                            for k in range(KD):
                                last = three_pass(nc, banks[i % 2][:, :], [v[:, k, i * P:(i + 1) * P] for v in w[key]],
                                                  [v[:, k, bass.ds(g * N, N)] for v in xt], k == 0, k == KD - 1)
                        last.then_inc(sem("up_filled"), 1)
                        return
                    elif name == "F":
                        if i == 0:
                            pe.wait_ge(released["FT"], g + 1)
                        last = nc.tensor.matmul(bank[:, :], w["owner"][:, i * P:(i + 1) * P], ft[:, bass.ds(g * N, N)], start=True, stop=True)
                    elif name == "D":
                        pe.wait_ge(sem("h_ready"), g * NT + i + 1 + credit("h_ready"))
                        if i == 0:
                            pe.wait_ge(sem("out_read"), 2 * g + credit("out_read"))
                        for e in range(KD):
                            last = three_pass(nc, out_t[e][:, :], [v[:, i, e * P:(e + 1) * P] for v in w["down"]],
                                              [v[:, i % (LAG + 1), :] for v in hs], i == 0, i == NT - 1)
                        last.then_inc(sem("down_done"), 1)
                        return
                    elif name == "E":
                        if i == 0:
                            pe.wait_ge(sem("out_read"), 2 * g + 2 + credit("out_read"))
                        for t in range(2):
                            for e in range(KD):
                                last = nc.tensor.transpose(bank[:, (t * KD + e) * P:(t * KD + e + 1) * P],
                                                           out_sb[:, e, (2 * i + t) * P:(2 * i + t + 1) * P], core.ident[:, :])
                    elif name == "RT":
                        pe.wait_ge(released["X"], 2 * m + 2)
                        for k in range(KD):
                            last = three_pass(nc, bank[:, :], [v[:, k, :] for v in w["router"]], [v[:, k, bass.ds(m * N, N)] for v in xt],
                                              k == 0, k == KD - 1)
                    elif name == "RTT":
                        pe.wait_ge(released["RT"], m + 1)
                        for b in range(GB):
                            last = nc.tensor.transpose(bank[:, b * P:(b + 1) * P], logit_t[:, b * P:(b + 1) * P], core.ident[:, :])
                    elif name == "FT":
                        pe.wait_ge(sem("factors_ready"), m + 1)
                        for b in range(GB):
                            last = nc.tensor.transpose(bank[:, b * P:(b + 1) * P], w["factors"][:, b, :], core.ident[:, :])
                    else:
                        return
                    last.then_inc(filled[name], 1)

                step.engine = pe
                walk(step)

            @block.scalar
            def _(act):
                def split_hi(g, i):
                    act.wait_ge(released["F"] if L == 1 else sem("up_read"), g * NT + i + 1)
                    nc.scalar.activation(hs[0][:, i % (LAG + 1), :], hid[:, i % 2, :], ACT.Copy).then_inc(sem("h_hi_ready"), 1)

                def step(part, g, name, i):
                    m = round_of(name, g)
                    bank = misc[rings[part][1][(name, i)]] if name in per else None
                    if name == "X":
                        act.wait_ge(filled[name], nth(2, m, i))
                        nc.scalar.activation(xt[0][:, i, bass.ds(m * N, N)], bank[:, :], ACT.Copy).then_inc(sem("x_hi_ready"), 1)
                    elif name == "A":
                        act.wait_ge(sem("up_filled"), g * NT + i + 1)
                        nc.scalar.activation(act_g[:, i % 2, :], g_bank[i % 2][:, :], ACT.Gelu_apprx_tanh if L == 0 else ACT.Silu).then_inc(sem("gate_read"), 1)
                        if i:
                            split_hi(g, i - 1)
                    elif name == "FLUSH":
                        split_hi(g, NT - 1)
                    elif name == "OUT":
                        act.wait_ge(sem("down_done"), g * NT + NT)
                        for e in range(KD):
                            nc.scalar.activation(out_sb[:, e, :], out_t[e][:, :], ACT.Copy).then_inc(sem("out_read"), 1)
                    elif name == "RT":
                        act.wait_ge(filled["RT"], m + 1)
                        nc.scalar.activation(logit_t[:, :], bank[:, :], ACT.Copy).then_inc(released["RT"], 1)
                    elif name == "RTT":
                        act.wait_ge(sem("shifted_ready"), m + 1)
                        nc.scalar.activation(flat(expd[:, :, :]), flat(shifted[:, :, :]), ACT.Exp).then_inc(sem("exp_ready"), 1)
                        act.wait_ge(sem("factor_ready"), m + 1)
                        nc.scalar.activation(w["factors"][:, :, 0:NF].bitcast(F32R), factor[:, :, :], ACT.Copy).then_inc(sem("factor_hi_ready"), 1)
                    elif name == "FT":
                        act.wait_ge(filled["FT"], m + 1)
                        nc.scalar.activation(ft[:, bass.ds(m * N, N)], bank[:, :], ACT.Copy).then_inc(released["FT"], 1)

                act.sem_inc(sem("out_read"), 1)
                step.engine = act
                walk(step)

            @block.vector
            def _(dve):
                CHAIN = 11

                def router_factors(m, bank):
                    steps = [0]

                    def chained(ins):
                        steps[0] += 1
                        ins.then_inc(sem("router_step"), 1)
                        dve.wait_ge(sem("router_step"), m * CHAIN + steps[0])

                    nc.vector.tensor_copy(logit[:, :, :], bank[:, :].rearrange("p (b r) -> p b r", r=P)[:, :, 0:NF]).then_inc(released["RTT"], 1)
                    dve.wait_ge(released["RTT"], m + 1)
                    chained(nc.vector.tensor_reduce(lmax[:, :], logit[:, :, 1:NF], AX.X, ALU.max))
                    nc.vector.tensor_scalar(shifted[:, :, 0:1], logit[:, :, 0:1], -1.0, None, ALU.mult)
                    nc.vector.tensor_tensor(shifted[:, :, 1:NF], logit[:, :, 1:NF], lmax[:, :].unsqueeze(2).to_broadcast([P, GB, E]),
                                            ALU.subtract).then_inc(sem("shifted_ready"), 1)
                    dve.wait_ge(sem("exp_ready"), m + 1)
                    chained(nc.vector.tensor_reduce(sums[:, :, 0:1], expd[:, :, 1:NF], AX.X, ALU.add))
                    chained(nc.vector.tensor_scalar(sums[:, :, 1:2], expd[:, :, 0:1], 1.0, None, ALU.add))
                    chained(nc.vector.reciprocal(rsums[:, :, :], sums[:, :, :]))
                    chained(nc.vector.tensor_copy(factor[:, :, 0:1], rsums[:, :, 1:2]))
                    chained(nc.vector.tensor_tensor(prob[:, :, :], expd[:, :, 1:NF], rsums[:, :, 0:1].to_broadcast([P, GB, E]), ALU.mult))
                    pj = prob[:, :, :].unsqueeze(2).to_broadcast([P, GB, E, E])
                    pe_ = prob[:, :, :].unsqueeze(3).to_broadcast([P, GB, E, E])
                    chained(nc.vector.tensor_tensor(ties[:, :, :, :], pj, pe_, ALU.is_equal))
                    nc.vector.tensor_tensor(above[:, :, :, :], pj, pe_, ALU.is_gt)
                    chained(nc.vector.tensor_tensor(ties[:, :, :, :], ties[:, :, :, :], w["tri"][:, :, :].unsqueeze(1).to_broadcast([P, GB, E, E]), ALU.mult))
                    chained(nc.vector.tensor_tensor(above[:, :, :, :], above[:, :, :, :], ties[:, :, :, :], ALU.add))
                    chained(nc.vector.tensor_reduce(rank[:, :, :], above[:, :, :, :], AX.X, ALU.add))
                    chained(nc.vector.scalar_tensor_tensor(out=factor[:, :, 1:NF], in0=rank[:, :, :], scalar=2.0, in1=prob[:, :, :],
                                                           op0=ALU.is_lt, op1=ALU.mult))
                    assert steps[0] == CHAIN
                    nc.vector.tensor_copy(logit[:, :, :], factor[:, :, :]).then_inc(sem("factor_ready"), 1)
                    dve.wait_ge(sem("factor_hi_ready"), m + 1)
                    nc.vector.tensor_tensor(w["factors"][:, :, NF:2 * NF], factor[:, :, :], w["factors"][:, :, 0:NF],
                                            ALU.subtract).then_inc(sem("factors_ready"), 1)

                def split_lo(g, i):
                    dve.wait_ge(sem("h_hi_ready"), g * NT + i + 1)
                    s = i % (LAG + 1)
                    nc.vector.tensor_tensor(hs[1][:, s, :], hid[:, i % 2, :], f32(hs[0][:, s, :]), ALU.subtract).then_inc(sem("h_ready"), 1)

                def step(part, g, name, i):
                    m = round_of(name, g)
                    bank = misc[rings[part][1][(name, i)]] if name in per else None
                    if name == "LNA":
                        for b in range(GB):
                            nc.vector.bn_stats(bn[:, b, :], flat(core.x[:, bass.ds(m * GB + b, 1), :])).then_inc(sem("stats_ready"), 1)
                        moments(nc, dve, m, bn, mv, sem)
                    elif name == "LNB":
                        dve.wait_ge(sem("rstd_ready"), m + 1)
                        for b in range(GB):
                            last = nc.vector.tensor_scalar(xn[:, b, :], flat(core.x[:, bass.ds(m * GB + b, 1), :]), mv[:, 0, b:b + 1],
                                                           rstd[:, b:b + 1], ALU.subtract, ALU.mult)
                        last.then_inc(sem("xn_ready"), 1)
                    elif name == "X":
                        dve.wait_ge(sem("x_hi_ready"), nth(2, m, i))
                        nc.vector.tensor_tensor(xt[1][:, i, bass.ds(m * N, N)], bank[:, :], f32(xt[0][:, i, bass.ds(m * N, N)]),
                                                ALU.subtract).then_inc(released["X"], 1)
                    elif name == "A":
                        dve.wait_ge(sem("h_ready"), g * NT + max(i - 1, 0) + credit("h_ready"))
                        dve.wait_ge(sem("gate_read"), g * NT + i + 1)
                        nc.vector.tensor_tensor(hid[:, i % 2, :], act_g[:, i % 2, :], u_bank[i % 2][:, :], ALU.mult).then_inc(sem("up_read"), 1)
                        if i:
                            split_lo(g, i - 1)
                        if L == 1:
                            dve.wait_ge(filled["F"], g * NT + i + 1)
                            dve.wait_ge(sem("up_read"), g * NT + i + 1)
                            nc.vector.tensor_tensor(hid[:, i % 2, :], hid[:, i % 2, :], misc[rings[part][1][("F", i)]][:, :],
                                                    ALU.mult).then_inc(released["F"], 1)
                    elif name == "FLUSH":
                        split_lo(g, NT - 1)
                    elif name == "RTT":
                        dve.wait_ge(filled["RTT"], m + 1)
                        router_factors(m, bank)
                    elif name == "E":
                        dve.wait_ge(filled[name], nth(2, g, i))
                        here = flat(core.x[:, bass.ds(g * GB + 2 * i, 2), :])
                        nc.vector.scalar_tensor_tensor(out=here, in0=bank[:, :], scalar=core.gates[:, 2 + L:3 + L], in1=here,
                                                       op0=ALU.mult, op1=ALU.add).then_inc(released[name], 1)

                dve.sem_inc(released["E"], 1)
                dve.sem_inc(sem("h_ready"), 1)
                step.engine = dve
                walk(step)

            @block.gpsimd
            def _(pool):
                def step(part, g, name, i):
                    m = round_of(name, g)
                    if name == "LNA":
                        pool.wait_ge(sem("moments_ready"), m + 1)
                        nc.gpsimd.tensor_tensor(rstd[:, :], mv[:, 1, :], core.half[:, 0:GB], ALU.pow).then_inc(sem("rstd_ready"), 1)

                step.engine = pool
                walk(step)


_INS = ["x", "ctx_1024", "mask_BxS2_bf1", "g_xattn", "g_ffn",
        "L0_xattn_Wq", "L0_xattn_Wk", "L0_xattn_Wv", "L0_xattn_Wo", "L0_xattn_gq", "L0_xattn_gk",
        "L0_ffn_gate_W_packed", "L0_ffn_gate_scales", "L0_ffn_up_W_packed", "L0_ffn_up_scales",
        "L0_ffn_down_W_packed", "L0_ffn_down_scales", "L1_xattn_Wq", "L1_xattn_Wk", "L1_xattn_Wv", "L1_xattn_Wo",
        "L1_ffn_W_router", "L1_ffn_W_sgate", "L1_ffn_Ws_gate_up", "L1_ffn_Ws_down", "L1_ffn_We_gate_up", "L1_ffn_We_down"]


def kernel(**inputs):
    import numpy as np
    import concourse.bacc as bacc
    from concourse.bass_utils import run_bass_kernel_spmd

    nc = bacc.Bacc("TRN2", target_bir_lowering=False, num_devices=1)
    arrays, aps = {}, {}
    for name in _INS:
        v = np.ascontiguousarray(inputs[name])
        if v.dtype == np.bool_:
            v = v.view(np.uint8)
        arrays[f"in_{name}"] = v
        aps[name] = nc.dram_tensor(f"in_{name}", v.shape, mybir.dt.from_np(v.dtype), kind="ExternalInput").ap()
    out = nc.dram_tensor("out", (B, P, D), F32, kind="ExternalOutput").ap()
    flamingo(nc, aps, out)
    r = run_bass_kernel_spmd(nc, [arrays], core_ids=[0])
    return r.results[0]["out"]
```

```python
from contextlib import ExitStack

import concourse.bass as bass
from concourse import mybir

F32 = mybir.dt.float32
F32R = mybir.dt.float32r
I32 = mybir.dt.int32
U8 = mybir.dt.uint8
F8 = mybir.dt.float8e3
ALU = mybir.AluOpType
ACT = mybir.ActivationFunctionType
AX = mybir.AxisListType

P = 128
B = 16
D = 256
KD = D // P
H = 16
GB = 4
G = B // GB
N = GB * P
QH = 4
NQ = H // QH
EPS = 1e-5
MASKED = -float(2 ** 100)
SKV = 8
I_SH, I_MOE, E = 704, 176, 8
NF0 = 2048
NF1 = I_SH + E * I_MOE


def f32(ap):
    return ap.bitcast(F32)


class Core:

    def __init__(self, nc, ctx):
        self.nc, self.ctx = nc, ctx
        self.x = self.sb("x_sb", [P, B, D])
        self.ident = self.sb("ident", [P, P])
        self.gates = self.sb("gates", [P, 4])
        self.half = self.sb("half", [P, 16])
        self.bn, self.mv, self.rstd = self.sb("bn", [P, GB, 6]), self.sb("mv", [P, 7, GB]), self.sb("rstd", [P, GB])
        self.bank = [ctx.enter_context(nc.psum_tensor(f"bank{i}", [P, N], F32)) for i in range(8)]

        self.sems = []
        self.x_loaded = self.sem("x_loaded_first"), self.sem("x_loaded_rest")

    def sem(self, name):
        self.sems.append(self.nc.alloc_semaphore(name))
        return self.sems[-1]

    def recycle_semaphores(self, kept):
        self.nc.clear_and_free_semaphores([s for s in self.sems if s not in kept])
        self.sems = list(kept)
        self.nc.all_engine_barrier()

    def sb(self, name, shape, dt=F32):
        return self.ctx.enter_context(self.nc.sbuf_tensor(name, shape, dt))

    def two_views(self, name, shape, ctx):
        offset = (self.nc.sbuf_base + 31) // 32 * 32
        rounded = ctx.enter_context(self.nc.sbuf_tensor(f"{name}_lo", shape, F32R))
        return self.nc.alloc_sbuf_tensor_at(f"{name}_raw", shape, F32, offset=offset), rounded


def three_pass(nc, out, w, x, start, stop):
    nc.tensor.matmul(out, w[0], x[0], start=start, stop=False)
    nc.tensor.matmul(out, w[0], x[1], start=False, stop=False)
    return nc.tensor.matmul(out, w[1], x[0], start=False, stop=stop)


class TokenNorm:

    def __init__(self, nc, core, name):
        self.nc, self.core = nc, core
        self.stats_ready, self.halves_ready, self.moments_ready, self.rstd_ready = self.sems = [
            core.sem(f"{n}_{name}") for n in ("stats_ready", "halves_ready", "moments_ready", "rstd_ready")]

    def statistics(self, dve, m):
        nc, bn, mv = self.nc, self.core.bn, self.core.mv
        for b in range(GB):
            nc.vector.bn_stats(bn[:, b, :], flat(self.core.x[:, bass.ds(m * GB + b, 1), :])).then_inc(self.stats_ready, 1)
        mean_e, dev_e, mean_o, dev_o = (bn[:, :, k] for k in (1, 2, 4, 5))
        dve.wait_ge(self.stats_ready, m * GB + GB)
        nc.vector.tensor_tensor(mv[:, 2, :], mean_e, mean_o, ALU.add)
        nc.vector.tensor_tensor(mv[:, 3, :], mean_e, mean_o, ALU.subtract)
        nc.vector.tensor_tensor(mv[:, 4, :], dev_e, dev_o, ALU.add).then_inc(self.halves_ready, 1)
        dve.wait_ge(self.halves_ready, m * 2 + 1)
        nc.vector.tensor_scalar(mv[:, 0, :], mv[:, 2, :], 0.5, None, ALU.mult)
        nc.vector.scalar_tensor_tensor(out=mv[:, 5, :], in0=mv[:, 3, :], scalar=0.25, in1=mv[:, 3, :], op0=ALU.mult, op1=ALU.mult)
        nc.vector.tensor_scalar(mv[:, 6, :], mv[:, 4, :], 1.0 / D, EPS, ALU.mult, ALU.add).then_inc(self.halves_ready, 1)
        dve.wait_ge(self.halves_ready, m * 2 + 2)
        nc.vector.tensor_tensor(mv[:, 1, :], mv[:, 6, :], mv[:, 5, :], ALU.add).then_inc(self.moments_ready, 1)

    def root(self, pool, m):
        pool.wait_ge(self.moments_ready, m + 1)
        self.nc.gpsimd.tensor_tensor(self.core.rstd[:, :], self.core.mv[:, 1, :], self.core.half[:, 0:GB], ALU.pow).then_inc(self.rstd_ready, 1)

    def normalise(self, dve, m, xn, ready):
        dve.wait_ge(self.rstd_ready, m + 1)
        for b in range(GB):
            last = self.nc.vector.tensor_scalar(xn[:, b, :], flat(self.core.x[:, bass.ds(m * GB + b, 1), :]), self.core.mv[:, 0, b:b + 1],
                                                self.core.rstd[:, b:b + 1], ALU.subtract, ALU.mult)
        last.then_inc(ready, 1)


def credit(name):
    return {"k_summed": 2, "pc_ready": 1, "out_read": 1}.get(name, 0)


def flat(ap):
    return ap.rearrange("p a b -> p (a b)")



class EarlyWeights:

    def __init__(self, nc, core, ctx, a):
        def sb(name, shape):
            return ctx.enter_context(nc.sbuf_tensor(name, shape, F32, side="right"))

        self.v, self.k, self.o = sb("v_early", [P, SKV * P]), sb("k_early", [P, SKV * P]), sb("o_early", [P, H, D])
        self.ctx = sb("ctx_early", [P, B, P])
        self.loaded = {n: core.sem(f"{n}_early_loaded") for n in "vkoc"}
        self.a = a

    def load(self, sp):
        a = self.a
        sp.dma_start(self.v[:, :], a["L1_xattn_Wv"]).then_inc(self.loaded["v"], 16)
        sp.dma_start(self.k[:, :], a["L1_xattn_Wk"]).then_inc(self.loaded["k"], 16)
        sp.dma_start(self.ctx[:, :, :], a["ctx_1024"].rearrange("b s c -> s b c")).then_inc(self.loaded["c"], 16)
        sp.dma_start(self.o[:, :, :], a["L1_xattn_Wo"].rearrange("(h d) e -> d h e", d=P)).then_inc(self.loaded["o"], 16)


def prepare_attention(nc, core, layer, Wq, Wk, Wv, Wo, w, a, early, norm):
    kv = H if layer == 0 else SKV
    rep = H // kv
    nq_t = 0 if layer == 0 else KD * H // 4
    nk_t = 0 if layer == 0 else kv // 4
    nv_t = kv // 4
    with ExitStack() as ctx:
        def sb(name, shape, dt=F32):
            return ctx.enter_context(nc.sbuf_tensor(f"{name}_p{layer}", shape, dt))

        def sem(name):
            return core.sem(f"{name}_p{layer}")

        q_raw = sb("q_raw", [P, KD, H * P])
        if early:
            k_raw, v_raw, o_raw, ctx_raw = early.k, early.v, early.o, early.ctx
        else:
            k_raw, v_raw, o_raw = sb("k_raw", [P, kv * P]), sb("v_raw", [P, kv * P]), sb("o_raw", [P, H, D])
        v_t = sb("v_t", [P, kv, P])
        loaded_q = [sem(f"loaded_q{k}") for k in range(KD)]
        loaded_k, loaded_v, loaded_o = (early.loaded[n] if early else sem(f"loaded_{n}") for n in "kvo")
        filled, hi_done, raw_hi, drained, split_done = (sem(n) for n in ("bank_filled", "hi_done", "raw_hi_done", "transposes_drained", "split_done"))
        if layer == 1:
            q_t = sb("q_t", [P, H, KD, P])
            k_t = sb("k_t", [P, kv, P])
            maskrow, maskcol8 = sb("maskrow", [1, B * P], U8), sb("maskcol8", [P, B], U8)
            loaded_c, loaded_m, zeroed = early.loaded["c"], sem("loaded_m"), sem("zeroed")
        else:
            small = sb("small", [P, 6])
            loaded_s, zeroed, ident_made, made = (sem(n) for n in ("loaded_s", "zeroed", "ident_made", "made"))

        units = [("v_t", i) for i in range(nv_t)] + [("k_t", i) for i in range(nk_t)]
        if layer == 1:
            units += [("ctx", i) for i in range(G)]
        units += [("vo", i) for i in range(H // 2)]
        if layer == 1:
            units += [("q_t", i) for i in range(nq_t)] + [("m", i) for i in range(KD * H // 4)]

        as_loaded = [("vo", 3), ("vo", 6)]

        def is_product(n):
            return units[n][0] in ("vo", "m")

        def before(n):
            return sum(is_product(k) == is_product(n) for k in range(n))

        with nc.Block() as block:

            @block.sync
            def _(sp):
                if layer == 0:
                    sp.dma_start(small[:, 0:2], a["g_xattn"].partition_broadcast(P)).then_inc(loaded_s, 16)
                    sp.dma_start(small[:, 2:4], a["g_ffn"].partition_broadcast(P)).then_inc(loaded_s, 16)
                    sp.dma_start(small[:, 4:5], a["L0_xattn_gq"].rearrange("(p a) -> p a", a=1)).then_inc(loaded_s, 16)
                    sp.dma_start(small[:, 5:6], a["L0_xattn_gk"].rearrange("(p a) -> p a", a=1)).then_inc(loaded_s, 16)
                    sp.dma_start(v_raw[:, :], Wv).then_inc(loaded_v, 16)
                    sp.dma_start(o_raw[:, :, :], Wo.rearrange("(h d) e -> d h e", d=P)).then_inc(loaded_o, 16)
                for k in range(KD):
                    sp.dma_start(q_raw[:, k, :], Wq[k * P:(k + 1) * P]).then_inc(loaded_q[k], 16)
                if layer == 0:
                    sp.dma_start(k_raw[:, :], Wk).then_inc(loaded_k, 16)
                if layer == 0:
                    for g in range(G):
                        tokens = slice(g * GB, (g + 1) * GB)
                        sp.dma_start(core.x[:, tokens, :], a["x"][tokens].rearrange("b s d -> s b d")).then_inc(core.x_loaded[g > 0], 16)
                else:
                    sp.dma_start(maskrow[:, :], a["mask_BxS2_bf1"].rearrange("(a b) s -> a (b s)", a=1)).then_inc(loaded_m, 16)
                    with nc.allow_non_contiguous_dma("2 KB of mask, transposed"):
                        sp.dma_start(maskcol8[:, :], a["mask_BxS2_bf1"].rearrange("b s -> s b")).then_inc(loaded_m, 16)

            if layer == 0:
                @block.gpsimd
                def _(pool):
                    nc.gpsimd.memset(core.ident[:, :], 0.0).then_inc(zeroed, 1)
                    nc.gpsimd.memset(core.half[:, :], -0.5).then_inc(made, 1)
                    pool.wait_ge(zeroed, 1)
                    nc.gpsimd.affine_select(out=core.ident[:, :], in_=core.ident[:, :], compare_op=ALU.not_equal,
                                            fill=1.0, base=0, pattern=[[-1, P]], channel_multiplier=1).then_inc(ident_made, 1)
                    pool.wait_ge(made, 1)
                    pool.wait_ge(raw_hi, 2)
                    nc.gpsimd.tensor_tensor(w["q"][1][:, 1, :], q_raw[:, 1, :], f32(w["q"][0][:, 1, :]), ALU.subtract)
            else:
                @block.gpsimd
                def _(pool):
                    norm.root(pool, 0)

            @block.tensor
            def _(pe):
                if layer == 0:
                    pe.wait_ge(ident_made, 1)
                for n, (kind, i) in enumerate(units):
                    out = core.bank[n % 8]
                    if n >= 8:
                        pe.wait_ge(split_done if is_product(n - 8) else drained, before(n - 8) + 1)
                    if kind == "v_t":
                        pe.wait_ge(loaded_v, 16)
                        for a in range(4):
                            last = nc.tensor.transpose(out[:, a * P:(a + 1) * P], v_raw[:, (4 * i + a) * P:(4 * i + a + 1) * P], core.ident[:, :])
                    elif kind == "q_t":
                        for s in loaded_q:
                            pe.wait_ge(s, 16)
                        for a in range(4):
                            h, k = divmod(4 * i + a, KD)
                            last = nc.tensor.transpose(out[:, a * P:(a + 1) * P], q_raw[:, k, h * P:(h + 1) * P], core.ident[:, :])
                    elif kind == "k_t":
                        pe.wait_ge(loaded_k, 16)
                        for a in range(4):
                            last = nc.tensor.transpose(out[:, a * P:(a + 1) * P], k_raw[:, (4 * i + a) * P:(4 * i + a + 1) * P], core.ident[:, :])
                    elif kind == "ctx":
                        pe.wait_ge(loaded_c, 16)
                        for a in range(4):
                            last = nc.tensor.transpose(out[:, a * P:(a + 1) * P], ctx_raw[:, 4 * i + a, :], core.ident[:, :])
                    elif kind == "vo":
                        if i == 0:
                            pe.wait_ge(loaded_o, 16)
                            pe.wait_ge(drained, nv_t)
                        for a in range(2):
                            h = 2 * i + a
                            last = nc.tensor.matmul(out[:, a * D:(a + 1) * D], v_t[:, h // rep, :], o_raw[:, h, :], start=True, stop=True)
                    else:
                        pe.wait_ge(drained, nv_t + nk_t + G + i + 1)
                        for a in range(4):
                            h, k = divmod(4 * i + a, KD)
                            last = nc.tensor.matmul(out[:, a * P:(a + 1) * P], q_t[:, h, k, :], k_t[:, h // rep, :], start=True, stop=True)
                    last.then_inc(filled, 1)

            def target(kind, i, part):
                if kind == "vo":
                    return flat(w["vo"][part][:, 2 * i:2 * i + 2, :])
                return w["q"][part].rearrange("p k (h c) -> p h k c", c=P)[:, 2 * i:2 * i + 2, :, :]

            def bank_view(n, kind):
                return core.bank[n % 8][:, :].rearrange("p (h k c) -> p h k c", h=2, k=KD) if kind == "m" else core.bank[n % 8][:, :]

            @block.scalar
            def _(act):
                if layer == 0:
                    act.wait_ge(loaded_s, 64)
                    nc.scalar.activation(core.gates[:, :], small[:, 0:4], ACT.Tanh)
                for n, (kind, i) in enumerate(units):
                    if layer == 0 and units[n] in as_loaded:
                        k = as_loaded.index(units[n])
                        act.wait_ge(loaded_q[k], 16)
                        nc.scalar.activation(w["q"][0][:, k, :], q_raw[:, k, :], ACT.Copy).then_inc(raw_hi, 1)
                    act.wait_ge(filled, n + 1)
                    if kind == "v_t":
                        nc.scalar.activation(flat(v_t[:, 4 * i:4 * i + 4, :]), core.bank[n % 8][:, :], ACT.Copy).then_inc(drained, 1)
                    elif kind == "q_t":
                        nc.scalar.activation(q_t[:, 2 * i:2 * i + 2, :, :].rearrange("p h k c -> p (h k c)"), core.bank[n % 8][:, :], ACT.Copy).then_inc(drained, 1)
                    elif kind == "ctx":
                        nc.scalar.activation(w["ctx_t"][:, i * N:(i + 1) * N], core.bank[n % 8][:, :], ACT.Copy).then_inc(drained, 1)
                    elif kind == "k_t":
                        nc.scalar.activation(flat(k_t[:, 4 * i:4 * i + 4, :]), core.bank[n % 8][:, :], ACT.Copy).then_inc(drained, 1)
                    else:
                        nc.scalar.activation(target(kind, i, 0), bank_view(n, kind), ACT.Copy).then_inc(hi_done, 1)
                if layer == 0:
                    act.wait_ge(loaded_k, 16)
                    nc.scalar.activation(w["k"][0][:, :], k_raw[:, :], ACT.Copy).then_inc(raw_hi, 1)

            @block.vector
            def _(dve):
                if layer == 0:
                    dve.wait_ge(loaded_s, 64)
                    nc.vector.scalar_tensor_tensor(out=w["gain"][:, :], in0=small[:, 4:5], scalar=float(P) ** 0.5, in1=small[:, 5:6],
                                                   op0=ALU.mult, op1=ALU.mult)
                else:
                    norm.statistics(dve, 0)
                    nc.vector.memset(f32(w["bias"][:, :]), 0.0).then_inc(zeroed, 1)
                    dve.wait_ge(loaded_m, 32)
                    dve.wait_ge(zeroed, 1)
                    nc.vector.tensor_scalar(w["bias"][0:1, :], maskrow[:, :], 1.0, -MASKED, ALU.subtract, ALU.mult)
                    nc.vector.tensor_copy(w["mask_col"][:, :], maskcol8[:, :])
                    nc.vector.memset(f32(w["bias_row"][:, :]), 0.0).then_inc(zeroed, 1)
                    dve.wait_ge(zeroed, 2)
                    nc.vector.memset(f32(w["bias_row"][0:1, :]), 1.0)
                for n, (kind, i) in enumerate(units):
                    if not is_product(n):
                        continue
                    if layer == 0 and units[n] == as_loaded[0]:
                        dve.wait_ge(raw_hi, 1)
                        nc.vector.tensor_tensor(w["q"][1][:, 0, :], q_raw[:, 0, :], f32(w["q"][0][:, 0, :]), ALU.subtract)
                    dve.wait_ge(hi_done, before(n) + 1)
                    nc.vector.tensor_tensor(target(kind, i, 1), bank_view(n, kind), f32(target(kind, i, 0)),
                                            ALU.subtract).then_inc(split_done, 1)
                if layer == 0:
                    dve.wait_ge(raw_hi, KD + 1)
                    nc.vector.tensor_tensor(w["k"][1][:, :], k_raw[:, :], f32(w["k"][0][:, :]), ALU.subtract)



def quad_order(layer, j):
    text = """
        K0 S1 Kc0 X0 EX0 Sm1 W0 R0 Kq0 K1 K2 W1 Rp0 K3 EX1 Kc1 Kq1 Kc2 Kr0 Kc3 X1 T0 R1 Th0 Kq2 S2 Kr1 Tl0 Kq3
        Q0 C0 Rp1 T1 Q1 Kr2 S3 Qv0 Kr3 Sm2 Ch0 KN0 QT0 Cl0 Th1 Qv1 KH0 Qq0 W2 EX2 Sm3 QTc0 Tl1 Q2 R2 Qr0 EX3 C1
        Rp2 Qq1 QT1 Qv2 Q3 Ch1 R3 Qr1 T2 QTc1 Cl1 Qv3 Qq2 Qr2 KT0 Th2 KH1 Tl2 CT0 KTc0 W3 KH2 KT1 Rp3 QT2 C2 Qq3
        KH3 OUT0 LNA0 KTc1 E0 QTc2 Ch2 E1 T3 KT2 Th3 KTc2 KT3 KTc3 Qp0 Qp1 Qp2 Cl2 QT3 Tl3 QTc3 LNB0 C3 Qr3 Ch3
        CT1 Cl3 Qp3 CN0 S4 Sm4""" if layer == 0 else """
        X0 X1 EX0 S1 Sm1 Q0 R0 Rp0 Qc0 EX1 W0 LNA0 Q1 R1 Rp1 W1 T0 S2 Th0 Tl0 W2 C0 T1 W3 S3 Sm2 Qc1 EX2 R2 Rp2
        Th1 Tl1 Ch0 Cl0 C1 OUT0 Sm3 E0 T2 E1 Ch1 Cl1 Th2 Tl2 EX3 Q2 Q3 R3 Rp3 Qc2 LNB0 Qc3 C2 Ch2 Cl2 T3 Th3 Tl3
        S4 Sm4 C3 Ch3 Cl3 CN0"""
    only = {"LNA": 2, "LNB": 2, "X": 3, "CT": 2, "CN": NQ - 1, "OUT": NQ, "E": NQ}
    order = []
    for word in text.split():
        name, i = word.rstrip("01234"), int(word[-1])
        if only.get(name, j) == j:
            order.append((name, i % GB, j + i // GB))
    return order


NEXT = ("LNA", "LNB", "X", "CT", "CN")
PROJ = ("K", "Kc", "Kq", "Kr", "KN", "KH", "KT", "KTc", "Q", "Qc", "Qv", "Qq", "Qr", "Qp", "QT", "QTc")
RING = ("X", "CT", "K", "Q", "KT", "QT", "E")
DRAINED = {"Kc": "K", "Qc": "Q", "Qv": "Q", "KTc": "KT", "QTc": "QT"}


def orders_of(layer):
    def each(j, *names):
        return [(name, i, j) for i in range(4) for name in names]

    pre = NQ - 1
    start = [("LNA", 0, pre)] if layer == 0 else []
    start += [("LNB", 0, pre)]
    if layer == 0:
        start += [("CT", 0, pre), ("CT", 1, pre)] + [("K", 0, pre), ("Kc", 0, pre), ("K", 1, pre), ("Kc", 1, pre), ("Kq", 0, pre), ("Kr", 0, pre), ("K", 2, pre), ("Kc", 2, pre),
                                                    ("Kq", 1, pre), ("Kr", 1, pre), ("K", 3, pre), ("Kc", 3, pre)] + [(n, i, pre) for i in (2, 3) for n in ("Kq", "Kr")]
    start += [("X", 0, pre), ("X", 1, pre)]
    if layer == 0:
        start += [("KN", 0, pre)] + each(pre, "KH") + [("Q", 0, pre), ("Qv", 0, pre)]
        for i in range(4):
            start += [("Q", i + 1, pre)] * (i < 3) + [("Qq", i, pre), ("QT", i, pre), ("QTc", i, pre), ("Qr", i, pre), ("Qp", i, pre)]
            start += [("Qv", i + 1, pre)] * (i < 3)
        start += each(pre, "KT", "KTc")
    else:
        start += each(pre, "Q", "Qc")
    start += [("S", 0, NQ), ("Sm", 0, NQ), ("CN", 0, pre)]
    start += [s for s in quad_order(layer, NQ) if s[0] not in ("W", "OUT", "E")]
    body = [s for j in range(1, NQ + 1) for s in quad_order(layer, j)]
    last = [s for j in range(1, NQ) for s in quad_order(layer, j)
            if s[0] not in NEXT and not (j == NQ - 1 and s[0] in PROJ) and s[2] < NQ]
    last += [("LNF", 0, NQ)] + each(NQ, "W") + [("OUT", 0, NQ), ("E", 0, NQ), ("E", 1, NQ)]
    return {"start": start, "body": body, "last": last}


def attention(nc, core, layer, w, a, gate_up, norm, norm_after):
    L = layer
    ctx_dram = a["ctx_1024"]
    with ExitStack() as ctx:
        def sb(name, shape, dt=F32):
            return ctx.enter_context(nc.sbuf_tensor(f"{name}_a{L}", shape, dt))

        def pair(name, shape):
            return [sb(f"{name}_{p}", shape, F32R) for p in ("hi", "lo")]

        sems = {}

        def sem(name):
            if name not in sems:
                sems[name] = core.sem(f"{name}_a{L}")
            return sems[name]

        q = sb("q", [P, 2, QH, N])
        probs = sb("probs", [P, 2, QH, P])
        pt = pair("pt", [P, QH * P])
        pc = pair("pc", [P, 2, GB, QH, P])
        xt = pair("xt", [P, KD, N])
        cn = pair("cn", [P, GB, P])
        ctx_raw = sb("ctx_raw", [P, GB, P])
        out_sb = sb("out_sb", [P, KD, N])
        xn = out_sb[:, :, :].rearrange("p k (b d) -> p (k b) d", d=D)
        nmax = sb("nmax", [P, 2, QH])
        nbias = sb("nbias", [P, 2, QH])
        den = sb("den", [P, 2, QH])
        rden = sb("rden", [P, 2, QH])
        if L == 0:
            q_tok = sb("q_tok", [P, 2, QH * P])
            q_sq = sb("q_sq", [P, 2, QH * P])
            k_raw = sb("k_raw", [P, GB, QH * P])
            k_sq = sb("k_sq", [P, 2, QH * P])
            kt = sb("kt", [P, GB, QH * P])
            ct = pair("ct", [P, GB, P])
            k_ss = sb("k_ss", [P, GB * QH])
            k_r = sb("k_r", [P, GB * QH])
            q_ss = sb("q_ss", [P, GB, QH])
            q_r = sb("q_r", [P, 2, GB, QH])
        else:
            cm = sb("cm", [P, GB, P])
        out_t = core.bank[0:2]
        proj_bank, s_bank, t_bank, c_bank = core.bank[2:4], core.bank[4:6], core.bank[6], core.bank[7]
        root = float(P) ** -0.5

        def quads(g, j):
            return g * NQ + j

        def nth(per, m, i):
            return m * per + (i + 1)

        def round_of(name, g, j):
            if name in PROJ:
                return quads(g, j + 1)
            if name in NEXT:
                return g + 1
            if name in ("OUT", "E"):
                return g
            return quads(g, j)

        per = {"X": 2, "CT": 2, "K": 4, "Q": 4, "KT": 4, "QT": 4, "E": 2}
        filled = {n: sem(f"{n.lower()}_filled") for n in per}
        released = {"X": sem("x_split"), "CT": sem("ct_split"), "K": sem("k_copied"), "KT": sem("kt_copied"),
                    "Q": sem("q_tok_copied" if L == 0 else "q_copied"), "QT": sem("q_copied"), "E": sem("x_updated")}
        orders = orders_of(L)
        rings = {}
        for part, order in orders.items():
            ring = [s for s in order if s[0] in RING]
            shift = len(ring) % 2 if part == "start" else 0
            rings[part] = ring, {s: (n + shift) % 2 for n, s in enumerate(ring)}
        assert len(rings["body"][0]) % 2 == 0 and rings["start"][0][-2:] == rings["body"][0][-2:]

        def walk(emit):
            for s in orders["start"]:
                emit("start", -1, *s)
            with emit.engine.Fori(0, G - 1) as g:
                for s in orders["body"]:
                    emit("body", g, *s)
            for s in orders["last"]:
                emit("last", G - 1, *s)

        with nc.Block() as block:

            @block.sync
            def _(sp):
                def load(g):
                    src = ctx_dram[bass.ds(g * GB, GB)].rearrange("b s c -> s b c")
                    sp.dma_start(ctx_raw[:, :, :], src).then_inc(sem("ctx_loaded"), 16)

                load(0)
                if L == 1:
                    load_gate_up(sp, a, [raw for raw, _ in gate_up[0]], gate_up[1])
                with sp.Fori(1, G) as g:
                    sp.wait_ge(sem("cn_ready"), g)
                    load(g)

            @block.tensor
            def _(pe):
                def bank_free(part, g, step):
                    ring, slots = rings[part]
                    at = ring.index(step)
                    if at < 2 and part == "start":
                        return proj_bank[slots[step]]
                    before, gb = (ring, g) if at >= 2 else (rings["body"][0], g - 1)
                    n, i, j = before[at - 2]
                    pe.wait_ge(released[n], nth(per[n], round_of(n, gb, j), i))
                    return proj_bank[slots[step]]

                def step(part, g, name, i, j):
                    m = round_of(name, g, j)
                    if name in RING:
                        bank = bank_free(part, g, (name, i, j))
                    if name == "X":
                        if i == 0:
                            pe.wait_ge(sem("xn_ready"), m + 1)
                        for b in range(GB):
                            last = nc.tensor.transpose(bank[:, b * P:(b + 1) * P], xn[:, b, i * P:(i + 1) * P], core.ident[:, :])
                    elif name == "CT":
                        if i == 0:
                            pe.wait_ge(sem("ctx_loaded"), m * 16 + 16)
                        for a in range(2):
                            last = nc.tensor.transpose(bank[:, a * P:(a + 1) * P], ctx_raw[:, 2 * i + a, :], core.ident[:, :])
                    elif name == "K":
                        if i % 2 == 0:
                            pe.wait_ge(sem("ct_split"), nth(2, g + (j + 1) // NQ, i // 2))
                        t = (j + 1) % NQ
                        cols = slice(t * QH * P, (t + 1) * QH * P)
                        last = three_pass(nc, bank[:, :], [c[:, i, :] for c in ct], [k[:, cols] for k in w["k"]], True, True)
                    elif name == "Q":
                        if i == 0:
                            pe.wait_ge(sem("x_split"), nth(2, g + (j + 1) // NQ, 1))
                        h = (j + 1) % NQ * QH + i
                        cols = slice((j + 1) % NQ * QH * P, ((j + 1) % NQ + 1) * QH * P)
                        for k in range(KD if L == 0 else 0):
                            last = three_pass(nc, bank[:, :], [a[:, k, i * P:(i + 1) * P] for a in xt], [a[:, k, cols] for a in w["q"]],
                                              k == 0, k == KD - 1)
                        for k in range(KD if L == 1 else 0):
                            last = three_pass(nc, bank[:, :], [a[:, k, h * P:(h + 1) * P] for a in w["q"]], [a[:, k, :] for a in xt],
                                              k == 0, k == KD - 1)
                    elif name == "KT":
                        pe.wait_ge(sem("kh_ready"), nth(4, m, i))
                        for h in range(QH):
                            last = nc.tensor.transpose(bank[:, h * P:(h + 1) * P], k_raw[:, i, h * P:(h + 1) * P], core.ident[:, :])
                    elif name == "QT":
                        pe.wait_ge(sem("q_tok_copied"), nth(4, m, i))
                        for h in range(QH):
                            last = nc.tensor.transpose(bank[:, h * P:(h + 1) * P], q_tok[:, i % 2, h * P:(h + 1) * P], core.ident[:, :])
                    elif name == "S":
                        if i == 0:
                            pe.wait_ge(sem("q_copied"), nth(4, quads(g, j), 3))
                            if L == 0:
                                pe.wait_ge(sem("kt_copied"), nth(4, quads(g, j), 3))
                        bank = s_bank[i % 2]
                        if L == 1:
                            batch = (g + j // NQ) * GB + i
                            bias = w["bias"][:, bass.ds(batch * P, P)].unsqueeze(1).to_broadcast([P, QH, P])
                            nc.tensor.matmul(bank[:, :], w["bias_row"][:, :], bias, start=True, stop=False)
                            keys = w["ctx_t"][:, bass.ds(batch * P, P)]
                        for h in range(QH):
                            last = nc.tensor.matmul(bank[:, h * P:(h + 1) * P], q[:, j % 2, h, i * P:(i + 1) * P],
                                                    kt[:, i, h * P:(h + 1) * P] if L == 0 else keys, start=L == 0, stop=L == 0 or h == QH - 1)
                        last.then_inc(sem("s_filled"), 1)
                        return
                    elif name == "T":
                        pe.wait_ge(sem("probs_scaled"), nth(4, m, i))
                        for h in range(QH):
                            last = nc.tensor.transpose(t_bank[:, h * P:(h + 1) * P], probs[:, i % 2, h, :], core.ident[:, :])
                        last.then_inc(sem("t_filled"), 1)
                        return
                    elif name == "C":
                        if i == 0 and j == NQ:
                            pe.wait_ge(sem("cn_ready"), g + 2)
                        pe.wait_ge(sem("pt_ready"), nth(4, m, i))
                        pe.wait_ge(sem("pc_ready"), m * 4 + i + credit("pc_ready"))
                        last = three_pass(nc, c_bank[:, :], [a[:, i, :] for a in cn], [a[:, :] for a in pt], True, True)
                        last.then_inc(sem("c_filled"), 1)
                        return
                    elif name == "W":
                        if i == 0:
                            pe.wait_ge(sem("pc_ready"), nth(4, m - 1, GB - 1) + credit("pc_ready"))
                        if i == 0 and j == 1:
                            pe.wait_ge(sem("out_read"), 2 * g + credit("out_read"))
                        hh = (j - 1) * QH + i
                        for e in range(KD):
                            last = three_pass(nc, out_t[e][:, :], [a[:, hh, e * P:(e + 1) * P] for a in w["vo"]],
                                              [a[:, (j - 1) % 2, :, i, :] for a in pc], hh == 0, hh == H - 1)
                        last.then_inc(sem("w_done"), 1)
                        return
                    elif name == "E":
                        if i == 0:
                            pe.wait_ge(sem("out_read"), 2 * g + 2 + credit("out_read"))
                        for a in range(2):
                            for e in range(KD):
                                last = nc.tensor.transpose(bank[:, (a * KD + e) * P:(a * KD + e + 1) * P],
                                                           out_sb[:, e, (2 * i + a) * P:(2 * i + a + 1) * P], core.ident[:, :])
                    else:
                        return
                    last.then_inc(filled[name], 1)

                step.engine = pe
                walk(step)

            @block.scalar
            def _(act):
                def step(part, g, name, i, j):
                    m = round_of(name, g, j)
                    fill = DRAINED.get(name, name)
                    bank = proj_bank[rings[part][1][(fill, i, j)]] if fill in RING else None
                    if name in ("X", "CT", "KTc", "Qc", "QTc"):
                        act.wait_ge(filled[fill], nth(per[fill], m, i))
                    if name == "X":
                        nc.scalar.activation(xt[0][:, i, :], bank[:, :], ACT.Copy).then_inc(sem("x_hi_ready"), 1)
                    elif name == "CT":
                        nc.scalar.activation(flat(ct[0][:, 2 * i:2 * i + 2, :]), bank[:, 0:2 * P], ACT.Copy).then_inc(sem("ct_hi_ready"), 1)
                    elif name == "KTc":
                        nc.scalar.activation(kt[:, i, :], bank[:, :], ACT.Copy, scale=w["gain"][:, 0:1]).then_inc(sem("kt_copied"), 1)
                    elif name == "Qq":
                        act.wait_ge(sem("q_tok_copied"), nth(4, m, i))
                        nc.scalar.activation(q_sq[:, i % 2, :], q_tok[:, i % 2, :], ACT.Square).then_inc(sem("q_squared"), 1)
                    elif name == "QTc":
                        nc.scalar.activation(q[:, (j + 1) % 2, :, i * P:(i + 1) * P], bank[:, :].rearrange("p (h t) -> p h t", t=P),
                                             ACT.Copy).then_inc(sem("q_copied"), 1)
                    elif name == "Qc":
                        nc.scalar.activation(q[:, (j + 1) % 2, i, :], bank[:, :], ACT.Copy).then_inc(sem("q_copied"), 1)
                    elif name == "Kq":
                        act.wait_ge(sem("k_summed"), nth(4, m, i) - 2 + credit("k_summed"))
                        act.wait_ge(sem("k_copied"), nth(4, m, i))
                        nc.scalar.activation(k_sq[:, i % 2, :], k_raw[:, i, :], ACT.Square).then_inc(sem("k_squared"), 1)
                    elif name == "EX":
                        act.wait_ge(sem("bias_ready"), nth(4, m, i))
                        for h in range(QH):
                            scale = q_r[:, j % 2, i, h:h + 1] if L == 0 else root
                            last = nc.scalar.activation(probs[:, i % 2, h, :], s_bank[i % 2][:, h * P:(h + 1) * P], ACT.Exp,
                                                        bias=nbias[:, i % 2, h:h + 1], scale=scale, accum_out=den[:, i % 2, h:h + 1])
                        last.then_inc(sem("exp_done"), 1)
                    elif name == "Th":
                        act.wait_ge(sem("t_filled"), nth(4, m, i))
                        nc.scalar.activation(pt[0][:, :], t_bank[:, :], ACT.Copy).then_inc(sem("pt_hi_ready"), 1)
                    elif name == "Ch":
                        act.wait_ge(sem("c_filled"), nth(4, m, i))
                        nc.scalar.activation(flat(pc[0][:, j % 2, i, :, :]), c_bank[:, :], ACT.Copy).then_inc(sem("pc_hi_ready"), 1)
                    elif name == "OUT":
                        act.wait_ge(sem("w_done"), g * H + H)
                        for e in range(KD):
                            nc.scalar.activation(out_sb[:, e, :], out_t[e][:, :], ACT.Copy).then_inc(sem("out_read"), 1)
                    elif name == "CN":
                        if L == 0:
                            act.wait_ge(sem("ctx_loaded"), m * 16 + 16)
                            src = ctx_raw
                        else:
                            act.wait_ge(sem("ctx_masked"), m + 1)
                            src = cm
                        nc.scalar.activation(flat(cn[0][:, :, :]), flat(src[:, :, :]), ACT.Copy).then_inc(sem("cn_hi_ready"), 1)

                act.sem_inc(sem("out_read"), credit("out_read"))
                step.engine = act
                walk(step)

            @block.vector
            def _(dve):
                def step(part, g, name, i, j):
                    m = round_of(name, g, j)
                    fill = DRAINED.get(name, name)
                    bank = proj_bank[rings[part][1][(fill, i, j)]] if fill in RING else None
                    if name == "LNF":
                        norm_after.statistics(dve, 0)
                    elif name == "LNA":
                        if L == 0:
                            dve.wait_ge(core.x_loaded[part != "start"], 16 if part == "start" else 16 * (G - 1))
                        norm.statistics(dve, m)
                    elif name == "LNB":
                        norm.normalise(dve, m, xn, sem("xn_ready"))
                    elif name == "X":
                        dve.wait_ge(sem("x_hi_ready"), nth(2, m, i))
                        nc.vector.tensor_tensor(xt[1][:, i, :], bank[:, :], f32(xt[0][:, i, :]), ALU.subtract).then_inc(sem("x_split"), 1)
                    elif name == "CT":
                        dve.wait_ge(sem("ct_hi_ready"), nth(2, m, i))
                        hi, lo = (flat(c[:, 2 * i:2 * i + 2, :]) for c in ct)
                        nc.vector.tensor_tensor(lo, bank[:, 0:2 * P], f32(hi), ALU.subtract).then_inc(sem("ct_split"), 1)
                    elif name == "Qv":
                        dve.wait_ge(filled["Q"], nth(4, m, i))
                        nc.vector.tensor_copy(q_tok[:, i % 2, :], bank[:, :]).then_inc(sem("q_tok_copied"), 1)
                    elif name == "Kc":
                        dve.wait_ge(filled["K"], nth(4, m, i))
                        nc.vector.tensor_copy(k_raw[:, i, :], bank[:, :]).then_inc(sem("k_copied"), 1)
                    elif name == "Kr":
                        dve.wait_ge(sem("k_squared"), nth(4, m, i))
                        nc.vector.tensor_reduce(k_ss[:, i * QH:(i + 1) * QH], k_sq[:, i % 2, :].rearrange("p (h d) -> p h d", d=P), AX.X,
                                                ALU.add).then_inc(sem("k_summed"), 1)
                    elif name == "KN":
                        dve.wait_ge(sem("k_summed"), nth(4, m, GB - 1) + credit("k_summed"))
                        nc.vector.tensor_scalar(k_ss[:, :], k_ss[:, :], P * EPS, None, ALU.add).then_inc(sem("k_ss_ready"), 1)
                    elif name == "Qr":
                        dve.wait_ge(sem("q_squared"), nth(4, m, i))
                        nc.vector.tensor_reduce(q_ss[:, i, :], q_sq[:, i % 2, :].rearrange("p (h d) -> p h d", d=P), AX.X,
                                                ALU.add).then_inc(sem("q_summed"), 1)
                        dve.wait_ge(sem("q_summed"), nth(4, m, i))
                        nc.vector.tensor_scalar(q_ss[:, i, :], q_ss[:, i, :], P * EPS, None, ALU.add).then_inc(sem("q_ss_ready"), 1)
                    elif name == "Sm":
                        dve.wait_ge(sem("s_filled"), nth(4, m, i))
                        nc.vector.tensor_reduce(nmax[:, i % 2, :], s_bank[i % 2][:, :].rearrange("p (h s) -> p h s", s=P), AX.X, ALU.max,
                                                negate=True).then_inc(sem("max_ready"), 1)
                        if L == 0 and i == 0:
                            dve.wait_ge(sem("q_norm_ready"), nth(4, m, QH - 1))
                        dve.wait_ge(sem("max_ready"), nth(4, m, i))
                        if L == 0:
                            last = nc.vector.tensor_tensor(nbias[:, i % 2, :], nmax[:, i % 2, :], q_r[:, j % 2, i, :], ALU.mult)
                        else:
                            last = nc.vector.tensor_scalar(nbias[:, i % 2, :], nmax[:, i % 2, :], root, None, ALU.mult)
                        last.then_inc(sem("bias_ready"), 1)
                    elif name == "R":
                        dve.wait_ge(sem("exp_done"), nth(4, m, i))
                        nc.vector.reciprocal(rden[:, i % 2, :], den[:, i % 2, :]).then_inc(sem("rden_ready"), 1)
                    elif name == "Tl":
                        dve.wait_ge(sem("pt_hi_ready"), nth(4, m, i))
                        nc.vector.tensor_tensor(pt[1][:, :], t_bank[:, :], f32(pt[0][:, :]), ALU.subtract).then_inc(sem("pt_ready"), 1)
                    elif name == "Cl":
                        dve.wait_ge(sem("pc_hi_ready"), nth(4, m, i))
                        hi, lo = (flat(c[:, j % 2, i, :, :]) for c in pc)
                        nc.vector.tensor_tensor(lo, c_bank[:, :], f32(hi), ALU.subtract).then_inc(sem("pc_ready"), 1)
                    elif name == "CN":
                        if L == 1:
                            dve.wait_ge(sem("ctx_loaded"), m * 16 + 16)
                            mask = w["mask_col"][:, bass.ds(m * GB, GB)].unsqueeze(2).to_broadcast([P, GB, P])
                            nc.vector.tensor_tensor(cm[:, :, :], ctx_raw[:, :, :], mask, ALU.mult).then_inc(sem("ctx_masked"), 1)
                        dve.wait_ge(sem("cn_hi_ready"), m + 1)
                        src = ctx_raw if L == 0 else cm
                        nc.vector.tensor_tensor(flat(cn[1][:, :, :]), flat(src[:, :, :]), f32(flat(cn[0][:, :, :])),
                                                ALU.subtract).then_inc(sem("cn_ready"), 1)
                    elif name == "E":
                        dve.wait_ge(filled[name], nth(2, m, i))
                        here = flat(core.x[:, bass.ds(g * GB + 2 * i, 2), :])
                        nc.vector.scalar_tensor_tensor(out=here, in0=bank[:, :], scalar=core.gates[:, L:L + 1], in1=here,
                                                       op0=ALU.mult, op1=ALU.add).then_inc(sem("x_updated"), 1)

                for first in ["pc_ready"] + (["k_summed"] if L == 0 else []):
                    dve.sem_inc(sem(first), credit(first))
                step.engine = dve
                walk(step)

            @block.gpsimd
            def _(pool):
                def step(part, g, name, i, j):
                    m = round_of(name, g, j)
                    if name == "LNF":
                        norm_after.root(pool, 0)
                    elif name == "LNA":
                        norm.root(pool, m)
                    elif name == "Rp":
                        pool.wait_ge(sem("rden_ready"), nth(4, m, i))
                        scale = rden[:, i % 2, :].unsqueeze(2).to_broadcast([P, QH, P])
                        nc.gpsimd.tensor_tensor(probs[:, i % 2, :, :], probs[:, i % 2, :, :], scale, ALU.mult).then_inc(sem("probs_scaled"), 1)
                    elif name == "KN":
                        pool.wait_ge(sem("k_ss_ready"), m + 1)
                        nc.gpsimd.tensor_tensor(k_r[:, :], k_ss[:, :], core.half[:, :], ALU.pow).then_inc(sem("k_r_ready"), 1)
                        pool.wait_ge(sem("k_r_ready"), m + 1)
                    elif name == "KH":
                        pool.wait_ge(sem("k_copied"), nth(4, m, i))
                        keys = k_raw[:, i, :].rearrange("p (h d) -> p h d", d=P)
                        scale = k_r[:, i * QH:(i + 1) * QH].unsqueeze(2).to_broadcast([P, QH, P])
                        nc.gpsimd.tensor_tensor(keys, keys, scale, ALU.mult).then_inc(sem("kh_ready"), 1)
                    elif name == "Qp":
                        pool.wait_ge(sem("q_ss_ready"), nth(4, m, i))
                        nc.gpsimd.tensor_tensor(q_r[:, (j + 1) % 2, i, :], q_ss[:, i, :], core.half[:, 0:QH], ALU.pow).then_inc(sem("q_norm_ready"), 1)

                step.engine = pool
                walk(step)


def flamingo(nc, a, out):
    with ExitStack() as whole:
        core = Core(nc, whole)
        early, early_space = None, whole.enter_context(ExitStack())
        for layer in range(2):
            gate_up = None
            norm, norm_ffn = TokenNorm(nc, core, f"a{layer}"), TokenNorm(nc, core, f"f{layer}")
            if layer == 1:
                tiles = (NF1 + P - 1) // P
                gate_up = [core.two_views(f"w_{n}", [P, KD, tiles * P], whole) for n in ("gate", "up")], core.sem("gate_up_loaded")
            with ExitStack() as ctx:
                def pair(name, shape):
                    return [ctx.enter_context(nc.sbuf_tensor(f"{name}_{p}{layer}", shape, F32R)) for p in ("hi", "lo")]

                def sb(name, shape, dt=F32):
                    return ctx.enter_context(nc.sbuf_tensor(f"{name}{layer}", shape, dt))

                w = {"q": pair("wq", [P, KD, H * P]), "vo": pair("wvo", [P, H, D])}
                if layer == 0:
                    w["k"] = pair("wk", [P, H * P])
                    w["gain"] = sb("gain", [P, 1])
                else:
                    w["ctx_t"] = sb("ctx_t", [P, B * P])
                    w["bias"] = sb("bias", [P, B * P], F32R)
                    w["bias_row"] = sb("bias_row", [P, P], F32R)
                    w["mask_col"] = sb("mask_col", [P, B])
                prepare_attention(nc, core, layer, a[f"L{layer}_xattn_Wq"], a[f"L{layer}_xattn_Wk"], a[f"L{layer}_xattn_Wv"],
                                  a[f"L{layer}_xattn_Wo"], w, a, early, norm)
                early_space.close()
                attention(nc, core, layer, w, a, gate_up, norm, norm_ffn)
            if layer == 0:
                core.recycle_semaphores(norm_ffn.sems)
                early = EarlyWeights(nc, core, early_space, a)
            feed_forward(nc, core, layer, a, out, gate_up, early, norm_ffn)



def dequantise_stage(nc, core, packed, scales, targets):
    BLOCK = 32
    CODE_BITS = 0xB8 - 256 << 24
    CH = 1024
    chunks = [(m, half) for m in range(3) for half in range(2)]
    with ExitStack() as ctx:
        def sb(name, shape, dt=F32):
            return ctx.enter_context(nc.sbuf_tensor(f"{name}_dq", shape, dt))

        def sem(name):
            return core.sem(f"{name}_dq")

        words = [sb(f"words{m}", [P, 2 * CH], I32) for m in range(3)]
        scale = [sb(f"scale{m}", [P, P]) for m in range(3)]
        codes = sb("codes", [P, 2, 2, CH], I32)
        value = sb("value", [P, 2, 2 * CH])
        loaded = [sem(f"loaded{m}") for m in range(3)]
        scaled, shifted, placed, ready, filled, hi_done, drained = (
            sem(n) for n in ("scaled", "shifted", "placed", "ready", "filled", "hi_done", "drained"))
        units = [(c, u) for c in range(len(chunks)) for u in range(4)]
        with nc.Block() as block:

            def target(c, u, part):
                m, half = chunks[c]
                if m < 2:
                    cols = slice((half * 8 + 2 * u) * P, (half * 8 + 2 * u + 2) * P)
                    return targets[m][part][:, :, cols].rearrange("p k (t n) -> p t k n", n=P)
                return targets[2][part][:, 4 * u:4 * u + 4, half * P:(half + 1) * P]

            def view(n):
                c, u = units[n]
                b = core.bank[n % 8][:, :]
                return b.rearrange("p (t k n) -> p t k n", t=2, k=KD) if chunks[c][0] < 2 else b.rearrange("p (t n) -> p t n", n=P)

            @block.sync
            def _(sp):
                for m in range(3):
                    sp.dma_start(words[m][:, :], packed[m]).then_inc(loaded[m], 16)
                    sp.dma_start(scale[m][:, :], scales[m]).then_inc(loaded[m], 16)

            @block.gpsimd
            def _(pool):
                for c, (m, half) in enumerate(chunks):
                    if c >= 2:
                        pool.wait_ge(filled, 4 * (c - 1))
                    if half == 0:
                        pool.wait_ge(scaled, m + 1)
                    for nib in range(2):
                        pool.wait_ge(placed, 2 * c + nib + 1)
                        v = value[:, c % 2, :].rearrange("p (b e n) -> p b e n", e=BLOCK // 2, n=2)[:, :, :, nib]
                        quarter = codes[:, c % 2, nib, :].bitcast(F8).rearrange("p (b e n) -> p b e n", e=BLOCK // 2, n=4)[:, :, :, 3]
                        blocks = 2 * CH // BLOCK
                        sc = scale[m][:, half * blocks:(half + 1) * blocks].unsqueeze(2).to_broadcast([P, blocks, BLOCK // 2])
                        nc.gpsimd.tensor_tensor(v, quarter, sc, ALU.mult).then_inc(ready, 1)

            @block.vector
            def _(dve):
                def split(n):
                    c, u = units[n]
                    dve.wait_ge(hi_done, n + 1)
                    nc.vector.tensor_tensor(target(c, u, 1), view(n), f32(target(c, u, 0)), ALU.subtract).then_inc(drained, 1)

                for c, (m, half) in enumerate(chunks):
                    dve.wait_ge(loaded[m], 32)
                    if half == 0:
                        nc.vector.tensor_scalar(scale[m][:, :], scale[m][:, :], 4.0, None, ALU.mult).then_inc(scaled, 1)
                    if c >= 2:
                        dve.wait_ge(ready, 2 * (c - 1))
                    word = words[m][:, half * CH:(half + 1) * CH]
                    for nib in range(2):
                        nc.vector.tensor_scalar(codes[:, c % 2, nib, :], word, 28 - 4 * nib, 1, ALU.logical_shift_left,
                                                ALU.arith_shift_right).then_inc(shifted, 1)
                    for nib in range(2):
                        dve.wait_ge(shifted, 2 * c + nib + 1)
                        nc.vector.tensor_scalar(codes[:, c % 2, nib, :], codes[:, c % 2, nib, :], CODE_BITS, None,
                                                ALU.bitwise_and).then_inc(placed, 1)
                    if c:
                        for n in range(4 * (c - 1), 4 * c):
                            split(n)
                for n in range(len(units) - 4, len(units)):
                    split(n)

            @block.tensor
            def _(pe):
                for n, (c, u) in enumerate(units):
                    pe.wait_ge(ready, 2 * c + 2)
                    if n >= 8:
                        pe.wait_ge(drained, n - 7)
                    for a in range(4):
                        t = 4 * u + a
                        last = nc.tensor.transpose(core.bank[n % 8][:, a * P:(a + 1) * P], value[:, c % 2, t * P:(t + 1) * P], core.ident[:, :])
                    last.then_inc(filled, 1)

            @block.scalar
            def _(act):
                for n, (c, u) in enumerate(units):
                    act.wait_ge(filled, n + 1)
                    nc.scalar.activation(target(c, u, 0), view(n), ACT.Copy).then_inc(hi_done, 1)


def load_gate_up(dma, a, raw, loaded):
    shared, experts = a["L1_ffn_Ws_gate_up"], a["L1_ffn_We_gate_up"]
    for s in range(2):
        dma.dma_start(raw[s][:, :, 0:I_SH], shared[:, s * I_SH:(s + 1) * I_SH].rearrange("(k c) n -> c k n", c=P)).then_inc(loaded, 16)
        for k in range(KD):
            dma.dma_start(raw[s][:, k, I_SH:NF1].rearrange("p (e n) -> p e n", e=E),
                          experts[:, k * P:(k + 1) * P, s * I_MOE:(s + 1) * I_MOE].rearrange("e c n -> c e n")).then_inc(loaded, 16)


def feed_forward(nc, core, layer, a, out_dram, gate_up, early, norm):
    L = layer
    NT = (NF0 if L == 0 else NF1 + P - 1) // P
    LAG = 2
    with ExitStack() as ctx:
        def sb(name, shape, dt=F32):
            return ctx.enter_context(nc.sbuf_tensor(f"{name}_f{L}", shape, dt))

        def pair(name, shape):
            return [sb(f"{name}_{p}", shape, F32R) for p in ("hi", "lo")]

        sems = {}

        def sem(name):
            if name not in sems:
                sems[name] = core.sem(f"{name}_f{L}")
            return sems[name]

        if L == 0:
            w = {"gate": pair("w_gate", [P, KD, NT * P]), "up": pair("w_up", [P, KD, NT * P]), "down": pair("w_down", [P, NT, D])}

            def rows(v):
                return v.rearrange("(t p) c -> p t c", p=P)

            def tiled(v):
                return v.rearrange("(e p) c -> p e c", p=P)

            names = ("gate", "up", "down")
            packed = [rows(a["L0_ffn_gate_W_packed"]), rows(a["L0_ffn_up_W_packed"]), tiled(a["L0_ffn_down_W_packed"])]
            scales = [rows(a["L0_ffn_gate_scales"]), rows(a["L0_ffn_up_scales"]), tiled(a["L0_ffn_down_scales"])]
            dequantise_stage(nc, core, packed, scales, [w[n] for n in names])
        else:
            views = {"gate": gate_up[0][0], "up": gate_up[0][1], "down": core.two_views("w_down", [P, NT, D], ctx)}
            w_raw = {n: raw for n, (raw, _) in views.items()}
            w = {n: [sb(f"w_{n}_hi", lo.shape, F32R), lo] for n, (_, lo) in views.items()}
            w["router"] = pair("w_router", [P, KD, P])
            w["owner"] = sb("owner", [P, NT * P], F32R)
            w["tri"] = sb("tri", [P, E, E])
            w["factors"] = sb("factors", [P, GB, P])
            router_raw = sb("router_raw", [P, D])

        xt = pair("xt", [P, KD, B * P])
        xn = sb("xn", [P, GB, D])
        act_g = sb("act_g", [P, 2, N])
        hid = sb("hid", [P, 2, N])
        hs = pair("hs", [P, LAG + 1, N])
        out_sb = sb("out_sb", [P, KD, N])
        if L == 1:
            ft = sb("ft", [P, B * P], F32R)
            logit_t = sb("logit_t", [P, N])
            NF = E + 1
            logit = sb("logit", [P, GB, NF])
            lmax = sb("lmax", [P, GB])
            shifted, expd = sb("shifted", [P, GB, NF]), sb("expd", [P, GB, NF])
            sums, rsums = sb("sums", [P, GB, 2]), sb("rsums", [P, GB, 2])
            prob, factor = sb("prob", [P, GB, E]), sb("factor", [P, GB, NF])
            above, ties = sb("above", [P, GB, E, E]), sb("ties", [P, GB, E, E])
            rank = sb("rank", [P, GB, E])
        out_t, misc, g_bank, u_bank = core.bank[0:2], core.bank[2:4], core.bank[4:6], core.bank[6:8]

        ahead = {3: ["LNA 0"], 5: ["LNB 0"], 7: ["X 0", "X 1"]}
        if L == 1:
            ahead.update({8: ["RT 0"], 9: ["RTT 0"], 10: ["SM 0"], 11: ["TOP 0"], 13: ["FT 0"]})

        def steps(*words, groups=0):
            return [(word.split()[0], int(word.split()[1]), groups) for word in words]

        def group_order(first_tile, finish, prepare, split):
            rest = ["FLUSH 0"] + [f"D {i}" for i in range(NT - LAG, NT)], ["OUT 0"]
            order = []
            for i in range(first_tile, NT):
                order += steps(f"GU {i}") + (steps(*rest[0], groups=-1) if finish and i == 0 else [])
                order += steps(f"E {i - 1}", groups=-1) if finish and 1 <= i <= 2 else []
                order += steps(f"F {i}", f"A {i}", f"AF {i}") if L == 1 else steps(f"A {i}")
                order += steps(*rest[1], groups=-1) if finish and i == 0 else []
                order += steps(f"D {i - LAG}") if i >= LAG else []
                order += steps(f"SG {i // 2 + 2}") if split and i % 2 == 0 and i + 4 < NT else []
                order += steps(f"SD {i // 2}") if split and i % 2 == 0 else []
                order += steps(*ahead.get(i, []), groups=1) if prepare else []
            return order + (steps(*rest[0], *rest[1], "E 0", "E 1") if not prepare else [])

        if L == 0:
            start = steps("LNB 0", "X 0", "X 1") + group_order(0, False, True, False)
        else:
            start = steps(*"""LNB 0,SG 0,X 0,X 1,GU 0,SR 0,A 0,RT 0,SG 1,RTT 0,GU 1,SM 0,GU 2,TOP 0,FT 0,F 0,AF 0,A 1,F 1,
                          AF 1,SD 0,A 2,F 2,AF 2,SG 2,D 0,SD 1,SG 3""".replace("\n", "").split(",")) + group_order(3, False, True, True)
        orders = {"start": start, "body": group_order(0, True, True, False), "last": group_order(0, True, False, False)}
        per = {"X": 2, "SR": 1, "RT": 1, "RTT": 1, "FT": 1, "F": NT, "E": 2}
        filled = {n: sem(f"{n.lower()}_filled") for n in per if L == 1 or n in ("X", "E")}
        released = {n: sem(f"{n.lower()}_released") for n in filled}
        rings = {}
        for part, order in orders.items():
            ring = [s for s in order if s[0] in per]
            shift = len(ring) % 2 if part == "start" else 0
            rings[part] = ring, {s: (n + shift) % 2 for n, s in enumerate(ring)}
        assert len(rings["body"][0]) % 2 == 0 and rings["start"][0][-2:] == rings["body"][0][-2:]

        def nth(n, m, i):
            return m * n + (i + 1)

        def walk(emit):
            for s in orders["start"]:
                emit("start", 0, *s)
            with emit.engine.Fori(1, G - 1) as g:
                for s in orders["body"]:
                    emit("body", g, *s)
            for s in orders["last"]:
                emit("last", G - 1, *s)

        def wait_past(engine, semaphore, count):
            if not isinstance(count, int) or count > 0:
                engine.wait_ge(semaphore, count)

        with nc.Block() as block:

            if L == 0:
                @block.sync
                def _(sp):
                    early.load(sp)

            if L == 1:
                @block.sync
                def _(sp):
                    sp.wait_ge(sem("router_zeroed"), 1)
                    sp.dma_start(router_raw[0:1, :], a["L1_ffn_W_sgate"]).then_inc(sem("router_loaded"), 16)
                    sp.dma_start(router_raw[1:1 + E, :], a["L1_ffn_W_router"]).then_inc(sem("router_loaded"), 16)
                    full, tail = divmod(I_SH, P)
                    rest = E * I_MOE - (P - tail)
                    shared, experts = a["L1_ffn_Ws_down"], a["L1_ffn_We_down"].rearrange("e i d -> (e i) d")
                    raw = w_raw["down"]
                    sp.wait_ge(sem("down_zeroed"), 1)
                    for part, rows in ((raw[:, 0:full, :], shared[0:full * P].rearrange("(t p) d -> p t d", p=P)),
                                       (raw[0:tail, full, :], shared[full * P:I_SH]),
                                       (raw[tail:P, full, :], experts[0:P - tail]),
                                       (raw[:, full + 1:NT - 1, :], experts[P - tail:P - tail + rest // P * P].rearrange("(t p) d -> p t d", p=P)),
                                       (raw[0:rest % P, NT - 1, :], experts[E * I_MOE - rest % P:E * I_MOE])):
                        sp.dma_start(part, rows).then_inc(sem("down_loaded"), 16)
                    with sp.Fori(0, G) as g:
                        sp.wait_ge(released["E"], g * 2 + 2)
                        sp.dma_start(out_dram[bass.ds(g * GB, GB)].rearrange("b s d -> s b d"),
                                     core.x[:, bass.ds(g * GB, GB), :]).then_inc(sem("stored"), 16)
                    sp.wait_ge(sem("stored"), 16 * G)

            @block.tensor
            def _(pe):
                def bank_free(part, g, step):
                    ring, slots = rings[part]
                    k = ring.index(step)
                    if k >= 2 or part != "start":
                        before, gb = (ring, g) if k >= 2 else (rings["body"][0], g - 1)
                        n, i, groups = before[k - 2]
                        pe.wait_ge(released[n], nth(per[n], gb + groups, i))
                    return misc[slots[step]]

                def step(part, g, name, i, groups):
                    m = g + groups
                    if name in per:
                        bank = bank_free(part, g, (name, i, groups))
                    if name == "X":
                        if i == 0:
                            pe.wait_ge(sem("xn_ready"), m + 1)
                        for b in range(GB):
                            last = nc.tensor.transpose(bank[:, b * P:(b + 1) * P], xn[:, b, i * P:(i + 1) * P], core.ident[:, :])
                    elif name == "GU":
                        if i == 0:
                            pe.wait_ge(released["X"], 2 * m + 2)
                        if L == 1 and part == "start" and i % 2 == 0:
                            pe.wait_ge(sem("gate_up_split"), i + 2)
                        for key, banks, read in (("gate", g_bank, "gate_read"), ("up", u_bank, "up_read")):
                            former = i - 2 if i >= 2 else (i - 2 if NT % 2 == 0 else (-1, -2)[i])
                            wait_past(pe, sem(read), m * NT + former + 1)
                            for k in range(KD):
                                last = three_pass(nc, banks[i % 2][:, :], [v[:, k, i * P:(i + 1) * P] for v in w[key]],
                                                  [v[:, k, bass.ds(m * N, N)] for v in xt], k == 0, k == KD - 1)
                        last.then_inc(sem("up_filled"), 1)
                        return
                    elif name == "SR":
                        pe.wait_ge(sem("router_loaded"), 32)
                        for k in range(KD):
                            last = nc.tensor.transpose(bank[:, k * P:(k + 1) * P], router_raw[:, k * P:(k + 1) * P], core.ident[:, :])
                    elif name == "F":
                        if part == "start" and i == 0:
                            pe.wait_ge(sem("owner_made"), 5)
                        if i == 0:
                            pe.wait_ge(released["FT"], m + 1)
                        last = nc.tensor.matmul(bank[:, :], w["owner"][:, i * P:(i + 1) * P], ft[:, bass.ds(m * N, N)], start=True, stop=True)
                    elif name == "D":
                        pe.wait_ge(sem("h_ready"), m * NT + i + 1)
                        if L == 1 and part == "start" and i % 2 == 0:
                            pe.wait_ge(sem("down_split"), i // 2 + 1)
                        if i == 0:
                            wait_past(pe, sem("out_read"), 2 * m)
                        for e in range(KD):
                            last = three_pass(nc, out_t[e][:, :], [v[:, i, e * P:(e + 1) * P] for v in w["down"]],
                                              [v[:, i % (LAG + 1), :] for v in hs], i == 0, i == NT - 1)
                        last.then_inc(sem("down_done"), 1)
                        return
                    elif name == "E":
                        if i == 0:
                            pe.wait_ge(sem("out_read"), 2 * m + 2)
                        for t in range(2):
                            for e in range(KD):
                                last = nc.tensor.transpose(bank[:, (t * KD + e) * P:(t * KD + e + 1) * P],
                                                           out_sb[:, e, (2 * i + t) * P:(2 * i + t + 1) * P], core.ident[:, :])
                    elif name == "RT":
                        if part == "start":
                            pe.wait_ge(released["SR"], 1)
                        pe.wait_ge(released["X"], 2 * m + 2)
                        for k in range(KD):
                            last = three_pass(nc, bank[:, :], [v[:, k, :] for v in w["router"]], [v[:, k, bass.ds(m * N, N)] for v in xt],
                                              k == 0, k == KD - 1)
                    elif name == "RTT":
                        pe.wait_ge(released["RT"], m + 1)
                        for b in range(GB):
                            last = nc.tensor.transpose(bank[:, b * P:(b + 1) * P], logit_t[:, b * P:(b + 1) * P], core.ident[:, :])
                    elif name == "FT":
                        pe.wait_ge(sem("factors_ready"), m + 1)
                        for b in range(GB):
                            last = nc.tensor.transpose(bank[:, b * P:(b + 1) * P], w["factors"][:, b, :], core.ident[:, :])
                    else:
                        return
                    last.then_inc(filled[name], 1)

                step.engine = pe
                walk(step)

            @block.scalar
            def _(act):
                def gate_up_hi(i):
                    cols = slice(2 * i * P, min(2 * i + 2, NT) * P)
                    if i == 0:
                        act.wait_ge(gate_up[1], 16 * 6)
                        act.wait_ge(sem("padded"), 2)
                    for name in ("gate", "up"):
                        nc.scalar.activation(w[name][0][:, :, cols], w_raw[name][:, :, cols], ACT.Copy).then_inc(sem("gate_up_hi"), 1)

                def down_hi(i):
                    tiles = slice(2 * i, min(2 * i + 2, NT))
                    if i == 0:
                        act.wait_ge(sem("down_loaded"), 16 * 5)
                    nc.scalar.activation(w["down"][0][:, tiles, :], w_raw["down"][:, tiles, :], ACT.Copy).then_inc(sem("down_hi"), 1)

                def split_hi(m, i):
                    act.wait_ge(released["F"] if L == 1 else sem("up_read"), m * NT + i + 1)
                    nc.scalar.activation(hs[0][:, i % (LAG + 1), :], hid[:, i % 2, :], ACT.Copy).then_inc(sem("h_hi_ready"), 1)

                def step(part, g, name, i, groups):
                    m = g + groups
                    bank = misc[rings[part][1][(name, i, groups)]] if name in per else None
                    if name == "X":
                        act.wait_ge(filled[name], nth(2, m, i))
                        nc.scalar.activation(xt[0][:, i, bass.ds(m * N, N)], bank[:, :], ACT.Copy).then_inc(sem("x_hi_ready"), 1)
                    elif name == "SG":
                        gate_up_hi(i)
                    elif name == "SD":
                        down_hi(i)
                    elif name == "SR":
                        act.wait_ge(filled["SR"], 1)
                        nc.scalar.activation(flat(w["router"][0][:, :, :]), bank[:, 0:D], ACT.Copy).then_inc(sem("router_hi"), 1)
                    elif name == "A":
                        act.wait_ge(sem("up_filled"), m * NT + i + 1)
                        nc.scalar.activation(act_g[:, i % 2, :], g_bank[i % 2][:, :], ACT.Gelu_apprx_tanh if L == 0 else ACT.Silu).then_inc(sem("gate_read"), 1)
                        if i:
                            split_hi(m, i - 1)
                    elif name == "FLUSH":
                        split_hi(m, NT - 1)
                    elif name == "OUT":
                        act.wait_ge(sem("down_done"), m * NT + NT)
                        for e in range(KD):
                            nc.scalar.activation(out_sb[:, e, :], out_t[e][:, :], ACT.Copy).then_inc(sem("out_read"), 1)
                    elif name == "RT":
                        act.wait_ge(filled["RT"], m + 1)
                        nc.scalar.activation(logit_t[:, :], bank[:, :], ACT.Copy).then_inc(released["RT"], 1)
                    elif name == "RTT":
                        act.wait_ge(sem("shifted_ready"), m + 1)
                        nc.scalar.activation(flat(expd[:, :, :]), flat(shifted[:, :, :]), ACT.Exp).then_inc(sem("exp_ready"), 1)
                    elif name == "TOP":
                        act.wait_ge(sem("factor_ready"), m + 1)
                        if part == "start":
                            act.wait_ge(sem("factors_zeroed"), 1)
                        nc.scalar.activation(w["factors"][:, :, 0:NF].bitcast(F32R), factor[:, :, :], ACT.Copy).then_inc(sem("factor_hi_ready"), 1)
                    elif name == "FT":
                        act.wait_ge(filled["FT"], m + 1)
                        nc.scalar.activation(ft[:, bass.ds(m * N, N)], bank[:, :], ACT.Copy).then_inc(released["FT"], 1)

                step.engine = act
                walk(step)

            @block.vector
            def _(dve):
                CHAIN = 11

                def router_factors(name, m, bank):
                    steps = [{"RTT": 0, "SM": 1, "TOP": 6}[name]]

                    def chained(ins):
                        steps[0] += 1
                        ins.then_inc(sem("router_step"), 1)
                        dve.wait_ge(sem("router_step"), m * CHAIN + steps[0])

                    if name == "RTT":
                        nc.vector.tensor_copy(logit[:, :, :], bank[:, :].rearrange("p (b r) -> p b r", r=P)[:, :, 0:NF]).then_inc(released["RTT"], 1)
                        dve.wait_ge(released["RTT"], m + 1)
                        chained(nc.vector.tensor_reduce(lmax[:, :], logit[:, :, 1:NF], AX.X, ALU.max))
                        nc.vector.tensor_scalar(shifted[:, :, 0:1], logit[:, :, 0:1], -1.0, None, ALU.mult)
                        nc.vector.tensor_tensor(shifted[:, :, 1:NF], logit[:, :, 1:NF], lmax[:, :].unsqueeze(2).to_broadcast([P, GB, E]),
                                                ALU.subtract).then_inc(sem("shifted_ready"), 1)
                    elif name == "SM":
                        dve.wait_ge(sem("exp_ready"), m + 1)
                        chained(nc.vector.tensor_reduce(sums[:, :, 0:1], expd[:, :, 1:NF], AX.X, ALU.add))
                        chained(nc.vector.tensor_scalar(sums[:, :, 1:2], expd[:, :, 0:1], 1.0, None, ALU.add))
                        chained(nc.vector.reciprocal(rsums[:, :, :], sums[:, :, :]))
                        chained(nc.vector.tensor_copy(factor[:, :, 0:1], rsums[:, :, 1:2]))
                        chained(nc.vector.tensor_tensor(prob[:, :, :], expd[:, :, 1:NF], rsums[:, :, 0:1].to_broadcast([P, GB, E]), ALU.mult))
                    else:
                        pj = prob[:, :, :].unsqueeze(2).to_broadcast([P, GB, E, E])
                        pe_ = prob[:, :, :].unsqueeze(3).to_broadcast([P, GB, E, E])
                        tri = w["tri"][:, :, :].unsqueeze(1).to_broadcast([P, GB, E, E])
                        chained(nc.vector.tensor_tensor(ties[:, :, :, :], pj, pe_, ALU.is_equal))
                        nc.vector.tensor_tensor(above[:, :, :, :], pj, pe_, ALU.is_gt)
                        chained(nc.vector.tensor_tensor(ties[:, :, :, :], ties[:, :, :, :], tri, ALU.mult))
                        chained(nc.vector.tensor_tensor(above[:, :, :, :], above[:, :, :, :], ties[:, :, :, :], ALU.add))
                        chained(nc.vector.tensor_reduce(rank[:, :, :], above[:, :, :, :], AX.X, ALU.add))
                        chained(nc.vector.scalar_tensor_tensor(out=factor[:, :, 1:NF], in0=rank[:, :, :], scalar=2.0, in1=prob[:, :, :],
                                                               op0=ALU.is_lt, op1=ALU.mult))
                        assert steps[0] == CHAIN
                        nc.vector.tensor_copy(logit[:, :, :], factor[:, :, :]).then_inc(sem("factor_ready"), 1)
                        dve.wait_ge(sem("factor_hi_ready"), m + 1)
                        nc.vector.tensor_tensor(w["factors"][:, :, NF:2 * NF], factor[:, :, :], w["factors"][:, :, 0:NF],
                                                ALU.subtract).then_inc(sem("factors_ready"), 1)

                def gate_up_lo(i):
                    cols = slice(2 * i * P, min(2 * i + 2, NT) * P)
                    for s, name in enumerate(("gate", "up")):
                        hi, lo = (v[:, :, cols] for v in w[name])
                        dve.wait_ge(sem("gate_up_hi"), 2 * i + s + 1)
                        nc.vector.tensor_tensor(lo, w_raw[name][:, :, cols], f32(hi), ALU.subtract).then_inc(sem("gate_up_split"), 1)

                def down_lo(i):
                    hi, lo = (v[:, 2 * i:min(2 * i + 2, NT), :] for v in w["down"])
                    dve.wait_ge(sem("down_hi"), i + 1)
                    nc.vector.tensor_tensor(lo, w_raw["down"][:, 2 * i:min(2 * i + 2, NT), :], f32(hi), ALU.subtract).then_inc(sem("down_split"), 1)

                def split_lo(m, i):
                    dve.wait_ge(sem("h_hi_ready"), m * NT + i + 1)
                    s = i % (LAG + 1)
                    nc.vector.tensor_tensor(hs[1][:, s, :], hid[:, i % 2, :], f32(hs[0][:, s, :]), ALU.subtract).then_inc(sem("h_ready"), 1)

                def step(part, g, name, i, groups):
                    m = g + groups
                    bank = misc[rings[part][1][(name, i, groups)]] if name in per else None
                    if name == "LNA":
                        norm.statistics(dve, m)
                    elif name == "LNB":
                        norm.normalise(dve, m, xn, sem("xn_ready"))
                    elif name == "X":
                        dve.wait_ge(sem("x_hi_ready"), nth(2, m, i))
                        nc.vector.tensor_tensor(xt[1][:, i, bass.ds(m * N, N)], bank[:, :], f32(xt[0][:, i, bass.ds(m * N, N)]),
                                                ALU.subtract).then_inc(released["X"], 1)
                    elif name == "SG":
                        gate_up_lo(i)
                    elif name == "SD":
                        down_lo(i)
                    elif name == "SR":
                        dve.wait_ge(sem("router_hi"), 1)
                        nc.vector.tensor_tensor(flat(w["router"][1][:, :, :]), bank[:, 0:D], f32(flat(w["router"][0][:, :, :])),
                                                ALU.subtract).then_inc(released["SR"], 1)
                    elif name == "A":
                        wait_past(dve, sem("h_ready"), m * NT + max(i - 1, 0))
                        dve.wait_ge(sem("gate_read"), m * NT + i + 1)
                        nc.vector.tensor_tensor(hid[:, i % 2, :], act_g[:, i % 2, :], u_bank[i % 2][:, :], ALU.mult).then_inc(sem("up_read"), 1)
                        if i:
                            split_lo(m, i - 1)
                    elif name == "AF":
                        dve.wait_ge(filled["F"], m * NT + i + 1)
                        dve.wait_ge(sem("up_read"), m * NT + i + 1)
                        nc.vector.tensor_tensor(hid[:, i % 2, :], hid[:, i % 2, :], misc[rings[part][1][("F", i, 0)]][:, :],
                                                ALU.mult).then_inc(released["F"], 1)
                    elif name == "FLUSH":
                        split_lo(m, NT - 1)
                    elif name in ("RTT", "SM", "TOP"):
                        if name == "RTT":
                            dve.wait_ge(filled["RTT"], m + 1)
                        if name == "TOP" and part == "start":
                            dve.wait_ge(sem("tri_made"), 2)
                        router_factors(name, m, bank)
                    elif name == "E":
                        dve.wait_ge(filled[name], nth(2, m, i))
                        here = flat(core.x[:, bass.ds(m * GB + 2 * i, 2), :])
                        nc.vector.scalar_tensor_tensor(out=here, in0=bank[:, :], scalar=core.gates[:, 2 + L:3 + L], in1=here,
                                                       op0=ALU.mult, op1=ALU.add).then_inc(released[name], 1)

                if L == 1:
                    for name in ("gate", "up"):
                        nc.vector.memset(w_raw[name][:, :, NF1:NT * P], 0.0).then_inc(sem("padded"), 1)
                step.engine = dve
                walk(step)

            def router_masks(pool):
                owner = w["owner"]
                n = 1
                nc.gpsimd.memset(f32(owner[:, :]), 0.0).then_inc(sem("owner_made"), 1)
                shared, experts = owner[:, 0:I_SH], owner[:, I_SH:NF1].rearrange("p (e n) -> p e n", e=E)
                for first in (0, E + 1):
                    for view, pattern, base in ((shared, [[0, I_SH]], -first), (experts, [[-1, E], [0, I_MOE]], -first - 1)):
                        pool.wait_ge(sem("owner_made"), n)
                        nc.gpsimd.affine_select(out=view, in_=f32(view), compare_op=ALU.not_equal, fill=1.0, base=base,
                                                pattern=pattern, channel_multiplier=1).then_inc(sem("owner_made"), 1)
                        n += 1
                nc.gpsimd.memset(w["tri"][:, :, :], 1.0).then_inc(sem("tri_made"), 1)
                pool.wait_ge(sem("tri_made"), 1)
                nc.gpsimd.affine_select(out=w["tri"][:, :, :], in_=w["tri"][:, :, :], compare_op=ALU.is_gt, fill=0.0, base=0,
                                        pattern=[[1, E], [-1, E]], channel_multiplier=0).then_inc(sem("tri_made"), 1)

            @block.gpsimd
            def _(pool):
                def step(part, g, name, i, groups):
                    m = g + groups
                    if name == "LNA":
                        norm.root(pool, m)
                    elif name == "SR":
                        router_masks(pool)

                if L == 1:
                    nc.gpsimd.memset(router_raw[:, :], 0.0).then_inc(sem("router_zeroed"), 1)
                    nc.gpsimd.memset(w_raw["down"][:, NT - 1, :], 0.0).then_inc(sem("down_zeroed"), 1)
                    nc.gpsimd.memset(w["factors"][:, :, :], 0.0).then_inc(sem("factors_zeroed"), 1)
                step.engine = pool
                walk(step)


_INS = ["x", "ctx_1024", "mask_BxS2_bf1", "g_xattn", "g_ffn",
        "L0_xattn_Wq", "L0_xattn_Wk", "L0_xattn_Wv", "L0_xattn_Wo", "L0_xattn_gq", "L0_xattn_gk",
        "L0_ffn_gate_W_packed", "L0_ffn_gate_scales", "L0_ffn_up_W_packed", "L0_ffn_up_scales",
        "L0_ffn_down_W_packed", "L0_ffn_down_scales", "L1_xattn_Wq", "L1_xattn_Wk", "L1_xattn_Wv", "L1_xattn_Wo",
        "L1_ffn_W_router", "L1_ffn_W_sgate", "L1_ffn_Ws_gate_up", "L1_ffn_Ws_down", "L1_ffn_We_gate_up", "L1_ffn_We_down"]


def kernel(**inputs):
    import numpy as np
    import concourse.bacc as bacc
    from concourse.bass_utils import run_bass_kernel_spmd

    nc = bacc.Bacc("TRN2", target_bir_lowering=False, num_devices=1)
    arrays, aps = {}, {}
    for name in _INS:
        v = np.ascontiguousarray(inputs[name])
        if v.dtype == np.bool_:
            v = v.view(np.uint8)
        arrays[f"in_{name}"] = v
        aps[name] = nc.dram_tensor(f"in_{name}", v.shape, mybir.dt.from_np(v.dtype), kind="ExternalInput").ap()
    out = nc.dram_tensor("out", (B, P, D), F32, kind="ExternalOutput").ap()
    flamingo(nc, aps, out)
    r = run_bass_kernel_spmd(nc, [arrays], core_ids=[0])
    return r.results[0]["out"]
```
